# Optimizing a Trainium2 kernel written in Bass

```python
import numpy as np
import jax
import jax.numpy as jnp

def _softmax(x, axis=-1):
    return jax.nn.softmax(x, axis=axis)

def _gelu(x):
    return jax.nn.gelu(x, approximate=True)

def _silu(x):
    return jax.nn.silu(x)

def _sigmoid(x):
    return jax.nn.sigmoid(x)

def _layernorm(x, axis=-1, eps=1e-05):
    m = jnp.mean(x, axis=axis, keepdims=True)
    v = jnp.var(x, axis=axis, keepdims=True)
    return (x - m) / jnp.sqrt(v + eps)

def _scatter_add(tgt, idx, src, axis=0):
    return tgt.at[idx].add(src)

def _segment_sum(src, seg, n):
    return jax.ops.segment_sum(src, seg, n)
kernel_name = 'mk_flamingo_gated_d1_seqx_r4_2591c2'

def setup_inputs(seed: int=0):
    np.random.seed(seed)
    _w = jnp.asarray

    def _rec_inputs():
        import jax
        import jax.numpy as jnp
        _rk = jax.random.key(seed)
        x = 7.22e-05 + 1 * jax.random.normal(jax.random.fold_in(_rk, 1), (16, 256, 256), jnp.float32)
        _lenS = 256 - jax.random.randint(jax.random.fold_in(_rk, 7), (16,), 0, max(1, 256 // 4) + 1, jnp.int32)
        _lenS2 = 256 - jax.random.randint(jax.random.fold_in(_rk, 8), (16,), 0, max(1, 256 // 4) + 1, jnp.int32)
        _ctx_1024P = jax.random.normal(jax.random.fold_in(_rk, 11), (16, 16, 256), jnp.float32)
        _ctx_1024c = jax.random.dirichlet(jax.random.fold_in(_rk, 511), 0.3 * jnp.ones((16,), jnp.float32), (16, 256))
        _ctx_1024t = jnp.einsum('bsk,bkd->bsd', _ctx_1024c, _ctx_1024P)
        _ctx_1024t = _ctx_1024t * jax.lax.rsqrt(jnp.mean(jnp.square(_ctx_1024t)) + 1e-12) * 0.953939
        ctx_1024 = 4.13588e-05 + 0.999923 * (_ctx_1024t + 0.3 * jax.random.normal(jax.random.fold_in(_rk, 611), (16, 256, 256), jnp.float32))
        _g = jax.random.normal(jax.random.fold_in(_rk, 9001), (2, 1), jnp.float32)
        _g = jnp.sign(_g) * jnp.maximum(jnp.abs(_g), 1.0) + (_g == 0) * 1.0
        g_xattn = _g[0]
        g_ffn = _g[1]
        return (x, ctx_1024, g_xattn, g_ffn)
    x, ctx_1024, g_xattn, g_ffn = _rec_inputs()

    def _L0_xattn_setup():
        import jax, jax.numpy as jnp
        import numpy as np
        D_MODEL = 256
        NHEAD = 16
        HEAD_DIM = D_MODEL // NHEAD
        key = jax.random.key(seed)
        ks = jax.random.split(key, 11)
        B, L, D = (4, 512, D_MODEL)
        s = 1.0 / np.sqrt(D)
        return {'queries': jax.random.normal(ks[0], (B, L, D), jnp.float32), 'keys': jax.random.normal(ks[1], (B, L, D), jnp.float32), 'values': jax.random.normal(ks[2], (B, L, D), jnp.float32), 'Wq': jax.random.normal(ks[3], (D, D), jnp.float32) * s, 'bq': jnp.zeros((D,), jnp.float32), 'Wk': jax.random.normal(ks[4], (D, D), jnp.float32) * s, 'bk': jnp.zeros((D,), jnp.float32), 'Wv': jax.random.normal(ks[5], (D, D), jnp.float32) * s, 'bv': jnp.zeros((D,), jnp.float32), 'Wo': jax.random.normal(ks[6], (D, D), jnp.float32) * s, 'bo': jnp.zeros((D,), jnp.float32)}
    _L0_xattn_all = _L0_xattn_setup()
    _L0_xattn_in = {k: v for k, v in _L0_xattn_all.items() if k in ('Wq', 'bq', 'Wk', 'bk', 'Wv', 'bv', 'Wo', 'bo')}
    del _L0_xattn_all

    def _L0_ffn_setup():
        import jax, jax.numpy as jnp
        import numpy as np
        TOP_K = 2

        def _moe(x, Wr, br, W1, b1, W2, b2):
            B, S, D = x.shape
            E = Wr.shape[1]
            xt = x.reshape(-1, D)
            logits = xt @ Wr + br
            top_vals, top_idx = jax.lax.top_k(logits, TOP_K)
            mask = jnp.zeros_like(logits, dtype=bool).at[jnp.arange(xt.shape[0])[:, None], top_idx].set(True)
            sparse_logits = jnp.where(mask, logits, -jnp.inf)
            gate = jax.nn.softmax(sparse_logits, axis=-1)
            h = jax.nn.relu(jnp.einsum('td,edh->teh', xt, W1) + b1)
            y = jnp.einsum('teh,ehd->ted', h, W2) + b2
            out = jnp.einsum('ted,te->td', y, gate)
            return out.reshape(B, S, D)
        key = jax.random.key(seed)
        ks = jax.random.split(key, 5)
        B, S, D, E, H = (2, 512, 256, 8, 1024)
        scale = 1.0 / np.sqrt(D)
        return {'x': jax.random.normal(ks[0], (B, S, D), dtype=jnp.float32), 'Wr': jax.random.normal(ks[1], (D, E), dtype=jnp.float32) * scale, 'br': jnp.zeros((E,), dtype=jnp.float32), 'W1': jax.random.normal(ks[2], (E, D, H), dtype=jnp.float32) * scale, 'b1': jnp.zeros((E, H), dtype=jnp.float32), 'W2': jax.random.normal(ks[3], (E, H, D), dtype=jnp.float32) * (1.0 / np.sqrt(H)), 'b2': jnp.zeros((E, D), dtype=jnp.float32)}
    _L0_ffn_all = _L0_ffn_setup()
    _L0_ffn_in = {k: v for k, v in _L0_ffn_all.items() if k in ('Wr', 'br', 'W1', 'b1', 'W2', 'b2')}
    del _L0_ffn_all
    return {'x': x, 'ctx_1024': ctx_1024, 'g_xattn': g_xattn, 'g_ffn': g_ffn, 'L0_xattn_Wq': _L0_xattn_in['Wq'], 'L0_xattn_bq': _L0_xattn_in['bq'], 'L0_xattn_Wk': _L0_xattn_in['Wk'], 'L0_xattn_bk': _L0_xattn_in['bk'], 'L0_xattn_Wv': _L0_xattn_in['Wv'], 'L0_xattn_bv': _L0_xattn_in['bv'], 'L0_xattn_Wo': _L0_xattn_in['Wo'], 'L0_xattn_bo': _L0_xattn_in['bo'], 'L0_ffn_Wr': _L0_ffn_in['Wr'], 'L0_ffn_br': _L0_ffn_in['br'], 'L0_ffn_W1': _L0_ffn_in['W1'], 'L0_ffn_b1': _L0_ffn_in['b1'], 'L0_ffn_W2': _L0_ffn_in['W2'], 'L0_ffn_b2': _L0_ffn_in['b2']}

def reference(x, ctx_1024, g_xattn, g_ffn, L0_xattn_Wq, L0_xattn_bq, L0_xattn_Wk, L0_xattn_bk, L0_xattn_Wv, L0_xattn_bv, L0_xattn_Wo, L0_xattn_bo, L0_ffn_Wr, L0_ffn_br, L0_ffn_W1, L0_ffn_b1, L0_ffn_W2, L0_ffn_b2):
    import jax
    import jax.numpy as jnp

    def _L0_xattn_ref(queries, keys, values, Wq, bq, Wk, bk, Wv, bv, Wo, bo):
        import jax, jax.numpy as jnp
        import numpy as np
        D_MODEL = 256
        NHEAD = 16
        HEAD_DIM = D_MODEL // NHEAD
        B, L, D = queries.shape
        H, dh = (NHEAD, HEAD_DIM)
        q = (queries @ Wq + bq).reshape(B, L, H, dh).transpose(0, 2, 1, 3)
        k = (keys @ Wk + bk).reshape(B, L, H, dh).transpose(0, 2, 1, 3)
        v = (values @ Wv + bv).reshape(B, L, H, dh).transpose(0, 2, 1, 3)
        scores = jnp.einsum('bhqd,bhkd->bhqk', q, k) / jnp.sqrt(jnp.float32(dh))
        attn = jax.nn.softmax(scores, axis=-1)
        ctx = jnp.einsum('bhqk,bhkd->bhqd', attn, v)
        ctx = ctx.transpose(0, 2, 1, 3).reshape(B, L, D)
        return ctx @ Wo + bo

    def _L0_ffn_ref(x, Wr, br, W1, b1, W2, b2):
        import jax, jax.numpy as jnp
        import numpy as np
        TOP_K = 2

        def _moe(x, Wr, br, W1, b1, W2, b2):
            B, S, D = x.shape
            E = Wr.shape[1]
            xt = x.reshape(-1, D)
            logits = xt @ Wr + br
            top_vals, top_idx = jax.lax.top_k(logits, TOP_K)
            mask = jnp.zeros_like(logits, dtype=bool).at[jnp.arange(xt.shape[0])[:, None], top_idx].set(True)
            sparse_logits = jnp.where(mask, logits, -jnp.inf)
            gate = jax.nn.softmax(sparse_logits, axis=-1)
            h = jax.nn.relu(jnp.einsum('td,edh->teh', xt, W1) + b1)
            y = jnp.einsum('teh,ehd->ted', h, W2) + b2
            out = jnp.einsum('ted,te->td', y, gate)
            return out.reshape(B, S, D)
        return _moe(x, Wr, br, W1, b1, W2, b2)
    x = x + jnp.tanh(g_xattn[0]) * _L0_xattn_ref(_layernorm(x, axis=-1), ctx_1024, ctx_1024, L0_xattn_Wq, L0_xattn_bq, L0_xattn_Wk, L0_xattn_bk, L0_xattn_Wv, L0_xattn_bv, L0_xattn_Wo, L0_xattn_bo)
    x = x + jnp.tanh(g_ffn[0]) * _L0_ffn_ref(_layernorm(x, axis=-1), L0_ffn_Wr, L0_ffn_br, L0_ffn_W1, L0_ffn_b1, L0_ffn_W2, L0_ffn_b2)
    return x

_drawn_inputs = setup_inputs


def setup_inputs(seed=0):
    import zlib

    import numpy as np

    out = dict(_drawn_inputs(seed))
    spreads = {'L0_xattn_bq': (0.0, 0.1),
     'L0_xattn_bk': (0.0, 0.1),
     'L0_xattn_bv': (0.0, 0.1),
     'L0_xattn_bo': (0.0, 0.1),
     'L0_ffn_br': (0.0, 0.1),
     'L0_ffn_b1': (0.0, 0.1),
     'L0_ffn_b2': (0.0, 0.1)}
    factors = {}
    for name, (base, spread) in spreads.items():
        noise = np.random.default_rng([zlib.crc32(name.encode()), seed]).standard_normal(out[name].shape)
        drawn = base * np.exp(spread * noise) if base else spread * noise
        out[name] = jnp.asarray(drawn.astype(out[name].dtype))
    for name, factor in factors.items():
        out[name] = (out[name] * factor).astype(out[name].dtype)
    return out
```

```python
from contextlib import ExitStack

import concourse.bass as bass
from concourse import mybir

ALU = mybir.AluOpType
ACT = mybir.ActivationFunctionType
AX = mybir.AxisListType
F32 = mybir.dt.float32
F16 = mybir.dt.float16
BF16 = mybir.dt.bfloat16
I32 = mybir.dt.int32
ds = bass.ds

P = 128
EPS = 1e-5
WSCALE = 256.0
HSCALE = 16.0
Q_TERM = [0, 0, 1, 1, 0, 2]
K_TERM = [0, 1, 0, 1, 2, 0]
NTERM = len(Q_TERM)


def flamingo(nc, x, ctx_in, g_xattn, g_ffn, Wq, bq, Wk, bk, Wv, bv, Wo, bo, Wr, br, W1, b1, W2, b2, out):
    NB, L, D = x.shape
    E, _, H = W1.shape
    NH, DH = 16, D // 16
    C = L // P
    M = D // P
    HC = H // P
    T = NB * L
    NI = T // P
    NT = (2 * T + E * (P - 1)) // P
    KR = NTERM * DH
    BIG = 3.0e38

    x_rows = x.rearrange("b (c p) d -> b p c d", p=P)
    ctx_rows = ctx_in.rearrange("b (c p) d -> b p c d", p=P)

    ctx = ExitStack()
    with ctx:
        def sem(name):
            return ctx.enter_context(nc.semaphore(name))

        def dram(name, shape, dt):
            return nc.dram_tensor(name, shape, dt, kind="Internal").ap()

        cursor = [-(-nc.sbuf_base // 64) * 64]

        def sb(name, shape, dt, at=None):
            size = 1
            for s in shape[1:]:
                size *= s
            size *= 2 if dt in (F16, BF16) else 4
            size = -(-size // 32) * 32
            where = cursor if at is None else at
            t = nc.alloc_sbuf_tensor_at(name, shape, dt, offset=where[0])
            where[0] += size
            return t

        part_d = {s: [dram(f"{s}_parts{i}", (3, D, L), BF16) for i in range(2)] for s in "qk"}
        x1_d = dram("x1_rows", (T, D), F32)
        xn2_d = dram("xn2_rows", (T, D), F32)
        y_d = dram("y_rows", (2 * T + NT * P, D), F32)

        ident = sb("ident", [P, P], F32)
        tri = sb("tri", [P, P], BF16)
        ones = sb("ones", [P, P], BF16)
        logits = sb("logits", [P, NI, E], F32)
        b1_col = sb("b1_col", [P, E * HC], F32)
        gate1 = sb("gate1", [P, NI], F32)
        gate2 = sb("gate2", [P, NI], F32)
        tanh_x = sb("tanh_x", [P, 1], F32)
        tanh_f = sb("tanh_f", [P, 1], F32)
        slot_token = sb("slot_token", [P, NT], I32)
        slot_dest = sb("slot_dest", [P, NT], I32)
        tile_expert = sb("tile_expert", [1, NT], I32)
        W_KEPT = 6
        wall = sb("wall", [P, E, 2, 2, M * H], F16)
        over = [cursor[0] - (E - W_KEPT) * 2 * 2 * M * H * 2]
        late = [cursor[0]]

        A = over
        free_late = A[0]
        xin = [sb(f"xin{i}", [P, C, D], F32, A) for i in range(2)]
        cin = [sb(f"cin{i}", [P, C, D], F32, A) for i in range(2)]
        xn = sb("xn", [P, C, D], F32, A)
        xnT = sb("xnT", [P, M, L], F32, A)
        ctxT = sb("ctxT", [P, M, L], F32, A)
        yq = sb("yq", [P, M, L], F32, A)
        yk = sb("yk", [P, M, L], F32, A)
        rest = sb("rest", [P, M, L], F32, A)
        qparts = sb("qparts", [P, 3, M, L], BF16, A)
        kparts = sb("kparts", [P, 3, M, L], BF16, A)
        wq = sb("wq", [P, M, D], F32, A)
        wk = sb("wk", [P, M, D], F32, A)
        wv = sb("wv", [P, M, D], F32, A)
        assert A[0] >= late[0]
        wo = sb("wo", [P, M, D], F32, A)
        wr = sb("wr", [P, M, E], F32, A)
        out_bias = sb("out_bias", [P, D], F32, A)
        bo_b = sb("bo_b", [P, D], F32, A)
        br_b = sb("br_b", [P, E], F32, A)
        bias_col = sb("bias_col", [P, 3, M], F32, A)
        stats = sb("stats", [P, C, 6], F32, A)
        mean_var = [sb(f"mean_var{i}", [P, C, 2], F32, A) for i in range(2)]
        var_eps = [sb(f"var_eps{i}", [P, C], F32, A) for i in range(2)]
        rstd = [sb(f"rstd{i}", [P, C], F32, A) for i in range(2)]
        minus_half = sb("minus_half", [P, C], F32, A)
        qs = [sb(f"qs{i}", [P, NH, L], BF16, A) for i in range(2)]
        ks = [sb(f"ks{i}", [P, NH, L], BF16, A) for i in range(2)]
        vaug = [sb(f"vaug{i}", [P, C, NH, 32], F32, A) for i in range(2)]
        probs = [sb(f"probs{i}", [P, 4, L], F32, A) for i in range(2)]
        negmax = sb("negmax", [P, C, NH], F32, A)
        negmax_row = [sb(f"negmax_row{i}", [8, L], BF16, A) for i in range(2)]
        oT = sb("oT", [P, 4, L], F32, A)
        recip = [sb(f"recip{i}", [P, NH], F32, A) for i in range(2)]
        cn = sb("cn", [P, C, D], F32, A)
        cT = sb("cT", [P, M, L], F32, A)
        xres = sb("xres", [P, C, D], F32, A)
        x1b = sb("x1b", [P, C, D], F32, A)
        xn2b = sb("xn2b", [P, C, D], F32, A)
        wst_at = A[0]
        wst = [sb(f"wst{i}", [P, M * H // 2], F32, A) for i in range(1)]
        assert A[0] <= nc.sbuf_usable_end, (A[0], nc.sbuf_usable_end)

        R = late
        b2_b = sb("b2_b", [P, E, D], F32, R)
        x1_all = sb("x1_all", [P, NI, D], F32, R)
        B0 = [R[0]]
        iota_e = sb("iota_e", [P, E], F32, B0)
        iota_b = sb("iota_b", [P, P], F32, B0)
        unused_row = sb("unused_row", [P, NT], F32, B0)
        tok_val = sb("tok_val", [P, NI], F32, B0)
        tok_neg = sb("tok_neg", [P, NI], F32, B0)
        t3 = sb("t3", [P, NI, E], F32, B0)
        oh1 = sb("oh1", [P, NI, E], F32, B0)
        oh2 = sb("oh2", [P, NI, E], F32, B0)
        picked = sb("picked", [P, NI, E], BF16, B0)
        masked = sb("masked", [P, NI, E], F32, B0)
        totals = sb("totals", [P, E, NI], F32, B0)
        before = sb("before", [P, E, NI], F32, B0)
        onesf = sb("onesf", [P, E * NI], F32, B0)
        best1 = sb("best1", [P, NI], F32, B0)
        best2 = sb("best2", [P, NI], F32, B0)
        index = sb("index", [P, NI], F32, B0)
        gexp = sb("gexp", [P, NI], F32, B0)
        e_end = sb("e_end", [P, E + 1], F32, B0)
        e_cnt = sb("e_cnt", [P, E], F32, B0)
        e_int = sb("e_int", [P, E], I32, B0)
        e_tiles = sb("e_tiles", [P, E], F32, B0)
        t_end = sb("t_end", [P, E + 1], F32, B0)
        e_off = sb("e_off", [P, E], F32, B0)
        slot = sb("slot", [P, 2, NI], F32, B0)
        slot_i = sb("slot_i", [P, 2, NI], I32, B0)
        slot_t = sb("slot_t", [P, 2, NI], I32, B0)
        slot_col = sb("slot_col", [P, 2, NI], F32, B0)
        slot_row = sb("slot_row", [P, 2, NI], F32, B0)
        NHOT = 16
        hot_row = sb("hot_row", [P, NHOT, P], F16, B0)
        hot_col = sb("hot_col", [P, NHOT, NT], F16, B0)
        tval = sb("tval", [P, 2, NT], F32, B0)
        tsum = sb("tsum", [P, NT], F32, B0)
        tflag = sb("tflag", [P, NT], F32, B0)
        tfull = sb("tfull", [P, NT], F32, B0)
        te3 = sb("te3", [1, NT, E], F32, B0)
        wst_late = sb("wst_late", [P, M * H // 2], F32, B0)
        assert B0[0] <= wst_at, (B0[0], wst_at)
        C0 = [R[0]]
        gather_idx = [sb(f"gather_idx{i}", [P, 1], I32, C0) for i in range(2)]
        dest_idx = [sb(f"dest_idx{i}", [P, 1], I32, C0) for i in range(2)]
        xg = [sb(f"xg{i}", [P, D], F32, C0) for i in range(2)]
        xh = [sb(f"xh{i}", [P, M, P], F16, C0) for i in range(2)]
        xl = [sb(f"xl{i}", [P, M, P], F16, C0) for i in range(2)]
        hid = [sb(f"hid{i}", [P, H], F32, C0) for i in range(2)]
        hh = [sb(f"hh{i}", [P, H], F16, C0) for i in range(2)]
        hl = [sb(f"hl{i}", [P, H], F16, C0) for i in range(2)]
        yb = [sb(f"yb{i}", [P, D], F32, C0) for i in range(2)]
        assert C0[0] <= nc.sbuf_usable_end, C0[0]
        D0 = [R[0]]
        DT = 4
        y1b = [sb(f"y1b{i}", [P, DT, D], F32, D0) for i in range(2)]
        y2b = [sb(f"y2b{i}", [P, DT, D], F32, D0) for i in range(2)]
        assert D0[0] <= nc.sbuf_usable_end, D0[0]

        banks = ctx.enter_context(nc.psum_tensor("banks", [P, 8, 512], F32))

        def bank(i):
            return banks[:, i, :]

        passed = sem("passed")
        consts = sem("consts")
        pool_const = sem("pool_const")
        pool_ready = sem("pool_ready")
        tanh_ready = sem("tanh_ready")
        bvcol_ready = sem("bvcol_ready")
        bvwo_done = sem("bvwo_done")
        obias_ready = sem("obias_ready")
        b1t_done = sem("b1t_done")
        biases_ready = sem("biases_ready")
        xin_full = [sem(f"xin_full{i}") for i in range(2)]
        cin_full = [sem(f"cin_full{i}") for i in range(2)]
        xres_full = sem("xres_full")
        xn_ready = sem("xn_ready")
        var_ready = [sem(f"var_ready{i}") for i in range(2)]
        rstd_ready = [sem(f"rstd_ready{i}") for i in range(2)]
        xT_done, xT_evac = sem("xT_done"), sem("xT_evac")
        ctxT_done, ctxT_evac = sem("ctxT_done"), sem("ctxT_evac")
        q_done, q_evac = sem("q_done"), sem("q_evac")
        k_done, k_evac = sem("k_done"), sem("k_evac")
        v_done, v_evac = sem("v_done"), sem("v_evac")
        q_split, k_split = sem("q_split"), sem("k_split")
        q_stored, k_stored = sem("q_stored"), sem("k_stored")
        qs_full, ks_full = sem("qs_full"), sem("ks_full")
        mx_done, mx_red = sem("mx_done"), sem("mx_red")
        nm_done, nm_evac = sem("nm_done"), sem("nm_evac")
        row_full = [sem(f"row_full{i}") for i in range(2)]
        st_done, exp_done = sem("st_done"), sem("exp_done")
        av_mm, av_evac = sem("av_mm"), sem("av_evac")
        tok_done, cn_ready = sem("tok_done"), sem("cn_ready")
        cT_done, cT_evac, o_done = sem("cT_done"), sem("cT_evac"), sem("o_done")
        xb_ready, x1_ready, xn2_ready = sem("xb_ready"), sem("x1_ready"), sem("xn2_ready")
        x1_stored, xn2_stored = sem("x1_stored"), sem("xn2_stored")
        x2T_done, x2T_evac = sem("x2T_done"), sem("x2T_evac")
        lg_done, lg_evac = sem("lg_done"), sem("lg_evac")
        w_full, w_scaled, w_hi, w_lo = sem("w_full"), sem("w_scaled"), sem("w_hi"), sem("w_lo")
        dve_chain = sem("dve_chain")
        pool_chain = sem("pool_chain")
        late_full = [sem(f"late_full{i}") for i in range(2)]
        late_scaled, late_hi, late_lo = sem("late_scaled"), sem("late_hi"), sem("late_lo")
        b2_full, x1_full = sem("b2_full"), sem("x1_full")
        iota_ready = sem("iota_ready")
        diff_ready, gexp_ready = sem("diff_ready"), sem("gexp_ready")
        picked_ready, rank_done = sem("picked_ready"), sem("rank_done")
        hot_ready, hot_used, lists_ready = sem("hot_ready"), sem("hot_used"), sem("lists_ready")
        idx_ready, dest_ready = sem("idx_ready"), sem("dest_ready")
        xg_full = [sem(f"xg_full{i}") for i in range(2)]
        gT_done, xh_ready, xl_ready = sem("gT_done"), sem("xh_ready"), sem("xl_ready")
        h_done, hid_ready, hh_ready, hl_ready = sem("h_done"), sem("hid_ready"), sem("hh_ready"), sem("hl_ready")
        y_done, y_ready = sem("y_done"), sem("y_ready")
        y_sent = [sem(f"y_sent{i}") for i in range(2)]
        y_back = [sem(f"y_back{i}") for i in range(2)]
        out_ready = sem("out_ready")
        out_sent = [sem(f"out_sent{i}") for i in range(2)]

        N_CONST = 11
        HOLDS = (nc.sync.engine, nc.gpsimd.engine)

        def hold(eng, s, v):
            eng.wait_ge(s, v)
            if not isinstance(v, int):
                eng.sem_inc(passed, 1)

        def wait(eng, s, v):
            if isinstance(v, int) and v <= 0:
                return
            hold(eng, s, v) if eng.engine in HOLDS else eng.wait_ge(s, v)

        def bodies(eng, body):
            body(0, 0, False, True)
            body(0, 1, False, True)
            with eng.Fori(1, NB // 2 - 1) as t:
                body(t, 0, True, True)
                body(t, 1, True, True)
            body(NB // 2 - 1, 0, False, True)
            body(NB // 2 - 1, 1, False, False)

        assert NB // 2 - 2 == W_KEPT

        def weight_at(e, w, part, a, b):
            return wall[:, ds(e, 1), w, part, a:b].rearrange("p e n -> p (e n)")

        LATE = [(e, w, half) for e in range(W_KEPT, E) for w in range(2) for half in range(2)]
        HALF = M * H // 2

        def weight_rows(e, w, half):
            if w == 0:
                return W1[e, half * P:(half + 1) * P, :]
            return W2[e, half * H // 2:(half + 1) * H // 2, :].rearrange("(c p) n -> p c n", p=P)

        def stage_view(buf, w):
            return buf[:, :] if w == 0 else buf[:, :].rearrange("p (c n) -> p c n", n=D)

        late_stage = [wst[0], wst_late]

        block = ctx.enter_context(nc.Block())

        @block.sync
        def _(sp):
            def load_x(n, t, par):
                wait(sp, xn_ready, 2 * (n - 1))
                sp.dma_start(xin[par][:], x_rows[n]).then_inc(xin_full[par], 16)
                wait(sp, ctxT_done, n - 1)
                sp.dma_start(cin[par][:], ctx_rows[n]).then_inc(cin_full[par], 16)

            def parts(n, t, par):
                for name, src, cut_, dst_stored, full in (("k", kparts, k_split, k_stored, ks_full), ("q", qparts, q_split, q_stored, qs_full)):
                    wait(sp, full, 16 * NTERM * (n - 1))
                    hold(sp, cut_, n + 1)
                    sp.dma_start(part_d[name][par].rearrange("s (m p) t -> p s m t", p=P), src[:]).then_inc(dst_stored, 16)
                wait(sp, st_done, 8 * (n - 1))
                for name, terms, stored, dst, full in (("k", K_TERM, k_stored, ks, ks_full), ("q", Q_TERM, q_stored, qs, qs_full)):
                    hold(sp, stored, 16 * (n + 1))
                    for i, s in enumerate(terms):
                        sp.dma_start(dst[par][DH * i:DH * (i + 1), :, :],
                                     part_d[name][par][s].rearrange("(h d) t -> d h t", d=DH)).then_inc(full, 16)

            def results(n):
                hold(sp, x1_ready, 2 * (n + 1))
                sp.dma_start(x1_d[ds(n * L, L), :].rearrange("(c p) d -> p c d", p=P), x1b[:]).then_inc(x1_stored, 16)
                hold(sp, xn2_ready, 2 * (n + 1))
                sp.dma_start(xn2_d[ds(n * L, L), :].rearrange("(c p) d -> p c d", p=P), xn2b[:]).then_inc(xn2_stored, 16)

            def residual(n):
                wait(sp, x1_ready, 2 * n)
                sp.dma_start(xres[:], x_rows[n]).then_inc(xres_full, 16)

            sp.dma_start(xin[0][:], x_rows[0]).then_inc(xin_full[0], 16)
            sp.dma_start(cin[0][:], ctx_rows[0]).then_inc(cin_full[0], 16)
            for dst, w in ((wq, Wq), (wk, Wk), (wv, Wv), (wo, Wo), (wr, Wr)):
                sp.dma_start(dst[:], w.rearrange("(m p) n -> p m n", p=P)).then_inc(consts, 16)
            for i, b in enumerate((bq, bk, bv)):
                sp.dma_start(oT[E * HC + i * M:E * HC + (i + 1) * M, 0, 0:P], b.rearrange("(m p) -> m p", p=P)).then_inc(consts, 16)
            sp.dma_start(bo_b[:], bo.partition_broadcast(P)).then_inc(consts, 16)
            sp.dma_start(br_b[:], br.partition_broadcast(P)).then_inc(consts, 16)
            sp.dma_start(oT[0:E * HC, 0, 0:P], b1.rearrange("e (c p) -> (e c) p", p=P)).then_inc(consts, 16)
            load_x(1, 0, 1)
            parts(0, 0, 0)

            def body(t, par, weights, nxt):
                n = 2 * t + par
                static = isinstance(n, int)
                if not static or n + 2 < NB:
                    load_x(n + 2, t + 1, par)
                if weights:
                    e = t - 1
                    i = 2 * (t - 1) + par
                    for w in range(2):
                        wait(sp, w_lo, 2 * i + w)
                        if w == 0:
                            src = W1[ds(e, 1), par * P:(par + 1) * P, :].rearrange("e p n -> p (e n)")
                        else:
                            src = W2[ds(e, 1), par * H // 2:(par + 1) * H // 2, :].rearrange("e (c p) n -> p (e c) n", p=P)
                        sp.dma_start(stage_view(wst[0], w), src).then_inc(w_full, 16)
                        if w == 0 and (not static or n > 0):
                            residual(n - 1)
                elif n > 0:
                    residual(n - 1)
                for s in range(2):
                    hold(sp, nm_evac, 2 * n + s + 1)
                    sp.dma_start(qs[par][KR:KR + 1, 8 * s:8 * s + 8, :], negmax_row[s][:]).then_inc(row_full[s], 16)
                if not static or n > 0:
                    results(n - 1)
                if nxt:
                    parts(n + 1, t + par, 1 - par)

            bodies(sp, body)
            hold(sp, k_stored, 16 * NB)
            hold(sp, q_stored, 16 * NB)
            hold(sp, v_done, NB)
            residual(NB - 1)
            for i, (e, w, half) in enumerate(LATE):
                if i == 0:
                    wait(sp, w_lo, 4 * W_KEPT)
                if i == 1:
                    results(NB - 1)
                    hold(sp, lg_evac, NB)
                    hold(sp, x1_stored, 16 * NB)
                    hold(sp, xn2_stored, 16 * NB)
                    sp.dma_start(b2_b[:].rearrange("p e d -> p (e d)"), b2.rearrange("e d -> (e d)").partition_broadcast(P)).then_inc(b2_full, 16)
                if i >= 2:
                    hold(sp, late_lo, i - 1)
                sp.dma_start(stage_view(late_stage[i % 2], w), weight_rows(e, w, half)).then_inc(late_full[i % 2], 16)
            sp.dma_start(x1_all[:], x1_d.rearrange("(i p) d -> p i d", p=P)).then_inc(x1_full, 16)
            hold(sp, y_sent[0], 16 * ((NT + 1) // 2))
            hold(sp, y_sent[1], 16 * (NT // 2))
            for i in range(NI // DT):
                if i >= 2:
                    hold(sp, out_sent[i % 2], 16 * (i // 2))
                sp.dma_start(y1b[i % 2][:], y_d[i * DT * P:(i + 1) * DT * P, :].rearrange("(i p) d -> p i d", p=P)).then_inc(y_back[i % 2], 16)
                sp.dma_start(y2b[i % 2][:], y_d[T + i * DT * P:T + (i + 1) * DT * P, :].rearrange("(i p) d -> p i d", p=P)).then_inc(y_back[i % 2], 16)
            for s in range(2):
                hold(sp, out_sent[s], 16 * (NI // DT // 2))

        @block.gpsimd
        def _(pool):
            chain = [0, 0]

            def link(ins):
                chain[0] += 1
                ins.then_inc(pool_chain, 1)
                hold(pool, pool_chain, chain[0] + chain[1])

            for i in range(2):
                nc.gpsimd.memset(vaug[i][:], 0.0)
                nc.gpsimd.memset(ks[i][:], 1.0)
            nc.gpsimd.memset(ident[:], 0.0)
            nc.gpsimd.memset(minus_half[:], -0.5)
            nc.gpsimd.memset(ones[:], 1.0)
            nc.gpsimd.memset(tri[:], 1.0).then_inc(pool_const, 1)
            hold(pool, pool_const, 1)
            for i in range(2):
                nc.gpsimd.memset(vaug[i][:, :, :, DH:DH + 1], 1.0)
            nc.gpsimd.affine_select(out=ident[:], in_=ident[:], compare_op=ALU.not_equal, fill=1.0, base=0,
                                    pattern=[[-1, P]], channel_multiplier=1)
            nc.gpsimd.affine_select(out=tri[:], in_=tri[:], compare_op=ALU.is_gt, fill=0.0, base=0,
                                    pattern=[[1, P]], channel_multiplier=-1).then_inc(pool_ready, 1)

            def cut(src, dst):
                link(nc.gpsimd.tensor_copy(dst[:, 0], src[:]))
                link(nc.gpsimd.tensor_tensor(rest[:], src[:], dst[:, 0], ALU.subtract))
                link(nc.gpsimd.tensor_copy(dst[:, 1], rest[:]))
                return nc.gpsimd.tensor_tensor(dst[:, 2], rest[:], dst[:, 1], ALU.subtract)

            def inverse_root(n, which):
                hold(pool, var_ready[which], n + 1)
                nc.gpsimd.tensor_tensor(rstd[which][:], var_eps[which][:], minus_half[:], ALU.pow).then_inc(rstd_ready[which], 1)

            def cut_k(n):
                hold(pool, k_evac, n + 1)
                wait(pool, k_stored, 16 * n)
                wait(pool, q_split, n)
                cut(yk, kparts).then_inc(k_split, 1)

            def cut_q(n):
                hold(pool, q_evac, n + 1)
                wait(pool, q_stored, 16 * n)
                hold(pool, k_split, n + 1)
                cut(yq, qparts).then_inc(q_split, 1)

            def residual(n):
                hold(pool, xres_full, 16 * (n + 1))
                if isinstance(n, int) and n == 0:
                    hold(pool, obias_ready, 1)
                nc.gpsimd.tensor_tensor(xres[:], xres[:], out_bias[:].unsqueeze(1).broadcast_to([P, C, D]),
                                        ALU.add).then_inc(xb_ready, 1)

            hold(pool, pool_ready, 1)
            inverse_root(0, 0)
            cut_k(0)
            cut_q(0)

            def body(t, par, weights, nxt):
                n = 2 * t + par
                post = not isinstance(n, int) or n > 0
                if nxt:
                    inverse_root(n + 1, 0)
                if weights:
                    i = 2 * (t - 1) + par
                    hold(pool, w_full, 16 * (2 * i + 1))
                    nc.gpsimd.tensor_scalar(wst[0][:], wst[0][:], WSCALE, None, ALU.mult).then_inc(w_scaled, 1)
                if post:
                    residual(n - 1)
                if weights:
                    hold(pool, w_hi, 2 * i + 1)
                    nc.gpsimd.tensor_tensor(weight_at(t - 1, 0, 1, par * HALF, (par + 1) * HALF), wst[0][:],
                                            weight_at(t - 1, 0, 0, par * HALF, (par + 1) * HALF), ALU.subtract).then_inc(w_lo, 1)
                if nxt:
                    cut_k(n + 1)
                if post:
                    inverse_root(n - 1, 1)
                if nxt:
                    cut_q(n + 1)
                if weights:
                    hold(pool, w_full, 16 * (2 * i + 2))
                    nc.gpsimd.tensor_scalar(wst[0][:], wst[0][:], WSCALE, None, ALU.mult).then_inc(w_scaled, 1)
                    hold(pool, w_hi, 2 * i + 2)
                    nc.gpsimd.tensor_tensor(weight_at(t - 1, 1, 1, par * HALF, (par + 1) * HALF), wst[0][:],
                                            weight_at(t - 1, 1, 0, par * HALF, (par + 1) * HALF), ALU.subtract).then_inc(w_lo, 1)

            PER_BODY = 6
            body(0, 0, False, True)
            body(0, 1, False, True)
            with pool.Fori(1, NB // 2 - 1) as t:
                chain[1] = (t - 1) * (2 * PER_BODY)
                was = chain[0]
                body(t, 0, True, True)
                body(t, 1, True, True)
                assert chain[0] == was + 2 * PER_BODY
            chain[0], chain[1] = was + (NB // 2 - 2) * 2 * PER_BODY, 0
            body(NB // 2 - 1, 0, False, True)
            body(NB // 2 - 1, 1, False, False)

            def late_scale(i):
                hold(pool, late_full[i % 2], 16 * (i // 2 + 1))
                nc.gpsimd.tensor_scalar(late_stage[i % 2][:], late_stage[i % 2][:], WSCALE, None, ALU.mult).then_inc(late_scaled, 1)

            def late_low(i):
                e, w, half = LATE[i]
                hold(pool, late_hi, i + 1)
                nc.gpsimd.tensor_tensor(wall[:, e, w, 1, half * HALF:(half + 1) * HALF], late_stage[i % 2][:],
                                        wall[:, e, w, 0, half * HALF:(half + 1) * HALF], ALU.subtract).then_inc(late_lo, 1)

            late_scale(0)
            residual(NB - 1)
            inverse_root(NB - 1, 1)
            hold(pool, lg_evac, NB)
            hold(pool, x1_stored, 16 * NB)
            hold(pool, xn2_stored, 16 * NB)
            nc.gpsimd.iota(iota_e[:], [[1, E]], base=-E, channel_multiplier=0, allow_small_or_imprecise_dtypes=True)
            nc.gpsimd.iota(iota_b[:], [[1, P]], base=0, channel_multiplier=0, allow_small_or_imprecise_dtypes=True)
            nc.gpsimd.iota(unused_row[:], [[P, NT]], base=2 * T - T // 2, channel_multiplier=1, allow_small_or_imprecise_dtypes=True)
            nc.gpsimd.memset(onesf[:], 1.0)
            nc.gpsimd.iota(tok_val[:], [[P, NI]], base=-T // 2, channel_multiplier=1,
                           allow_small_or_imprecise_dtypes=True).then_inc(iota_ready, 1)
            for i in range(len(LATE)):
                if i + 1 < len(LATE):
                    late_scale(i + 1)
                late_low(i)

            hold(pool, lists_ready, 3)

            def gather(j, half, par):
                wait(pool, xg_full[par], 16 * half)
                nc.gpsimd.tensor_copy(gather_idx[par][:], slot_token[:, ds(j, 1)]).then_inc(idx_ready, 1)
                hold(pool, idx_ready, j + 1)
                wait(pool, gT_done, j - 1)
                nc.gpsimd.indirect_dma_start(xg[par][:], None, xn2_d,
                                             bass.IndirectOffsetOnAxis(gather_idx[par][:, 0:1], 0)).then_inc(xg_full[par], 16)

            def scatter(j, half, par):
                wait(pool, y_sent[par], 16 * half)
                nc.gpsimd.tensor_copy(dest_idx[par][:], slot_dest[:, ds(j, 1)]).then_inc(dest_ready, 1)
                hold(pool, dest_ready, j + 1)
                hold(pool, y_ready, j + 1)
                nc.gpsimd.indirect_dma_start(y_d, bass.IndirectOffsetOnAxis(dest_idx[par][:, 0:1], 0),
                                             yb[par][:], None).then_inc(y_sent[par], 16)

            gather(0, 0, 0)
            gather(1, 0, 1)
            scatter_from = 0
            for j in range(2):
                gather(j + 2, 1, j)
                scatter(j, 0, j)
            with pool.Fori(1, (NT - 3) // 2) as t:
                for par in range(2):
                    gather(2 * t + par + 2, t + 1, par)
                    scatter(2 * t + par, t, par)
            for j in range(NT - 3, NT):
                if j + 2 < NT:
                    gather(j + 2, (j + 2) // 2, j % 2)
                scatter(j, j // 2, j % 2)

        @block.scalar
        def _(act):
            act.dma_start(tanh_x[:], g_xattn.partition_broadcast(P)).then_inc(tanh_ready, 16)
            act.dma_start(tanh_f[:], g_ffn.partition_broadcast(P)).then_inc(tanh_ready, 16)
            act.wait_ge(tanh_ready, 32)
            nc.scalar.activation(tanh_x[:], tanh_x[:], ACT.Tanh).then_inc(tanh_ready, 1)
            nc.scalar.activation(tanh_f[:], tanh_f[:], ACT.Tanh).then_inc(tanh_ready, 1)
            act.wait_ge(b1t_done, 1)
            nc.scalar.activation(bias_col[:].rearrange("p i m -> p (i m)"), banks[:, 7, E * HC:E * HC + 3 * M], ACT.Copy).then_inc(biases_ready, 1)
            nc.scalar.activation(b1_col[:], banks[:, 7, 0:E * HC], ACT.Copy, scale=HSCALE).then_inc(biases_ready, 1)
            act.wait_ge(biases_ready, 1)
            act.wait_ge(pool_ready, 1)
            for m in range(M):
                ins = nc.scalar.activation(probs[0][:, m, 0:P], ident[:], ACT.Identity, bias=bias_col[:, 2, m:m + 1], scale=0.0)
            ins.then_inc(bvcol_ready, 1)

            def norm_T(n):
                act.wait_ge(xT_done, n + 1)
                wait(act, q_done, n)
                nc.scalar.activation(xnT[:].rearrange("p m t -> p (m t)"), bank(2), ACT.Copy).then_inc(xT_evac, 1)

            def context_T(n):
                act.wait_ge(ctxT_done, n + 1)
                wait(act, v_done, n)
                nc.scalar.activation(ctxT[:].rearrange("p m t -> p (m t)"), bank(3), ACT.Copy).then_inc(ctxT_evac, 1)

            def biased(n, which, src, done, split, dst, evac):
                act.wait_ge(done, n + 1)
                wait(act, split, n)
                for m in range(M):
                    ins = nc.scalar.activation(dst[:, m, :], banks[:, src, m * L:(m + 1) * L], ACT.Identity,
                                               bias=bias_col[:, which, m:m + 1])
                ins.then_inc(evac, 1)

            def values(n, par):
                act.wait_ge(v_done, n + 1)
                wait(act, av_mm, 8 * (n - 1))
                for c in range(C):
                    ins = nc.scalar.activation(vaug[par][:, c, :, 0:DH], banks[:, 2, c * D:(c + 1) * D].rearrange("p (h d) -> p h d", d=DH), ACT.Copy)
                ins.then_inc(v_evac, 1)

            def prep(n, par):
                context_T(n)
                norm_T(n)
                biased(n, 1, 7, k_done, k_split, yk, k_evac)
                biased(n, 0, 6, q_done, q_split, yq, q_evac)
                values(n, par)

            def attended_T(n):
                act.wait_ge(cT_done, n + 1)
                wait(act, lg_done, n)
                nc.scalar.activation(cT[:].rearrange("p m t -> p (m t)"), bank(3), ACT.Copy).then_inc(cT_evac, 1)

            def norm2_T(n):
                act.wait_ge(x2T_done, n + 1)
                act.wait_ge(o_done, n + 1)
                nc.scalar.activation(cT[:].rearrange("p m t -> p (m t)"), bank(5), ACT.Copy).then_inc(x2T_evac, 1)

            prep(0, 0)

            def body(t, par, weights, nxt):
                n = 2 * t + par
                post = not isinstance(n, int) or n > 0

                def high(w):
                    i = 2 * (2 * (t - 1) + par) + w
                    act.wait_ge(w_scaled, i + 1)
                    nc.scalar.activation(weight_at(t - 1, w, 0, par * HALF, (par + 1) * HALF), wst[0][:], ACT.Copy).then_inc(w_hi, 1)

                if weights:
                    high(0)
                if nxt:
                    prep(n + 1, 1 - par)
                if post:
                    attended_T(n - 1)
                    norm2_T(n - 1)
                for v in range(8):
                    act.wait_ge(st_done, 8 * n + v + 1)
                    wait(act, av_mm, 8 * n + v - 1)
                    nc.scalar.activation(probs[v % 2][:].rearrange("p h t -> p (h t)"),
                                         banks[:, 2 + 2 * (v % 2):4 + 2 * (v % 2), :].rearrange("p b t -> p (b t)"),
                                         ACT.Exp, scale=float(DH) ** -0.5).then_inc(exp_done, 1)
                    if weights and v == 3:
                        high(1)

            bodies(act, body)

            def late_high(i):
                e, w, half = LATE[i]
                act.wait_ge(late_scaled, i + 1)
                nc.scalar.activation(wall[:, e, w, 0, half * HALF:(half + 1) * HALF], late_stage[i % 2][:], ACT.Copy).then_inc(late_hi, 1)

            late_high(0)
            attended_T(NB - 1)
            norm2_T(NB - 1)
            for i in range(1, 2):
                late_high(i)
            act.wait_ge(diff_ready, 1)
            nc.scalar.activation(gexp[:], gexp[:], ACT.Exp).then_inc(gexp_ready, 1)
            for i in range(2, len(LATE)):
                late_high(i)

            act.wait_ge(lists_ready, 3)

            def high_x(j, par):
                act.wait_ge(gT_done, j + 1)
                wait(act, h_done, 2 * (j - 1))
                nc.scalar.activation(xh[par][:].rearrange("p m t -> p (m t)"), banks[:, par, 0:M * P], ACT.Copy,
                                     scale=WSCALE).then_inc(xh_ready, 1)

            def relu(j, par):
                e = act.value_load(tile_expert[0:1, ds(j, 1)], min_val=0, max_val=E - 1)
                wait(act, hl_ready, j - 1)
                for half in range(2):
                    act.wait_ge(h_done, 2 * j + half + 1)
                    for i in range(HC // 2):
                        c = half * (HC // 2) + i
                        ins = nc.scalar.activation(hid[par][:, c * P:(c + 1) * P], banks[:, 2 + 2 * par + half, i * P:(i + 1) * P],
                                                   ACT.Relu, bias=b1_col[:, ds(e * HC + c, 1)], scale=HSCALE / WSCALE / WSCALE)
                    ins.then_inc(hid_ready, 1)

            high_x(0, 0)
            high_x(1, 1)
            relu(0, 0)
            for j in range(2):
                high_x(j + 2, j)
                relu(j + 1, 1 - j)
            with act.Fori(1, (NT - 3) // 2) as t:
                for par in range(2):
                    high_x(2 * t + par + 2, par)
                    relu(2 * t + par + 1, 1 - par)
            for j in range(NT - 3, NT):
                if j + 2 < NT:
                    high_x(j + 2, j % 2)
                if j + 1 < NT:
                    relu(j + 1, (j + 1) % 2)
            for i in range(NI // DT):
                act.wait_ge(out_ready, i + 1)
                act.dma_start(out.rearrange("b (c p) d -> p (b c) d", p=P)[:, i * DT:(i + 1) * DT, :], y1b[i % 2][:]).then_inc(out_sent[i % 2], 16)

        @block.vector
        def _(dve):
            chain = [0, 0]

            def link(ins):
                chain[0] += 1
                ins.then_inc(dve_chain, 1)
                dve.wait_ge(dve_chain, chain[0] + chain[1])

            dve.wait_ge(consts, 16 * N_CONST)
            dve.wait_ge(bvwo_done, 1)
            dve.wait_ge(tanh_ready, 34)
            link(nc.vector.tensor_tensor(out_bias[:], banks[:, 6, 0:D], bo_b[:], ALU.add))
            nc.vector.tensor_scalar(out_bias[:], out_bias[:], tanh_x[:], None, ALU.mult).then_inc(obias_ready, 1)

            def variance(src, which):
                for c in range(C):
                    ins = nc.vector.bn_stats(stats[:, c, :], src[:, c, :])
                chain[0] += 1
                ins.then_inc(dve_chain, 1)
                hold(dve, dve_chain, chain[0] + chain[1])
                for c in range(C):
                    ins = nc.vector.bn_aggr(mean_var[which][:, c, :], stats[:, c, :])
                link(ins)
                nc.vector.tensor_scalar(var_eps[which][:], mean_var[which][:, :, 1], EPS, None, ALU.add).then_inc(var_ready[which], 1)

            def normalize(n, src, dst, which, ready):
                dve.wait_ge(rstd_ready[which], n + 1)
                for c in range(C):
                    nc.vector.tensor_scalar(dst[:, c, :], src[:, c, :], mean_var[which][:, c, 0:1], rstd[which][:, c:c + 1],
                                            ALU.subtract, ALU.mult).then_inc(ready, 1)

            def norm1_stats(n, t, par):
                dve.wait_ge(xin_full[par], 16 * (t + 1))
                variance(xin[par], 0)

            def norm1(n, par):
                wait(dve, xT_done, n)
                normalize(n, xin[par], xn, 0, xn_ready)

            def attended(n, c):
                dve.wait_ge(tok_done, 2 * n + c + 1)
                rows = bank(4 + c).rearrange("p (h w) -> p h w", w=32)
                link(nc.vector.reciprocal(recip[c][:].unsqueeze(2), rows[:, :, DH:DH + 1]))
                if c == 0:
                    wait(dve, cT_done, n)
                nc.vector.tensor_tensor(cn[:, c, :].rearrange("p (h d) -> p h d", d=DH), rows[:, :, 0:DH],
                                        recip[c][:].unsqueeze(2).broadcast_to([P, NH, DH]), ALU.mult).then_inc(cn_ready, 1)

            def residual(n):
                dve.wait_ge(o_done, n + 1)
                dve.wait_ge(xb_ready, n + 1)
                wait(dve, x1_stored, 16 * n)
                for c in range(C):
                    nc.vector.scalar_tensor_tensor(out=x1b[:, c, :], in0=banks[:, 4, c * D:(c + 1) * D], scalar=tanh_x[:],
                                                   in1=xres[:, c, :], op0=ALU.mult, op1=ALU.add).then_inc(x1_ready, 1)

            def norm2_stats(n):
                dve.wait_ge(x1_ready, 2 * (n + 1))
                variance(x1b, 1)

            def norm2(n):
                wait(dve, xn2_stored, 16 * n)
                wait(dve, x2T_done, n)
                normalize(n, x1b, xn2b, 1, xn2_ready)

            def router(n):
                dve.wait_ge(lg_done, n + 1)
                nc.vector.tensor_tensor(logits[:, ds(n * C, C), :], banks[:, 6, 0:C * E].rearrange("p (c e) -> p c e", e=E),
                                        br_b[:].unsqueeze(1).broadcast_to([P, C, E]), ALU.add).then_inc(lg_evac, 1)

            def reduce(n, u):
                hp, c = u // 2, u % 2
                dve.wait_ge(mx_done, 16 * n + u + 1)
                if u % 8 == 0:
                    wait(dve, nm_done, 2 * n - 1 + u // 8)
                nc.vector.tensor_reduce(negmax[:, c, 2 * hp:2 * hp + 2], bank(u % 2).rearrange("p (h k) -> p h k", k=L),
                                        AX.X, ALU.max, negate=True).then_inc(mx_red, 1)

            def max_row(n, s):
                dve.wait_ge(nm_done, 2 * n + s + 1)
                wait(dve, row_full[s], 16 * n)
                nc.vector.tensor_copy(negmax_row[s][:], banks[0:8, 7, 0:L]).then_inc(nm_evac, 1)

            norm1_stats(0, 0, 0)
            norm1(0, 0)

            def body(t, par, weights, nxt):
                n = 2 * t + par
                post = not isinstance(n, int) or n > 0
                if nxt:
                    norm1_stats(n + 1, t + par, 1 - par)
                for u in range(16):
                    reduce(n, u)
                    if nxt and u == 1:
                        norm1(n + 1, 1 - par)
                    if post and u in (3, 4):
                        attended(n - 1, u - 3)
                    if u == 10:
                        max_row(n, 0)
                    if post and u == 11:
                        residual(n - 1)
                        norm2_stats(n - 1)
                    if post and u == 13:
                        norm2(n - 1)
                max_row(n, 1)
                if post:
                    router(n - 1)
                for g in range(4):
                    dve.wait_ge(av_mm, 8 * n + 2 * g + 2)
                    if g == 0:
                        wait(dve, tok_done, 2 * n)
                    nc.vector.tensor_copy(oT[:, g, :], banks[:, 6 + g % 2, 0:L]).then_inc(av_evac, 1)

            PER_BODY = 2 + 2 + 2
            body(0, 0, False, True)
            body(0, 1, False, True)
            with dve.Fori(1, NB // 2 - 1) as t:
                chain[1] = (t - 1) * (2 * PER_BODY)
                was = chain[0]
                body(t, 0, True, True)
                body(t, 1, True, True)
                assert chain[0] == was + 2 * PER_BODY, (chain, was)
            chain[0], chain[1] = was + (NB // 2 - 2) * 2 * PER_BODY, 0
            body(NB // 2 - 1, 0, False, True)
            body(NB // 2 - 1, 1, False, False)
            attended(NB - 1, 0)
            attended(NB - 1, 1)
            residual(NB - 1)
            norm2_stats(NB - 1)
            norm2(NB - 1)
            router(NB - 1)

            dve.wait_ge(iota_ready, 1)
            dve.wait_ge(lg_evac, NB)
            dve.wait_ge(xn2_stored, 16 * NB)
            dve.wait_ge(x1_stored, 16 * NB)

            def over_e(a):
                return a.unsqueeze(2).broadcast_to([P, NI, E])

            iota_ie = iota_e[:].unsqueeze(1).broadcast_to([P, NI, E])

            def choose(values, best, onehot):
                link(nc.vector.tensor_reduce(best[:], values[:], AX.X, ALU.max))
                link(nc.vector.tensor_tensor(t3[:], values[:], over_e(best[:]), ALU.is_equal))
                link(nc.vector.tensor_tensor(t3[:], t3[:], iota_ie, ALU.mult))
                link(nc.vector.tensor_reduce(index[:], t3[:], AX.X, ALU.min))
                link(nc.vector.tensor_tensor(onehot[:], iota_ie, over_e(index[:]), ALU.is_equal))

            choose(logits, best1, oh1)
            link(nc.vector.scalar_tensor_tensor(out=masked[:], in0=oh1[:], scalar=-BIG, in1=logits[:], op0=ALU.mult, op1=ALU.add))
            choose(masked, best2, oh2)
            nc.vector.tensor_tensor(picked[:], oh1[:], oh2[:], ALU.add).then_inc(picked_ready, 1)
            nc.vector.tensor_tensor(gexp[:], best2[:], best1[:], ALU.subtract).then_inc(diff_ready, 1)
            dve.wait_ge(rank_done, 1)
            link(nc.vector.tensor_copy(totals[:], bank(1)[:, 0:NI * E].rearrange("p (i e) -> p e i", e=E)))
            tot = totals[:].rearrange("p e i -> p (e i)")
            bef = before[:].rearrange("p e i -> p (e i)")
            link(nc.vector.tensor_tensor_scan(bef, onesf[:], tot, 0.0, ALU.mult, ALU.add))
            link(nc.vector.memset(e_end[:, 0:1], 0.0))
            link(nc.vector.tensor_copy(e_end[:, 1:E + 1], before[:, :, NI - 1]))
            link(nc.vector.tensor_tensor(bef, bef, tot, ALU.subtract))
            link(nc.vector.tensor_tensor(e_cnt[:], e_end[:, 1:E + 1], e_end[:, 0:E], ALU.subtract))
            link(nc.vector.tensor_scalar(e_int[:], e_cnt[:], float(P - 1), None, ALU.add))
            link(nc.vector.tensor_scalar(e_int[:], e_int[:], 7, None, ALU.arith_shift_right))
            link(nc.vector.tensor_copy(e_tiles[:], e_int[:]))
            link(nc.vector.memset(t_end[:, 0:1], 0.0))
            link(nc.vector.tensor_tensor_scan(t_end[:, 1:E + 1], onesf[:, 0:E], e_tiles[:], 0.0, ALU.mult, ALU.add))
            link(nc.vector.scalar_tensor_tensor(out=e_off[:], in0=t_end[:, 0:E], scalar=float(P), in1=e_end[:, 0:E],
                                                op0=ALU.mult, op1=ALU.subtract))
            link(nc.vector.tensor_tensor(t3[:], before[:].rearrange("p e i -> p i e"),
                                         e_off[:].unsqueeze(1).broadcast_to([P, NI, E]), ALU.add))
            link(nc.vector.tensor_tensor(t3[:], bank(0)[:, 0:NI * E].rearrange("p (i e) -> p i e", e=E), t3[:], ALU.add))
            for k, oh in enumerate((oh1, oh2)):
                link(nc.vector.tensor_tensor(oh[:], oh[:], t3[:], ALU.mult))
                link(nc.vector.tensor_reduce(slot[:, k, :], oh[:], AX.X, ALU.add))
            link(nc.vector.tensor_copy(slot_i[:], slot[:]))
            link(nc.vector.tensor_scalar(slot_t[:], slot_i[:], 7, None, ALU.arith_shift_right))
            link(nc.vector.tensor_copy(slot_col[:], slot_t[:]))
            link(nc.vector.tensor_scalar(slot_t[:], slot_i[:], P - 1, None, ALU.bitwise_and))
            link(nc.vector.tensor_copy(slot_row[:], slot_t[:]))
            link(nc.vector.tensor_scalar(tok_neg[:], tok_val[:], 0.0, None, ALU.is_ge))
            link(nc.vector.tensor_tensor(tok_val[:], tok_val[:], tok_neg[:], ALU.add))
            for n in range(2 * NI):
                k, i = n // NI, n % NI
                if n >= NHOT:
                    dve.wait_ge(hot_used, n - NHOT + 1)
                nc.vector.tensor_scalar(hot_row[:, n % NHOT, :], iota_b[:], slot_row[:, k, i:i + 1], None, ALU.is_equal)
                nc.vector.tensor_scalar(hot_col[:, n % NHOT, :], iota_b[:, 0:NT], slot_col[:, k, i:i + 1], tok_val[:, i:i + 1],
                                        ALU.is_equal, ALU.mult).then_inc(hot_ready, 1)
            dve.wait_ge(gexp_ready, 1)
            link(nc.vector.tensor_scalar(index[:], gexp[:], 1.0, None, ALU.add))
            link(nc.vector.reciprocal(index[:], index[:]))
            link(nc.vector.tensor_scalar(gate1[:], index[:], tanh_f[:], None, ALU.mult))
            link(nc.vector.tensor_tensor(gate2[:], gate1[:], gexp[:], ALU.mult))
            link(nc.vector.tensor_tensor(te3[:], iota_b[0:1, 0:NT].unsqueeze(2).broadcast_to([1, NT, E]),
                                         t_end[0:1, 1:E + 1].unsqueeze(1).broadcast_to([1, NT, E]), ALU.is_ge))
            link(nc.vector.tensor_reduce(tsum[0:1, :], te3[:], AX.X, ALU.add))
            nc.vector.tensor_scalar(tile_expert[:], tsum[0:1, :], float(E - 1), None, ALU.min).then_inc(lists_ready, 1)
            dve.wait_ge(hot_used, 2 * NI)
            link(nc.vector.tensor_copy(tval[:], banks[:, 2, 0:2 * NT].rearrange("p (k j) -> p k j", k=2)))
            link(nc.vector.tensor_tensor(tsum[:], tval[:, 0, :], tval[:, 1, :], ALU.add))
            link(nc.vector.tensor_scalar(tflag[:], tsum[:], 0.0, None, ALU.is_gt))
            link(nc.vector.tensor_tensor(tfull[:], tsum[:], tflag[:], ALU.subtract))
            link(nc.vector.tensor_scalar(tfull[:], tfull[:], float(T // 2), None, ALU.add))
            nc.vector.tensor_copy(slot_token[:], tfull[:]).then_inc(lists_ready, 1)
            link(nc.vector.tensor_scalar(tflag[:], tval[:, 1, :], 0.0, float(T), ALU.not_equal, ALU.mult))
            link(nc.vector.tensor_tensor(tfull[:], tfull[:], tflag[:], ALU.add))
            link(nc.vector.scalar_tensor_tensor(out=tflag[:], in0=tsum[:], scalar=0.0, in1=unused_row[:], op0=ALU.is_equal, op1=ALU.mult))
            nc.vector.tensor_tensor(slot_dest[:], tfull[:], tflag[:], ALU.add).then_inc(lists_ready, 1)

            dve.wait_ge(lists_ready, 3)
            dve.wait_ge(b2_full, 16)

            def low_x(j, par):
                dve.wait_ge(xh_ready, j + 1)
                nc.vector.scalar_tensor_tensor(out=xl[par][:].rearrange("p m t -> p (m t)"), in0=banks[:, par, 0:M * P], scalar=WSCALE,
                                               in1=xh[par][:].rearrange("p m t -> p (m t)"), op0=ALU.mult,
                                               op1=ALU.subtract).then_inc(xl_ready, 1)

            def cut_hidden(j, par):
                dve.wait_ge(hid_ready, 2 * (j + 1))
                wait(dve, y_done, j - 1)
                nc.vector.tensor_copy(hh[par][:], hid[par][:]).then_inc(hh_ready, 1)
                dve.wait_ge(hh_ready, j + 1)
                nc.vector.tensor_tensor(hl[par][:], hid[par][:], hh[par][:], ALU.subtract).then_inc(hl_ready, 1)

            def result(j, half, par):
                e = dve.value_load(tile_expert[0:1, ds(j, 1)], min_val=0, max_val=E - 1)
                dve.wait_ge(y_done, j + 1)
                wait(dve, y_sent[par], 16 * half)
                nc.vector.scalar_tensor_tensor(out=yb[par][:], in0=banks[:, 6 + par, 0:D], scalar=1.0 / HSCALE / WSCALE,
                                               in1=b2_b[:, ds(e, 1), :].rearrange("p e d -> p (e d)"), op0=ALU.mult, op1=ALU.add).then_inc(y_ready, 1)

            low_x(0, 0)
            low_x(1, 1)
            cut_hidden(0, 0)
            for j in range(2):
                low_x(j + 2, j)
                cut_hidden(j + 1, 1 - j)
                result(j, 0, j)
            with dve.Fori(1, (NT - 3) // 2) as t:
                for par in range(2):
                    low_x(2 * t + par + 2, par)
                    cut_hidden(2 * t + par + 1, 1 - par)
                    result(2 * t + par, t, par)
            for j in range(NT - 3, NT):
                if j + 2 < NT:
                    low_x(j + 2, j % 2)
                if j + 1 < NT:
                    cut_hidden(j + 1, (j + 1) % 2)
                result(j, j // 2, j % 2)

            dve.wait_ge(x1_full, 16)
            for i in range(NI // DT):
                dve.wait_ge(y_back[i % 2], 32 * (i // 2 + 1))
                for k in range(DT):
                    n = i * DT + k
                    ins = nc.vector.scalar_tensor_tensor(out=y1b[i % 2][:, k, :], in0=y1b[i % 2][:, k, :], scalar=gate1[:, n:n + 1],
                                                         in1=x1_all[:, n, :], op0=ALU.mult, op1=ALU.add)
                link(ins)
                for k in range(DT):
                    n = i * DT + k
                    ins = nc.vector.scalar_tensor_tensor(out=y1b[i % 2][:, k, :], in0=y2b[i % 2][:, k, :], scalar=gate2[:, n:n + 1],
                                                         in1=y1b[i % 2][:, k, :], op0=ALU.mult, op1=ALU.add)
                ins.then_inc(out_ready, 1)

        @block.tensor
        def _(pe):
            pe.wait_ge(pool_ready, 1)
            pe.wait_ge(consts, 16 * N_CONST)
            NV = E * HC + 3 * M
            nc.tensor.transpose(banks[:, 7, 0:NV], oT[0:NV, 0, 0:P], ident[0:NV, 0:NV]).then_inc(b1t_done, 1)
            pe.wait_ge(bvcol_ready, 1)
            for m in range(M):
                ins = nc.tensor.matmul(banks[:, 6, 0:D], probs[0][:, m, 0:P], wo[:, m, :], start=(m == 0), stop=(m == M - 1))
            ins.then_inc(bvwo_done, 1)

            def turn(src, dst_bank, done):
                for c in range(C):
                    for m in range(M):
                        ins = nc.tensor.transpose(banks[:, dst_bank, m * L + c * P:m * L + (c + 1) * P], src[:, c, m * P:(m + 1) * P], ident[:])
                ins.then_inc(done, 1)

            def norm_T(n):
                pe.wait_ge(xn_ready, 2 * (n + 1))
                wait(pe, exp_done, 8 * (n - 2) + 7)
                if isinstance(n, int):
                    wait(pe, v_evac, n)
                turn(xn, 2, xT_done)

            def context_T(n, t, par):
                pe.wait_ge(cin_full[par], 16 * (t + 1))
                wait(pe, exp_done, 8 * (n - 2) + 7)
                if isinstance(n, int):
                    wait(pe, ctxT_evac, n)
                turn(cin[par], 3, ctxT_done)

            def project_T(n, w, src, dst_bank, done):
                for m in range(M):
                    for k in range(M):
                        ins = nc.tensor.matmul(banks[:, dst_bank, m * L:(m + 1) * L], w[:, k, m * P:(m + 1) * P], src[:, k, :],
                                               start=(k == 0), stop=(k == M - 1))
                ins.then_inc(done, 1)

            def q(n):
                pe.wait_ge(xT_evac, n + 1)
                if isinstance(n, int) and n == 0:
                    pe.wait_ge(obias_ready, 1)
                wait(pe, av_evac, 4 * (n - 2) + 3)
                if isinstance(n, int):
                    wait(pe, q_evac, n)
                project_T(n, wq, xnT, 6, q_done)

            def k(n):
                pe.wait_ge(ctxT_evac, n + 1)
                if isinstance(n, int) and n == 0:
                    pe.wait_ge(biases_ready, 2)
                wait(pe, av_evac, 4 * (n - 1))
                if isinstance(n, int):
                    wait(pe, k_evac, n)
                project_T(n, wk, ctxT, 7, k_done)

            def v(n):
                pe.wait_ge(xT_evac, n + 1)
                for c in range(C):
                    for m in range(M):
                        ins = nc.tensor.matmul(banks[:, 2, c * D:(c + 1) * D], ctxT[:, m, c * P:(c + 1) * P], wv[:, m, :],
                                               start=(m == 0), stop=(m == M - 1))
                ins.then_inc(v_done, 1)

            def scores_max(n, par, u):
                hp, c = u // 2, u % 2
                if u == 0:
                    pe.wait_ge(qs_full, 16 * NTERM * (n + 1))
                    pe.wait_ge(ks_full, 16 * NTERM * (n + 1))
                wait(pe, mx_red, 16 * n + u - 1)
                for i in range(2):
                    h = 2 * hp + i
                    ins = nc.tensor.matmul(banks[:, u % 2, i * L:(i + 1) * L], qs[par][0:KR, h, c * P:(c + 1) * P], ks[par][0:KR, h, :],
                                           start=True, stop=True)
                ins.then_inc(mx_done, 1)

            def turn_max(n, s, nxt):
                pe.wait_ge(mx_red, 16 * n + 8 * (s + 1))
                if s == 0:
                    if nxt:
                        pe.wait_ge(k_evac, n + 2)
                    else:
                        pe.wait_ge(av_evac, 4 * n)
                else:
                    pe.wait_ge(nm_evac, 2 * n + 1)
                for c in range(C):
                    ins = nc.tensor.matmul(banks[0:8, 7, c * P:(c + 1) * P], negmax[:, c, 8 * s:8 * s + 8], ident[:], start=True, stop=True)
                ins.then_inc(nm_done, 1)

            def scores(n, par, v_, nxt, post):
                g, c = v_ // 2, v_ % 2
                if v_ in (0, 4):
                    pe.wait_ge(row_full[v_ // 4], 16 * (n + 1))
                if v_ == 0 and nxt:
                    pe.wait_ge(v_evac, n + 2)
                if v_ == 0 and post:
                    pe.wait_ge(cT_evac, n)
                if v_ == 1 and post:
                    pe.wait_ge(x1_ready, 2 * n)
                    pe.wait_ge(x2T_evac, n)
                if v_ >= 2:
                    pe.wait_ge(exp_done, 8 * n + v_ - 1)
                for j in range(4):
                    h = 4 * g + j
                    ins = nc.tensor.matmul(banks[:, 2 + 2 * (v_ % 2) + j // 2, (j % 2) * L:(j % 2 + 1) * L],
                                           ks[par][0:KR + 1, h, c * P:(c + 1) * P], qs[par][0:KR + 1, h, :], start=True, stop=True)
                ins.then_inc(st_done, 1)

            def attend(n, par, v_, post):
                g, c = v_ // 2, v_ % 2
                pe.wait_ge(exp_done, 8 * n + v_ + 1)
                if v_ == 0:
                    pe.wait_ge(v_evac, n + 1)
                    if post:
                        pe.wait_ge(lg_evac, n)
                if v_ == 2:
                    pe.wait_ge(nm_evac, 2 * n + 2)
                if c == 0 and g >= 2:
                    pe.wait_ge(av_evac, 4 * n + g - 1)
                for j in range(4):
                    ins = nc.tensor.matmul(banks[32 * j:32 * j + 32, 6 + g % 2, 0:L], vaug[par][:, c, 4 * g + j, :],
                                           probs[v_ % 2][:, j, :], start=(c == 0), stop=(c == C - 1))
                ins.then_inc(av_mm, 1)

            def turn_out(n, c):
                pe.wait_ge(av_evac, 4 * (n + 1))
                pe.wait_ge(exp_done, 8 * (n + 1))
                for g in range(4):
                    ins = nc.tensor.transpose(banks[:, 4 + c, g * P:(g + 1) * P], oT[:, g, c * P:(c + 1) * P], ident[:])
                ins.then_inc(tok_done, 1)

            def attended_T(n, nxt):
                pe.wait_ge(cn_ready, 2 * (n + 1))
                if nxt:
                    pe.wait_ge(ctxT_evac, n + 3)
                turn(cn, 3, cT_done)

            def output(n):
                pe.wait_ge(cT_evac, n + 1)
                for c in range(C):
                    for m in range(M):
                        ins = nc.tensor.matmul(banks[:, 4, c * D:(c + 1) * D], cT[:, m, c * P:(c + 1) * P], wo[:, m, :],
                                               start=(m == 0), stop=(m == M - 1))
                ins.then_inc(o_done, 1)

            def norm2_T(n):
                pe.wait_ge(xn2_ready, 2 * (n + 1))
                turn(xn2b, 5, x2T_done)

            def router(n, nxt):
                pe.wait_ge(x2T_evac, n + 1)
                if nxt:
                    pe.wait_ge(q_evac, n + 3)
                for c in range(C):
                    for m in range(M):
                        ins = nc.tensor.matmul(banks[:, 6, c * E:(c + 1) * E], cT[:, m, c * P:(c + 1) * P], wr[:, m, :],
                                               start=(m == 0), stop=(m == M - 1))
                ins.then_inc(lg_done, 1)

            context_T(0, 0, 0)
            norm_T(0)
            k(0)
            q(0)
            v(0)

            def body(t, par, weights, nxt):
                n = 2 * t + par
                post = not isinstance(n, int) or n > 0
                for u in range(16):
                    scores_max(n, par, u)
                    if nxt:
                        if u == 1:
                            context_T(n + 1, t + par, 1 - par)
                        if u == 4:
                            norm_T(n + 1)
                        if u == 5:
                            k(n + 1)
                        if u == 6:
                            q(n + 1)
                        if u == 7:
                            v(n + 1)
                    if post:
                        if u in (2, 3):
                            turn_out(n - 1, u - 2)
                        if u == 8:
                            attended_T(n - 1, nxt)
                        if u == 10:
                            output(n - 1)
                        if u == 15:
                            norm2_T(n - 1)
                    if u == 9:
                        turn_max(n, 0, nxt)
                turn_max(n, 1, nxt)
                if post:
                    router(n - 1, nxt)
                for v_ in range(8):
                    scores(n, par, v_, nxt, post)
                    if v_ >= 1:
                        attend(n, par, v_ - 1, post)
                attend(n, par, 7, post)

            bodies(pe, body)
            turn_out(NB - 1, 0)
            turn_out(NB - 1, 1)
            attended_T(NB - 1, False)
            output(NB - 1)
            norm2_T(NB - 1)
            router(NB - 1, False)

            pe.wait_ge(picked_ready, 1)
            flat = picked[:].rearrange("p i e -> p (i e)")
            nc.tensor.matmul(banks[:, 0, 0:NI * E], tri[:], flat, start=True, stop=True)
            nc.tensor.matmul(banks[:, 1, 0:NI * E], ones[:], flat, start=True, stop=True).then_inc(rank_done, 1)
            for n in range(2 * NI):
                kk, i = n // NI, n % NI
                pe.wait_ge(hot_ready, n + 1)
                nc.tensor.matmul(banks[:, 2, kk * NT:(kk + 1) * NT], hot_row[:, n % NHOT, :], hot_col[:, n % NHOT, :],
                                 start=(i == 0), stop=(i == NI - 1)).then_inc(hot_used, 1)

            pe.wait_ge(lists_ready, 3)
            pe.wait_ge(late_lo, len(LATE))

            def gathered_T(j, half, par):
                pe.wait_ge(xg_full[par], 16 * (half + 1))
                wait(pe, xl_ready, j - 1)
                for m in range(M):
                    ins = nc.tensor.transpose(banks[:, par, m * P:(m + 1) * P], xg[par][:, m * P:(m + 1) * P], ident[:])
                ins.then_inc(gT_done, 1)

            def first(j, par):
                e = pe.value_load(tile_expert[0:1, ds(j, 1)], min_val=0, max_val=E - 1)
                pe.wait_ge(xl_ready, j + 1)
                wait(pe, hid_ready, 2 * (j - 1))
                for c in range(HC):
                    half, i = c // (HC // 2), c % (HC // 2)
                    dst = banks[:, 2 + 2 * par + half, i * P:(i + 1) * P]
                    for m in range(M):
                        a = m * H + c * P
                        hi, lo = weight_at(e, 0, 0, a, a + P), weight_at(e, 0, 1, a, a + P)
                        nc.tensor.matmul(dst, hi, xh[par][:, m, :], start=(m == 0), stop=False)
                        nc.tensor.matmul(dst, hi, xl[par][:, m, :], start=False, stop=False)
                        ins = nc.tensor.matmul(dst, lo, xh[par][:, m, :], start=False, stop=(m == M - 1))
                    if i == HC // 2 - 1:
                        ins.then_inc(h_done, 1)

            def second(j, par):
                e = pe.value_load(tile_expert[0:1, ds(j, 1)], min_val=0, max_val=E - 1)
                pe.wait_ge(hl_ready, j + 1)
                wait(pe, y_ready, j - 1)
                dst = banks[:, 6 + par, 0:D]
                for c in range(HC):
                    hi, lo = weight_at(e, 1, 0, c * D, (c + 1) * D), weight_at(e, 1, 1, c * D, (c + 1) * D)
                    nc.tensor.matmul(dst, hh[par][:, c * P:(c + 1) * P], hi, start=(c == 0), stop=False)
                    nc.tensor.matmul(dst, hh[par][:, c * P:(c + 1) * P], lo, start=False, stop=False)
                    ins = nc.tensor.matmul(dst, hl[par][:, c * P:(c + 1) * P], hi, start=False, stop=(c == HC - 1))
                ins.then_inc(y_done, 1)

            gathered_T(0, 0, 0)
            gathered_T(1, 0, 1)
            first(0, 0)
            for j in range(2):
                gathered_T(j + 2, 1, j)
                first(j + 1, 1 - j)
                second(j, j)
            with pe.Fori(1, (NT - 3) // 2) as t:
                for par in range(2):
                    gathered_T(2 * t + par + 2, t + 1, par)
                    first(2 * t + par + 1, 1 - par)
                    second(2 * t + par, par)
            for j in range(NT - 3, NT):
                if j + 2 < NT:
                    gathered_T(j + 2, (j + 2) // 2, j % 2)
                if j + 1 < NT:
                    first(j + 1, (j + 1) % 2)
                second(j, j % 2)


_INS = ['x', 'ctx_1024', 'g_xattn', 'g_ffn', 'L0_xattn_Wq', 'L0_xattn_bq', 'L0_xattn_Wk', 'L0_xattn_bk', 'L0_xattn_Wv',
        'L0_xattn_bv', 'L0_xattn_Wo', 'L0_xattn_bo', 'L0_ffn_Wr', 'L0_ffn_br', 'L0_ffn_W1', 'L0_ffn_b1', 'L0_ffn_W2', 'L0_ffn_b2']


def kernel(**inputs):
    import numpy as np
    import concourse.bacc as bacc
    from concourse.bass_utils import run_bass_kernel_spmd

    nc = bacc.Bacc("TRN2", target_bir_lowering=False, num_devices=1)
    arrays, args = {}, []
    for name in _INS:
        a = np.ascontiguousarray(inputs[name])
        arrays[f"in_{name}"] = a
        args.append(nc.dram_tensor(f"in_{name}", a.shape, mybir.dt.from_np(a.dtype), kind="ExternalInput").ap())
    out = nc.dram_tensor("out_dram", inputs["x"].shape, F32, kind="ExternalOutput").ap()
    flamingo(nc, *args, out)
    r = run_bass_kernel_spmd(nc, [arrays], core_ids=[0])
    return r.results[0]["out_dram"]
```

```python
from contextlib import ExitStack

import concourse.bass as bass
from concourse import mybir

ALU = mybir.AluOpType
ACT = mybir.ActivationFunctionType
AX = mybir.AxisListType
F32 = mybir.dt.float32
F16 = mybir.dt.float16
BF16 = mybir.dt.bfloat16
I32 = mybir.dt.int32
ds = bass.ds

P = 128
EPS = 1e-5
WSCALE = 256.0
HSCALE = 16.0
Q_TERM = [0, 0, 1, 1, 0, 2]
K_TERM = [0, 1, 0, 1, 2, 0]
NTERM = len(Q_TERM)


def flamingo(nc, x, ctx_in, g_xattn, g_ffn, Wq, bq, Wk, bk, Wv, bv, Wo, bo, Wr, br, W1, b1, W2, b2, out):
    NB, L, D = x.shape
    E, _, H = W1.shape
    NH, DH = 16, D // 16
    C = L // P
    M = D // P
    HC = H // P
    T = NB * L
    NI = T // P
    NT = (2 * T + E * (P - 1)) // P
    KR = NTERM * DH
    BIG = 3.0e38

    x_rows = x.rearrange("b (c p) d -> b p c d", p=P)
    ctx_rows = ctx_in.rearrange("b (c p) d -> b p c d", p=P)

    ctx = ExitStack()
    with ctx:
        def sem(name):
            return ctx.enter_context(nc.semaphore(name))

        def dram(name, shape, dt):
            return nc.dram_tensor(name, shape, dt, kind="Internal").ap()

        cursor = [-(-nc.sbuf_base // 64) * 64]

        def sb(name, shape, dt, at=None):
            size = 1
            for s in shape[1:]:
                size *= s
            size *= 2 if dt in (F16, BF16) else 4
            size = -(-size // 32) * 32
            where = cursor if at is None else at
            t = nc.alloc_sbuf_tensor_at(name, shape, dt, offset=where[0])
            where[0] += size
            return t

        part_d = {s: [dram(f"{s}_parts{i}", (3, D, L), BF16) for i in range(2)] for s in "qk"}
        x1_d = dram("x1_rows", (T, D), F32)
        xn2_d = dram("xn2_rows", (T, D), F32)
        y_d = dram("y_rows", (2 * T + NT * P, D), F32)

        ident = sb("ident", [P, P], F32)
        tri = sb("tri", [P, P], BF16)
        ones = sb("ones", [P, P], BF16)
        logits = sb("logits", [P, NI, E], F32)
        b1_col = sb("b1_col", [P, E * HC], F32)
        gate1 = sb("gate1", [P, NI], F32)
        gate2 = sb("gate2", [P, NI], F32)
        tanh_x = sb("tanh_x", [P, 1], F32)
        tanh_f = sb("tanh_f", [P, 1], F32)
        slot_token = sb("slot_token", [P, NT], I32)
        slot_dest = sb("slot_dest", [P, NT], I32)
        tile_expert = sb("tile_expert", [1, NT], I32)
        W_KEPT = 6
        wall = sb("wall", [P, E, 2, 2, M * H], F16)
        over = [cursor[0] - (E - W_KEPT) * 2 * 2 * M * H * 2]
        late = [cursor[0]]

        A = over
        free_late = A[0]
        xin = [sb(f"xin{i}", [P, C, D], F32, A) for i in range(2)]
        cin = [sb(f"cin{i}", [P, C, D], F32, A) for i in range(2)]
        xn = sb("xn", [P, C, D], F32, A)
        xnT = sb("xnT", [P, M, L], F32, A)
        ctxT = sb("ctxT", [P, M, L], F32, A)
        yq = sb("yq", [P, M, L], F32, A)
        yk = sb("yk", [P, M, L], F32, A)
        rest = sb("rest", [P, M, L], F32, A)
        qparts = sb("qparts", [P, 3, M, L], BF16, A)
        kparts = sb("kparts", [P, 3, M, L], BF16, A)
        wq = sb("wq", [P, M, D], F32, A)
        wk = sb("wk", [P, M, D], F32, A)
        wv = sb("wv", [P, M, D], F32, A)
        assert A[0] >= late[0]
        wo = sb("wo", [P, M, D], F32, A)
        wr = sb("wr", [P, M, E], F32, A)
        out_bias = sb("out_bias", [P, D], F32, A)
        bo_b = sb("bo_b", [P, D], F32, A)
        br_b = sb("br_b", [P, E], F32, A)
        bias_col = sb("bias_col", [P, 3, M], F32, A)
        stats = sb("stats", [P, C, 6], F32, A)
        mean_var = [sb(f"mean_var{i}", [P, C, 2], F32, A) for i in range(2)]
        var_eps = [sb(f"var_eps{i}", [P, C], F32, A) for i in range(2)]
        rstd = [sb(f"rstd{i}", [P, C], F32, A) for i in range(2)]
        minus_half = sb("minus_half", [P, C], F32, A)
        qs = [sb(f"qs{i}", [P, NH, L], BF16, A) for i in range(2)]
        ks = [sb(f"ks{i}", [P, NH, L], BF16, A) for i in range(2)]
        vaug = [sb(f"vaug{i}", [P, C, NH, 32], F32, A) for i in range(2)]
        probs = [sb(f"probs{i}", [P, 4, L], F32, A) for i in range(2)]
        negmax = sb("negmax", [P, C, NH], F32, A)
        negmax_row = [sb(f"negmax_row{i}", [8, L], BF16, A) for i in range(2)]
        oT = sb("oT", [P, 4, L], F32, A)
        recip = [sb(f"recip{i}", [P, NH], F32, A) for i in range(2)]
        cn = sb("cn", [P, C, D], F32, A)
        cT = sb("cT", [P, M, L], F32, A)
        xres = sb("xres", [P, C, D], F32, A)
        x1b = sb("x1b", [P, C, D], F32, A)
        xn2b = sb("xn2b", [P, C, D], F32, A)
        wst_at = A[0]
        wst = [sb(f"wst{i}", [P, M * H // 2], F32, A) for i in range(2)]
        assert A[0] <= nc.sbuf_usable_end, (A[0], nc.sbuf_usable_end)

        R = late
        b2_b = sb("b2_b", [P, E, D], F32, R)
        x1_all = sb("x1_all", [P, NI, D], F32, R)
        B0 = [R[0]]
        iota_e = sb("iota_e", [P, E], F32, B0)
        iota_b = sb("iota_b", [P, P], F32, B0)
        unused_row = sb("unused_row", [P, NT], F32, B0)
        tok_val = sb("tok_val", [P, NI], F32, B0)
        tok_neg = sb("tok_neg", [P, NI], F32, B0)
        t3 = sb("t3", [P, NI, E], F32, B0)
        oh1 = sb("oh1", [P, NI, E], F32, B0)
        oh2 = sb("oh2", [P, NI, E], F32, B0)
        picked = sb("picked", [P, NI, E], BF16, B0)
        masked = sb("masked", [P, NI, E], F32, B0)
        totals = sb("totals", [P, E, NI], F32, B0)
        before = sb("before", [P, E, NI], F32, B0)
        onesf = sb("onesf", [P, E * NI], F32, B0)
        best1 = sb("best1", [P, NI], F32, B0)
        best2 = sb("best2", [P, NI], F32, B0)
        index = sb("index", [P, NI], F32, B0)
        gexp = sb("gexp", [P, NI], F32, B0)
        e_end = sb("e_end", [P, E + 1], F32, B0)
        e_cnt = sb("e_cnt", [P, E], F32, B0)
        e_int = sb("e_int", [P, E], I32, B0)
        e_tiles = sb("e_tiles", [P, E], F32, B0)
        t_end = sb("t_end", [P, E + 1], F32, B0)
        e_off = sb("e_off", [P, E], F32, B0)
        slot = sb("slot", [P, 2, NI], F32, B0)
        slot_i = sb("slot_i", [P, 2, NI], I32, B0)
        slot_t = sb("slot_t", [P, 2, NI], I32, B0)
        slot_col = sb("slot_col", [P, 2, NI], F32, B0)
        slot_row = sb("slot_row", [P, 2, NI], F32, B0)
        NHOT = 16
        hot_row = sb("hot_row", [P, NHOT, P], F16, B0)
        hot_col = sb("hot_col", [P, NHOT, NT], F16, B0)
        tval = sb("tval", [P, 2, NT], F32, B0)
        tsum = sb("tsum", [P, NT], F32, B0)
        tflag = sb("tflag", [P, NT], F32, B0)
        tfull = sb("tfull", [P, NT], F32, B0)
        te3 = sb("te3", [1, NT, E], F32, B0)
        assert B0[0] <= wst_at, (B0[0], wst_at)
        RING = 4
        C0 = [R[0]]
        gather_idx = [sb(f"gather_idx{i}", [P, 1], I32, C0) for i in range(RING)]
        dest_idx = [sb(f"dest_idx{i}", [P, 1], I32, C0) for i in range(2)]
        xg = [sb(f"xg{i}", [P, D], F32, C0) for i in range(RING)]
        xh = [sb(f"xh{i}", [P, M, P], F16, C0) for i in range(2)]
        xl = [sb(f"xl{i}", [P, M, P], F16, C0) for i in range(2)]
        hid = [sb(f"hid{i}", [P, H], F32, C0) for i in range(2)]
        hh = [sb(f"hh{i}", [P, H], F16, C0) for i in range(2)]
        hl = [sb(f"hl{i}", [P, H], F16, C0) for i in range(2)]
        yb = [sb(f"yb{i}", [P, D], F32, C0) for i in range(2)]
        assert C0[0] <= nc.sbuf_usable_end, C0[0]
        D0 = [R[0]]
        DT = 4
        y1b = [sb(f"y1b{i}", [P, DT, D], F32, D0) for i in range(2)]
        y2b = [sb(f"y2b{i}", [P, DT, D], F32, D0) for i in range(2)]
        assert D0[0] <= nc.sbuf_usable_end, D0[0]

        banks = ctx.enter_context(nc.psum_tensor("banks", [P, 8, 512], F32))

        def bank(i):
            return banks[:, i, :]

        passed = sem("passed")
        consts = sem("consts")
        pool_const = sem("pool_const")
        pool_ready = sem("pool_ready")
        tanh_ready = sem("tanh_ready")
        bvcol_ready = sem("bvcol_ready")
        bvwo_done = sem("bvwo_done")
        obias_ready = sem("obias_ready")
        b1t_done = sem("b1t_done")
        biases_ready = sem("biases_ready")
        xin_full = [sem(f"xin_full{i}") for i in range(2)]
        cin_full = [sem(f"cin_full{i}") for i in range(2)]
        xres_full = sem("xres_full")
        xn_ready = sem("xn_ready")
        var_ready = [sem(f"var_ready{i}") for i in range(2)]
        rstd_ready = [sem(f"rstd_ready{i}") for i in range(2)]
        xT_done, xT_evac = sem("xT_done"), sem("xT_evac")
        ctxT_done, ctxT_evac = sem("ctxT_done"), sem("ctxT_evac")
        q_done, q_evac = sem("q_done"), sem("q_evac")
        k_done, k_evac = sem("k_done"), sem("k_evac")
        v_done, v_evac = sem("v_done"), sem("v_evac")
        q_split, k_split = sem("q_split"), sem("k_split")
        q_stored, k_stored = sem("q_stored"), sem("k_stored")
        qs_full, ks_full = sem("qs_full"), sem("ks_full")
        mx_done, mx_red = sem("mx_done"), sem("mx_red")
        nm_done, nm_evac = sem("nm_done"), sem("nm_evac")
        row_full = [sem(f"row_full{i}") for i in range(2)]
        st_done, exp_done = sem("st_done"), sem("exp_done")
        av_mm, av_evac = sem("av_mm"), sem("av_evac")
        tok_done, cn_ready = sem("tok_done"), sem("cn_ready")
        cT_done, cT_evac, o_done = sem("cT_done"), sem("cT_evac"), sem("o_done")
        xb_ready, x1_ready, xn2_ready = sem("xb_ready"), sem("x1_ready"), sem("xn2_ready")
        x1_stored, xn2_stored = sem("x1_stored"), sem("xn2_stored")
        x2T_done, x2T_evac = sem("x2T_done"), sem("x2T_evac")
        lg_done, lg_evac = sem("lg_done"), sem("lg_evac")
        w_full = [sem(f"w_full{i}") for i in range(2)]
        w_hi = sem("w_hi")
        w_lo = [sem(f"w_lo{i}") for i in range(2)]
        dve_chain = sem("dve_chain")
        pool_chain = sem("pool_chain")
        late_full = [sem(f"late_full{i}") for i in range(2)]
        late_hi, late_lo = sem("late_hi"), sem("late_lo")
        b2_full, x1_full = sem("b2_full"), sem("x1_full")
        iota_ready = sem("iota_ready")
        diff_ready, gexp_ready = sem("diff_ready"), sem("gexp_ready")
        picked_ready, rank_done = sem("picked_ready"), sem("rank_done")
        hot_ready, hot_used, lists_ready = sem("hot_ready"), sem("hot_used"), sem("lists_ready")
        idx_ready, dest_ready = sem("idx_ready"), sem("dest_ready")
        xg_full = [sem(f"xg_full{i}") for i in range(RING)]
        gT_done, xh_ready, xl_ready = sem("gT_done"), sem("xh_ready"), sem("xl_ready")
        h_done, hid_ready, hh_ready, hl_ready = sem("h_done"), sem("hid_ready"), sem("hh_ready"), sem("hl_ready")
        y_done, y_ready = sem("y_done"), sem("y_ready")
        y_sent = [sem(f"y_sent{i}") for i in range(2)]
        y_back = [sem(f"y_back{i}") for i in range(2)]
        out_ready = sem("out_ready")
        out_sent = [sem(f"out_sent{i}") for i in range(2)]

        N_CONST = 11
        HOLDS = (nc.sync.engine, nc.gpsimd.engine)

        def hold(eng, s, v):
            eng.wait_ge(s, v)
            if not isinstance(v, int):
                eng.sem_inc(passed, 1)

        def wait(eng, s, v):
            if isinstance(v, int) and v <= 0:
                return
            hold(eng, s, v) if eng.engine in HOLDS else eng.wait_ge(s, v)

        def bodies(eng, body):
            body(0, 0, False, 2)
            body(0, 1, False, 2)
            with eng.Fori(1, NB // 2 - 1) as t:
                body(t, 0, True, 2)
                body(t, 1, True, 2)
            body(NB // 2 - 1, 0, False, 1)
            body(NB // 2 - 1, 1, False, 0)

        assert NB // 2 - 2 == W_KEPT

        def tiles(eng, step, chain=None):
            for j in range(RING):
                step(j, 0, j, False)
            laps = NT // RING - 1
            with eng.Fori(1, laps) as t:
                if chain:
                    chain[1] = (t - 1) * RING
                for i in range(RING):
                    step(RING * t + i, t, i, False)
            if chain:
                chain[0], chain[1] = chain[0] + (laps - 2) * RING, 0
            for j in range(RING * laps, NT):
                step(j, j // RING, j % RING, j + RING >= NT)

        def weight_at(e, w, part, a, b):
            return wall[:, ds(e, 1), w, part, a:b].rearrange("p e n -> p (e n)")

        LATE = [(e, w, half) for e in range(W_KEPT, E) for w in range(2) for half in range(2)]
        HALF = M * H // 2

        def weight_rows(e, w, half):
            if w == 0:
                return W1[e, half * P:(half + 1) * P, :]
            return W2[e, half * H // 2:(half + 1) * H // 2, :].rearrange("(c p) n -> p c n", p=P)

        def stage_view(buf, w):
            return buf[:, :] if w == 0 else buf[:, :].rearrange("p (c n) -> p c n", n=D)

        block = ctx.enter_context(nc.Block())

        @block.sync
        def _(sp):
            def load_x(n, t, par):
                wait(sp, xn_ready, 2 * (n - 1))
                sp.dma_start(xin[par][:], x_rows[n]).then_inc(xin_full[par], 16)
                wait(sp, ctxT_done, n - 1)
                sp.dma_start(cin[par][:], ctx_rows[n]).then_inc(cin_full[par], 16)

            def store_part(n, par, name):
                src, cut_, stored, full = (kparts, k_split, k_stored, ks_full) if name == "k" else (qparts, q_split, q_stored, qs_full)
                wait(sp, full, 16 * NTERM * (n - 1))
                hold(sp, cut_, n + 1)
                sp.dma_start(part_d[name][par].rearrange("s (m p) t -> p s m t", p=P), src[:]).then_inc(stored, 16)

            def load_part(n, par, name):
                terms, stored, dst, full = (K_TERM, k_stored, ks, ks_full) if name == "k" else (Q_TERM, q_stored, qs, qs_full)
                wait(sp, st_done, 8 * (n - 1))
                hold(sp, stored, 16 * (n + 1))
                for i, s in enumerate(terms):
                    sp.dma_start(dst[par][DH * i:DH * (i + 1), :, :],
                                 part_d[name][par][s].rearrange("(h d) t -> d h t", d=DH)).then_inc(full, 16)

            def max_row(n, par, s):
                hold(sp, nm_evac, 2 * n + s + 1)
                sp.dma_start(qs[par][KR:KR + 1, 8 * s:8 * s + 8, :], negmax_row[s][:]).then_inc(row_full[s], 16)

            def results(n):
                hold(sp, x1_ready, 2 * (n + 1))
                sp.dma_start(x1_d[ds(n * L, L), :].rearrange("(c p) d -> p c d", p=P), x1b[:]).then_inc(x1_stored, 16)
                hold(sp, xn2_ready, 2 * (n + 1))
                sp.dma_start(xn2_d[ds(n * L, L), :].rearrange("(c p) d -> p c d", p=P), xn2b[:]).then_inc(xn2_stored, 16)

            def residual(n):
                wait(sp, x1_ready, 2 * n)
                sp.dma_start(xres[:], x_rows[n]).then_inc(xres_full, 16)

            sp.dma_start(xin[0][:], x_rows[0]).then_inc(xin_full[0], 16)
            sp.dma_start(cin[0][:], ctx_rows[0]).then_inc(cin_full[0], 16)
            for dst, w in ((wq, Wq), (wk, Wk), (wv, Wv), (wo, Wo), (wr, Wr)):
                sp.dma_start(dst[:], w.rearrange("(m p) n -> p m n", p=P)).then_inc(consts, 16)
            for i, b in enumerate((bq, bk, bv)):
                sp.dma_start(oT[E * HC + i * M:E * HC + (i + 1) * M, 0, 0:P], b.rearrange("(m p) -> m p", p=P)).then_inc(consts, 16)
            sp.dma_start(bo_b[:], bo.partition_broadcast(P)).then_inc(consts, 16)
            sp.dma_start(br_b[:], br.partition_broadcast(P)).then_inc(consts, 16)
            sp.dma_start(oT[0:E * HC, 0, 0:P], b1.rearrange("e (c p) -> (e c) p", p=P)).then_inc(consts, 16)
            load_x(1, 0, 1)
            for name in "kq":
                store_part(0, 0, name)
                load_part(0, 0, name)

            def body(t, par, weights, ahead):
                n = 2 * t + par
                static = isinstance(n, int)
                post = not static or n > 0
                if post:
                    residual(n - 1)
                if ahead == 2:
                    load_x(n + 2, t + 1, par)

                if weights:
                    for w in range(2):
                        e = t - 1
                        wait(sp, w_lo[w], 2 * (t - 1) + par)
                        if w == 0:
                            src = W1[ds(e, 1), par * P:(par + 1) * P, :].rearrange("e p n -> p (e n)")
                        else:
                            src = W2[ds(e, 1), par * H // 2:(par + 1) * H // 2, :].rearrange("e (c p) n -> p (e c) n", p=P)
                        sp.dma_start(stage_view(wst[w], w), src).then_inc(w_full[w], 16)
                if ahead:
                    store_part(n + 1, 1 - par, "k")
                max_row(n, par, 0)
                if ahead:
                    load_part(n + 1, 1 - par, "k")
                max_row(n, par, 1)
                if ahead:
                    store_part(n + 1, 1 - par, "q")
                if ahead:
                    load_part(n + 1, 1 - par, "q")
                if post:
                    results(n - 1)

            bodies(sp, body)
            hold(sp, k_stored, 16 * NB)
            hold(sp, q_stored, 16 * NB)
            hold(sp, v_done, NB)
            residual(NB - 1)
            for i, (e, w, half) in enumerate(LATE):
                if i == 0:
                    for w_ in range(2):
                        hold(sp, w_lo[w_], 2 * W_KEPT)
                if i == 1:
                    results(NB - 1)
                    hold(sp, lg_evac, NB)
                    hold(sp, x1_stored, 16 * NB)
                    hold(sp, xn2_stored, 16 * NB)
                    sp.dma_start(b2_b[:].rearrange("p e d -> p (e d)"), b2.rearrange("e d -> (e d)").partition_broadcast(P)).then_inc(b2_full, 16)
                if i >= 2:
                    hold(sp, late_lo, i - 1)
                sp.dma_start(stage_view(wst[i % 2], w), weight_rows(e, w, half)).then_inc(late_full[i % 2], 16)
            sp.dma_start(x1_all[:], x1_d.rearrange("(i p) d -> p i d", p=P)).then_inc(x1_full, 16)
            hold(sp, y_sent[0], 16 * ((NT + 1) // 2))
            hold(sp, y_sent[1], 16 * (NT // 2))
            for i in range(NI // DT):
                if i >= 2:
                    hold(sp, out_sent[i % 2], 16 * (i // 2))
                sp.dma_start(y1b[i % 2][:], y_d[i * DT * P:(i + 1) * DT * P, :].rearrange("(i p) d -> p i d", p=P)).then_inc(y_back[i % 2], 16)
                sp.dma_start(y2b[i % 2][:], y_d[T + i * DT * P:T + (i + 1) * DT * P, :].rearrange("(i p) d -> p i d", p=P)).then_inc(y_back[i % 2], 16)
            for s in range(2):
                hold(sp, out_sent[s], 16 * (NI // DT // 2))

        @block.gpsimd
        def _(pool):
            chain = [0, 0]

            def link(ins):
                chain[0] += 1
                ins.then_inc(pool_chain, 1)
                hold(pool, pool_chain, chain[0] + chain[1])

            for i in range(2):
                nc.gpsimd.memset(vaug[i][:], 0.0)
                nc.gpsimd.memset(ks[i][:], 1.0)
            nc.gpsimd.memset(ident[:], 0.0)
            nc.gpsimd.memset(minus_half[:], -0.5)
            nc.gpsimd.memset(ones[:], 1.0)
            nc.gpsimd.memset(tri[:], 1.0).then_inc(pool_const, 1)
            hold(pool, pool_const, 1)
            for i in range(2):
                nc.gpsimd.memset(vaug[i][:, :, :, DH:DH + 1], 1.0)
            nc.gpsimd.affine_select(out=ident[:], in_=ident[:], compare_op=ALU.not_equal, fill=1.0, base=0,
                                    pattern=[[-1, P]], channel_multiplier=1)
            nc.gpsimd.affine_select(out=tri[:], in_=tri[:], compare_op=ALU.is_gt, fill=0.0, base=0,
                                    pattern=[[1, P]], channel_multiplier=-1).then_inc(pool_ready, 1)

            def cut(src, dst):
                link(nc.gpsimd.tensor_tensor(rest[:], src[:], dst[:, 0], ALU.subtract))
                link(nc.gpsimd.tensor_copy(dst[:, 1], rest[:]))
                return nc.gpsimd.tensor_tensor(dst[:, 2], rest[:], dst[:, 1], ALU.subtract)

            def inverse_root(n, which):
                hold(pool, var_ready[which], n + 1)
                nc.gpsimd.tensor_tensor(rstd[which][:], var_eps[which][:], minus_half[:], ALU.pow).then_inc(rstd_ready[which], 1)

            def cut_k(n):
                hold(pool, k_evac, n + 1)
                wait(pool, q_split, n)
                cut(yk, kparts).then_inc(k_split, 1)

            def cut_q(n):
                hold(pool, q_evac, n + 1)
                hold(pool, k_split, n + 1)
                cut(yq, qparts).then_inc(q_split, 1)

            def residual(n):
                hold(pool, xres_full, 16 * (n + 1))
                if isinstance(n, int) and n == 0:
                    hold(pool, obias_ready, 1)
                nc.gpsimd.tensor_tensor(xres[:], xres[:], out_bias[:].unsqueeze(1).broadcast_to([P, C, D]),
                                        ALU.add).then_inc(xb_ready, 1)

            hold(pool, pool_ready, 1)
            inverse_root(0, 0)
            inverse_root(1, 0)
            cut_k(0)
            cut_q(0)

            def body(t, par, weights, ahead):
                n = 2 * t + par
                post = not isinstance(n, int) or n > 0
                if ahead:
                    cut_k(n + 1)
                if post:
                    residual(n - 1)
                if ahead:
                    cut_q(n + 1)
                if ahead == 2:
                    inverse_root(n + 2, 0)
                if post:
                    inverse_root(n - 1, 1)

            PER_BODY = 4
            body(0, 0, False, 2)
            body(0, 1, False, 2)
            with pool.Fori(1, NB // 2 - 1) as t:
                chain[1] = (t - 1) * (2 * PER_BODY)
                was = chain[0]
                body(t, 0, True, 2)
                body(t, 1, True, 2)
                assert chain[0] == was + 2 * PER_BODY
            chain[0], chain[1] = was + (NB // 2 - 2) * 2 * PER_BODY, 0
            body(NB // 2 - 1, 0, False, 1)
            body(NB // 2 - 1, 1, False, 0)

            residual(NB - 1)
            inverse_root(NB - 1, 1)
            hold(pool, lg_evac, NB)
            hold(pool, x1_stored, 16 * NB)
            hold(pool, xn2_stored, 16 * NB)
            nc.gpsimd.iota(iota_e[:], [[1, E]], base=-E, channel_multiplier=0, allow_small_or_imprecise_dtypes=True)
            nc.gpsimd.iota(iota_b[:], [[1, P]], base=0, channel_multiplier=0, allow_small_or_imprecise_dtypes=True)
            nc.gpsimd.iota(unused_row[:], [[P, NT]], base=2 * T - T // 2, channel_multiplier=1, allow_small_or_imprecise_dtypes=True)
            nc.gpsimd.memset(onesf[:], 1.0)
            nc.gpsimd.iota(tok_val[:], [[P, NI]], base=-T // 2, channel_multiplier=1,
                           allow_small_or_imprecise_dtypes=True).then_inc(iota_ready, 1)
            hold(pool, lists_ready, 3)

            def gather(j, lap, slot_):
                wait(pool, xg_full[slot_], 16 * lap)
                nc.gpsimd.tensor_copy(gather_idx[slot_][:], slot_token[:, ds(j, 1)]).then_inc(idx_ready, 1)
                hold(pool, idx_ready, j + 1)
                if not isinstance(lap, int) or lap > 0:
                    hold(pool, gT_done, j - RING + 1)
                nc.gpsimd.indirect_dma_start(xg[slot_][:], None, xn2_d,
                                             bass.IndirectOffsetOnAxis(gather_idx[slot_][:, 0:1], 0)).then_inc(xg_full[slot_], 16)

            def scatter(j, half, par):
                wait(pool, y_sent[par], 16 * half)
                nc.gpsimd.tensor_copy(dest_idx[par][:], slot_dest[:, ds(j, 1)]).then_inc(dest_ready, 1)
                hold(pool, dest_ready, j + 1)
                hold(pool, y_ready, j + 1)
                nc.gpsimd.indirect_dma_start(y_d, bass.IndirectOffsetOnAxis(dest_idx[par][:, 0:1], 0),
                                             yb[par][:], None).then_inc(y_sent[par], 16)

            for j in range(RING):
                gather(j, 0, j)

            def step(j, t, i, last):
                if not last:
                    gather(j + RING, t + 1, i)
                if not isinstance(j, int) or j > 0:
                    scatter(j - 1, 2 * t + (i - 1) // 2, 1 - i % 2)

            tiles(pool, step)
            step(NT, NT // RING, NT % RING, True)

        @block.scalar
        def _(act):
            act.dma_start(tanh_x[:], g_xattn.partition_broadcast(P)).then_inc(tanh_ready, 16)
            act.dma_start(tanh_f[:], g_ffn.partition_broadcast(P)).then_inc(tanh_ready, 16)
            act.wait_ge(tanh_ready, 32)
            nc.scalar.activation(tanh_x[:], tanh_x[:], ACT.Tanh).then_inc(tanh_ready, 1)
            nc.scalar.activation(tanh_f[:], tanh_f[:], ACT.Tanh).then_inc(tanh_ready, 1)
            act.wait_ge(b1t_done, 1)
            nc.scalar.activation(bias_col[:].rearrange("p i m -> p (i m)"), banks[:, 7, E * HC:E * HC + 3 * M], ACT.Copy).then_inc(biases_ready, 1)
            nc.scalar.activation(b1_col[:], banks[:, 7, 0:E * HC], ACT.Copy, scale=HSCALE).then_inc(biases_ready, 1)
            act.wait_ge(biases_ready, 1)
            act.wait_ge(pool_ready, 1)
            for m in range(M):
                ins = nc.scalar.activation(probs[0][:, m, 0:P], ident[:], ACT.Identity, bias=bias_col[:, 2, m:m + 1], scale=0.0)
            ins.then_inc(bvcol_ready, 1)

            def norm_T(n):
                act.wait_ge(xT_done, n + 1)
                wait(act, q_done, n)
                nc.scalar.activation(xnT[:].rearrange("p m t -> p (m t)"), bank(1), ACT.Copy).then_inc(xT_evac, 1)

            def context_T(n):
                act.wait_ge(ctxT_done, n + 1)
                wait(act, v_done, n)
                nc.scalar.activation(ctxT[:].rearrange("p m t -> p (m t)"), bank(0), ACT.Copy).then_inc(ctxT_evac, 1)

            def biased(n, which, src, done, split, stored, dst, parts_, evac):
                act.wait_ge(done, n + 1)
                wait(act, split, n)
                wait(act, stored, 16 * n)
                for m in range(M):
                    nc.scalar.activation(dst[:, m, :], banks[:, src, m * L:(m + 1) * L], ACT.Identity,
                                         bias=bias_col[:, which, m:m + 1])
                for m in range(M):
                    ins = nc.scalar.activation(parts_[:, 0, m, :], banks[:, src, m * L:(m + 1) * L], ACT.Identity,
                                               bias=bias_col[:, which, m:m + 1])
                ins.then_inc(evac, 1)

            def values(n, par):
                act.wait_ge(v_done, n + 1)
                wait(act, av_mm, 8 * (n - 1))
                for c in range(C):
                    ins = nc.scalar.activation(vaug[par][:, c, :, 0:DH], banks[:, 2, c * D:(c + 1) * D].rearrange("p (h d) -> p h d", d=DH), ACT.Copy)
                ins.then_inc(v_evac, 1)

            def prep(n, par):
                biased(n, 1, 7, k_done, k_split, k_stored, yk, kparts, k_evac)
                biased(n, 0, 6, q_done, q_split, q_stored, yq, qparts, q_evac)
                values(n, par)

            def attended_T(n):
                act.wait_ge(cT_done, n + 1)
                wait(act, lg_done, n)
                nc.scalar.activation(cT[:].rearrange("p m t -> p (m t)"), bank(3), ACT.Copy).then_inc(cT_evac, 1)

            def norm2_T(n):
                act.wait_ge(x2T_done, n + 1)
                act.wait_ge(o_done, n + 1)
                nc.scalar.activation(cT[:].rearrange("p m t -> p (m t)"), bank(0), ACT.Copy).then_inc(x2T_evac, 1)

            context_T(0)
            norm_T(0)
            prep(0, 0)
            context_T(1)
            norm_T(1)

            def body(t, par, weights, ahead):
                n = 2 * t + par
                post = not isinstance(n, int) or n > 0

                def high(w):
                    act.wait_ge(w_full[w], 16 * (2 * (t - 1) + par + 1))
                    nc.scalar.activation(weight_at(t - 1, w, 0, par * HALF, (par + 1) * HALF), wst[w][:], ACT.Copy,
                                         scale=WSCALE).then_inc(w_hi, 1)

                if ahead:
                    prep(n + 1, 1 - par)
                if post:
                    attended_T(n - 1)
                if weights:
                    high(0)
                for v in range(8):
                    act.wait_ge(st_done, 8 * n + v + 1)
                    wait(act, av_mm, 8 * n + v - 1)
                    nc.scalar.activation(probs[v % 2][:].rearrange("p h t -> p (h t)"),
                                         banks[:, 2 + 2 * (v % 2):4 + 2 * (v % 2), :].rearrange("p b t -> p (b t)"),
                                         ACT.Exp, scale=float(DH) ** -0.5).then_inc(exp_done, 1)
                    if ahead == 2 and v == 1:
                        context_T(n + 2)
                    if ahead == 2 and v == 4:
                        norm_T(n + 2)
                    if post and v == 5:
                        norm2_T(n - 1)
                    if weights and v == 3:
                        high(1)

            bodies(act, body)

            def late_high(i):
                e, w, half = LATE[i]
                act.wait_ge(late_full[i % 2], 16 * (i // 2 + 1))
                nc.scalar.activation(wall[:, e, w, 0, half * HALF:(half + 1) * HALF], wst[i % 2][:], ACT.Copy,
                                     scale=WSCALE).then_inc(late_hi, 1)

            late_high(0)
            attended_T(NB - 1)
            norm2_T(NB - 1)
            for i in range(1, 2):
                late_high(i)
            act.wait_ge(diff_ready, 1)
            nc.scalar.activation(gexp[:], gexp[:], ACT.Exp).then_inc(gexp_ready, 1)
            for i in range(2, len(LATE)):
                late_high(i)

            act.wait_ge(lists_ready, 3)

            def high_x(j, par):
                act.wait_ge(gT_done, j + 1)
                wait(act, h_done, 2 * (j - 1))
                nc.scalar.activation(xh[par][:].rearrange("p m t -> p (m t)"), banks[:, par, 0:M * P], ACT.Copy,
                                     scale=WSCALE).then_inc(xh_ready, 1)

            def relu(j, par):
                e = act.value_load(tile_expert[0:1, ds(j, 1)], min_val=0, max_val=E - 1)
                wait(act, hl_ready, j - 1)
                for half in range(2):
                    act.wait_ge(h_done, 2 * j + half + 1)
                    for i in range(HC // 2):
                        c = half * (HC // 2) + i
                        ins = nc.scalar.activation(hid[par][:, c * P:(c + 1) * P], banks[:, 2 + 2 * par + half, i * P:(i + 1) * P],
                                                   ACT.Relu, bias=b1_col[:, ds(e * HC + c, 1)], scale=HSCALE / WSCALE / WSCALE)
                    ins.then_inc(hid_ready, 1)

            high_x(0, 0)
            high_x(1, 1)
            relu(0, 0)

            def step(j, t, i, last):
                if not isinstance(j, int) or j + 2 < NT:
                    high_x(j + 2, i % 2)
                if not isinstance(j, int) or j + 1 < NT:
                    relu(j + 1, 1 - i % 2)

            tiles(act, step)
            for i in range(NI // DT):
                act.wait_ge(out_ready, i + 1)
                act.dma_start(out.rearrange("b (c p) d -> p (b c) d", p=P)[:, i * DT:(i + 1) * DT, :], y1b[i % 2][:]).then_inc(out_sent[i % 2], 16)

        @block.vector
        def _(dve):
            chain = [0, 0]

            def link(ins):
                chain[0] += 1
                ins.then_inc(dve_chain, 1)
                dve.wait_ge(dve_chain, chain[0] + chain[1])

            dve.wait_ge(consts, 16 * N_CONST)
            dve.wait_ge(bvwo_done, 1)
            dve.wait_ge(tanh_ready, 34)
            link(nc.vector.tensor_tensor(out_bias[:], banks[:, 6, 0:D], bo_b[:], ALU.add))
            nc.vector.tensor_scalar(out_bias[:], out_bias[:], tanh_x[:], None, ALU.mult).then_inc(obias_ready, 1)

            def variance(src, which):
                for c in range(C):
                    ins = nc.vector.bn_stats(stats[:, c, :], src[:, c, :])
                chain[0] += 1
                ins.then_inc(dve_chain, 1)
                hold(dve, dve_chain, chain[0] + chain[1])
                for c in range(C):
                    ins = nc.vector.bn_aggr(mean_var[which][:, c, :], stats[:, c, :])
                link(ins)
                nc.vector.tensor_scalar(var_eps[which][:], mean_var[which][:, :, 1], EPS, None, ALU.add).then_inc(var_ready[which], 1)

            def normalize(n, src, dst, which, ready):
                dve.wait_ge(rstd_ready[which], n + 1)
                for c in range(C):
                    nc.vector.tensor_scalar(dst[:, c, :], src[:, c, :], mean_var[which][:, c, 0:1], rstd[which][:, c:c + 1],
                                            ALU.subtract, ALU.mult).then_inc(ready, 1)

            def norm1_stats(n, t, par):
                dve.wait_ge(xin_full[par], 16 * (t + 1))
                variance(xin[par], 0)

            def norm1(n, par):
                wait(dve, xT_done, n)
                normalize(n, xin[par], xn, 0, xn_ready)

            def attended(n, c):
                dve.wait_ge(tok_done, 2 * n + c + 1)
                rows = bank(4 + c).rearrange("p (h w) -> p h w", w=32)
                link(nc.vector.reciprocal(recip[c][:].unsqueeze(2), rows[:, :, DH:DH + 1]))
                if c == 0:
                    wait(dve, cT_done, n)
                nc.vector.tensor_tensor(cn[:, c, :].rearrange("p (h d) -> p h d", d=DH), rows[:, :, 0:DH],
                                        recip[c][:].unsqueeze(2).broadcast_to([P, NH, DH]), ALU.mult).then_inc(cn_ready, 1)

            def residual(n):
                dve.wait_ge(o_done, n + 1)
                dve.wait_ge(xb_ready, n + 1)
                wait(dve, x1_stored, 16 * n)
                for c in range(C):
                    nc.vector.scalar_tensor_tensor(out=x1b[:, c, :], in0=banks[:, 4, c * D:(c + 1) * D], scalar=tanh_x[:],
                                                   in1=xres[:, c, :], op0=ALU.mult, op1=ALU.add).then_inc(x1_ready, 1)

            def norm2_stats(n):
                dve.wait_ge(x1_ready, 2 * (n + 1))
                variance(x1b, 1)

            def norm2(n):
                wait(dve, xn2_stored, 16 * n)
                wait(dve, x2T_done, n)
                normalize(n, x1b, xn2b, 1, xn2_ready)

            def router(n):
                dve.wait_ge(lg_done, n + 1)
                nc.vector.tensor_tensor(logits[:, ds(n * C, C), :], banks[:, 1, 0:C * E].rearrange("p (c e) -> p c e", e=E),
                                        br_b[:].unsqueeze(1).broadcast_to([P, C, E]), ALU.add).then_inc(lg_evac, 1)

            def reduce(n, u):
                hp, c = u // 2, u % 2
                dve.wait_ge(mx_done, 16 * n + u + 1)
                if u % 8 == 0:
                    wait(dve, nm_done, 2 * n - 1 + u // 8)
                nc.vector.tensor_reduce(negmax[:, c, 2 * hp:2 * hp + 2], bank(u % 2).rearrange("p (h k) -> p h k", k=L),
                                        AX.X, ALU.max, negate=True).then_inc(mx_red, 1)

            def max_row(n, s):
                dve.wait_ge(nm_done, 2 * n + s + 1)
                wait(dve, row_full[s], 16 * n)
                nc.vector.tensor_copy(negmax_row[s][:], banks[0:8, 7, 0:L]).then_inc(nm_evac, 1)

            def low(dst, stage, hi):
                return nc.vector.scalar_tensor_tensor(out=dst, in0=stage[:], scalar=WSCALE, in1=hi, op0=ALU.mult, op1=ALU.subtract)

            for n in range(2):
                norm1_stats(n, 0, n)
                norm1(n, n)

            def body(t, par, weights, ahead):
                n = 2 * t + par
                post = not isinstance(n, int) or n > 0

                def weight_low(w):
                    dve.wait_ge(w_hi, 2 * (2 * (t - 1) + par) + w + 1)
                    low(weight_at(t - 1, w, 1, par * HALF, (par + 1) * HALF), wst[w],
                        weight_at(t - 1, w, 0, par * HALF, (par + 1) * HALF)).then_inc(w_lo[w], 1)

                for u in range(16):
                    reduce(n, u)
                    if post and u in (5, 6):
                        attended(n - 1, u - 5)
                    if u == 10:
                        max_row(n, 0)
                    if post and u == 13:
                        residual(n - 1)
                max_row(n, 1)
                if ahead == 2:
                    norm1_stats(n + 2, t + 1, par)
                if post:
                    norm2_stats(n - 1)
                for g in range(4):
                    dve.wait_ge(av_mm, 8 * n + 2 * g + 2)
                    if g == 0:
                        wait(dve, tok_done, 2 * n)
                    nc.vector.tensor_copy(oT[:, g, :], banks[:, 6 + g % 2, 0:L]).then_inc(av_evac, 1)
                    if ahead == 2 and g == 0:
                        norm1(n + 2, par)
                    if post and g == 0:
                        norm2(n - 1)
                    if weights and g in (1, 2):
                        weight_low(g - 1)
                    if post and g == 3:
                        router(n - 1)

            PER_BODY = 2 + 2 + 2
            body(0, 0, False, 2)
            body(0, 1, False, 2)
            with dve.Fori(1, NB // 2 - 1) as t:
                chain[1] = (t - 1) * (2 * PER_BODY)
                was = chain[0]
                body(t, 0, True, 2)
                body(t, 1, True, 2)
                assert chain[0] == was + 2 * PER_BODY, (chain, was)
            chain[0], chain[1] = was + (NB // 2 - 2) * 2 * PER_BODY, 0
            body(NB // 2 - 1, 0, False, 1)
            body(NB // 2 - 1, 1, False, 0)
            attended(NB - 1, 0)
            attended(NB - 1, 1)
            residual(NB - 1)
            norm2_stats(NB - 1)
            norm2(NB - 1)
            router(NB - 1)

            dve.wait_ge(iota_ready, 1)
            dve.wait_ge(lg_evac, NB)
            dve.wait_ge(xn2_stored, 16 * NB)
            dve.wait_ge(x1_stored, 16 * NB)

            def late_low(i):
                e, w, half = LATE[i]
                dve.wait_ge(late_hi, i + 1)
                low(wall[:, e, w, 1, half * HALF:(half + 1) * HALF], wst[i % 2],
                    wall[:, e, w, 0, half * HALF:(half + 1) * HALF]).then_inc(late_lo, 1)

            def over_e(a):
                return a.unsqueeze(2).broadcast_to([P, NI, E])

            iota_ie = iota_e[:].unsqueeze(1).broadcast_to([P, NI, E])

            def choose(values, best, onehot):
                link(nc.vector.tensor_reduce(best[:], values[:], AX.X, ALU.max))
                link(nc.vector.tensor_tensor(t3[:], values[:], over_e(best[:]), ALU.is_equal))
                link(nc.vector.tensor_tensor(t3[:], t3[:], iota_ie, ALU.mult))
                link(nc.vector.tensor_reduce(index[:], t3[:], AX.X, ALU.min))
                link(nc.vector.tensor_tensor(onehot[:], iota_ie, over_e(index[:]), ALU.is_equal))

            choose(logits, best1, oh1)
            link(nc.vector.scalar_tensor_tensor(out=masked[:], in0=oh1[:], scalar=-BIG, in1=logits[:], op0=ALU.mult, op1=ALU.add))
            choose(masked, best2, oh2)
            nc.vector.tensor_tensor(picked[:], oh1[:], oh2[:], ALU.add).then_inc(picked_ready, 1)
            nc.vector.tensor_tensor(gexp[:], best2[:], best1[:], ALU.subtract).then_inc(diff_ready, 1)
            dve.wait_ge(rank_done, 1)
            link(nc.vector.tensor_copy(totals[:], bank(1)[:, 0:NI * E].rearrange("p (i e) -> p e i", e=E)))
            tot = totals[:].rearrange("p e i -> p (e i)")
            bef = before[:].rearrange("p e i -> p (e i)")
            link(nc.vector.tensor_tensor_scan(bef, onesf[:], tot, 0.0, ALU.mult, ALU.add))
            link(nc.vector.memset(e_end[:, 0:1], 0.0))
            link(nc.vector.tensor_copy(e_end[:, 1:E + 1], before[:, :, NI - 1]))
            link(nc.vector.tensor_tensor(bef, bef, tot, ALU.subtract))
            link(nc.vector.tensor_tensor(e_cnt[:], e_end[:, 1:E + 1], e_end[:, 0:E], ALU.subtract))
            link(nc.vector.tensor_scalar(e_int[:], e_cnt[:], float(P - 1), None, ALU.add))
            link(nc.vector.tensor_scalar(e_int[:], e_int[:], 7, None, ALU.arith_shift_right))
            link(nc.vector.tensor_copy(e_tiles[:], e_int[:]))
            link(nc.vector.memset(t_end[:, 0:1], 0.0))
            link(nc.vector.tensor_tensor_scan(t_end[:, 1:E + 1], onesf[:, 0:E], e_tiles[:], 0.0, ALU.mult, ALU.add))
            link(nc.vector.scalar_tensor_tensor(out=e_off[:], in0=t_end[:, 0:E], scalar=float(P), in1=e_end[:, 0:E],
                                                op0=ALU.mult, op1=ALU.subtract))
            link(nc.vector.tensor_tensor(t3[:], before[:].rearrange("p e i -> p i e"),
                                         e_off[:].unsqueeze(1).broadcast_to([P, NI, E]), ALU.add))
            link(nc.vector.tensor_tensor(t3[:], bank(0)[:, 0:NI * E].rearrange("p (i e) -> p i e", e=E), t3[:], ALU.add))
            for k, oh in enumerate((oh1, oh2)):
                link(nc.vector.tensor_tensor(oh[:], oh[:], t3[:], ALU.mult))
                link(nc.vector.tensor_reduce(slot[:, k, :], oh[:], AX.X, ALU.add))
            link(nc.vector.tensor_copy(slot_i[:], slot[:]))
            link(nc.vector.tensor_scalar(slot_t[:], slot_i[:], 7, None, ALU.arith_shift_right))
            link(nc.vector.tensor_copy(slot_col[:], slot_t[:]))
            link(nc.vector.tensor_scalar(slot_t[:], slot_i[:], P - 1, None, ALU.bitwise_and))
            link(nc.vector.tensor_copy(slot_row[:], slot_t[:]))
            link(nc.vector.tensor_scalar(tok_neg[:], tok_val[:], 0.0, None, ALU.is_ge))
            link(nc.vector.tensor_tensor(tok_val[:], tok_val[:], tok_neg[:], ALU.add))
            for n in range(2 * NI):
                k, i = n // NI, n % NI
                if n >= NHOT:
                    dve.wait_ge(hot_used, n - NHOT + 1)
                nc.vector.tensor_scalar(hot_row[:, n % NHOT, :], iota_b[:], slot_row[:, k, i:i + 1], None, ALU.is_equal)
                nc.vector.tensor_scalar(hot_col[:, n % NHOT, :], iota_b[:, 0:NT], slot_col[:, k, i:i + 1], tok_val[:, i:i + 1],
                                        ALU.is_equal, ALU.mult).then_inc(hot_ready, 1)
                if n % 8 == 7:
                    late_low(n // 8)
            dve.wait_ge(gexp_ready, 1)
            link(nc.vector.tensor_scalar(index[:], gexp[:], 1.0, None, ALU.add))
            link(nc.vector.reciprocal(index[:], index[:]))
            link(nc.vector.tensor_scalar(gate1[:], index[:], tanh_f[:], None, ALU.mult))
            link(nc.vector.tensor_tensor(gate2[:], gate1[:], gexp[:], ALU.mult))
            link(nc.vector.tensor_tensor(te3[:], iota_b[0:1, 0:NT].unsqueeze(2).broadcast_to([1, NT, E]),
                                         t_end[0:1, 1:E + 1].unsqueeze(1).broadcast_to([1, NT, E]), ALU.is_ge))
            link(nc.vector.tensor_reduce(tsum[0:1, :], te3[:], AX.X, ALU.add))
            nc.vector.tensor_scalar(tile_expert[:], tsum[0:1, :], float(E - 1), None, ALU.min).then_inc(lists_ready, 1)
            dve.wait_ge(hot_used, 2 * NI)
            link(nc.vector.tensor_copy(tval[:], banks[:, 2, 0:2 * NT].rearrange("p (k j) -> p k j", k=2)))
            link(nc.vector.tensor_tensor(tsum[:], tval[:, 0, :], tval[:, 1, :], ALU.add))
            link(nc.vector.tensor_scalar(tflag[:], tsum[:], 0.0, None, ALU.is_gt))
            link(nc.vector.tensor_tensor(tfull[:], tsum[:], tflag[:], ALU.subtract))
            link(nc.vector.tensor_scalar(tfull[:], tfull[:], float(T // 2), None, ALU.add))
            nc.vector.tensor_copy(slot_token[:], tfull[:]).then_inc(lists_ready, 1)
            link(nc.vector.tensor_scalar(tflag[:], tval[:, 1, :], 0.0, float(T), ALU.not_equal, ALU.mult))
            link(nc.vector.tensor_tensor(tfull[:], tfull[:], tflag[:], ALU.add))
            link(nc.vector.scalar_tensor_tensor(out=tflag[:], in0=tsum[:], scalar=0.0, in1=unused_row[:], op0=ALU.is_equal, op1=ALU.mult))
            nc.vector.tensor_tensor(slot_dest[:], tfull[:], tflag[:], ALU.add).then_inc(lists_ready, 1)

            dve.wait_ge(lists_ready, 3)
            dve.wait_ge(b2_full, 16)

            def low_x(j, par):
                dve.wait_ge(xh_ready, j + 1)
                nc.vector.scalar_tensor_tensor(out=xl[par][:].rearrange("p m t -> p (m t)"), in0=banks[:, par, 0:M * P], scalar=WSCALE,
                                               in1=xh[par][:].rearrange("p m t -> p (m t)"), op0=ALU.mult,
                                               op1=ALU.subtract).then_inc(xl_ready, 1)

            def cut_hidden(j, par):
                dve.wait_ge(hid_ready, 2 * (j + 1))
                wait(dve, y_done, j - 1)
                nc.vector.tensor_copy(hh[par][:], hid[par][:]).then_inc(hh_ready, 1)
                dve.wait_ge(hh_ready, j + 1)
                nc.vector.tensor_tensor(hl[par][:], hid[par][:], hh[par][:], ALU.subtract).then_inc(hl_ready, 1)

            def result(j, half, par):
                e = dve.value_load(tile_expert[0:1, ds(j, 1)], min_val=0, max_val=E - 1)
                dve.wait_ge(y_done, j + 1)
                wait(dve, y_sent[par], 16 * half)
                link(nc.vector.scalar_tensor_tensor(out=yb[par][:], in0=banks[:, 6 + par, 0:D], scalar=1.0 / HSCALE / WSCALE,
                                                    in1=b2_b[:, ds(e, 1), :].rearrange("p e d -> p (e d)"), op0=ALU.mult, op1=ALU.add))
                nc.vector.scalar_tensor_tensor(out=yb[par][:], in0=banks[:, 6 + par, D:2 * D], scalar=1.0 / HSCALE / WSCALE,
                                               in1=yb[par][:], op0=ALU.mult, op1=ALU.add).then_inc(y_ready, 1)

            low_x(0, 0)
            low_x(1, 1)
            cut_hidden(0, 0)

            def step(j, t, i, last):
                if not isinstance(j, int) or j + 2 < NT:
                    low_x(j + 2, i % 2)
                if not isinstance(j, int) or j + 1 < NT:
                    cut_hidden(j + 1, 1 - i % 2)
                if not isinstance(j, int) or j > 0:
                    result(j - 1, 2 * t + (i - 1) // 2, 1 - i % 2)

            tiles(dve, step, chain)
            step(NT, NT // RING, NT % RING, True)

            dve.wait_ge(x1_full, 16)
            for i in range(NI // DT):
                dve.wait_ge(y_back[i % 2], 32 * (i // 2 + 1))
                for k in range(DT):
                    n = i * DT + k
                    ins = nc.vector.scalar_tensor_tensor(out=y1b[i % 2][:, k, :], in0=y1b[i % 2][:, k, :], scalar=gate1[:, n:n + 1],
                                                         in1=x1_all[:, n, :], op0=ALU.mult, op1=ALU.add)
                link(ins)
                for k in range(DT):
                    n = i * DT + k
                    ins = nc.vector.scalar_tensor_tensor(out=y1b[i % 2][:, k, :], in0=y2b[i % 2][:, k, :], scalar=gate2[:, n:n + 1],
                                                         in1=y1b[i % 2][:, k, :], op0=ALU.mult, op1=ALU.add)
                ins.then_inc(out_ready, 1)

        @block.tensor
        def _(pe):
            pe.wait_ge(pool_ready, 1)
            pe.wait_ge(consts, 16 * N_CONST)
            NV = E * HC + 3 * M
            nc.tensor.transpose(banks[:, 7, 0:NV], oT[0:NV, 0, 0:P], ident[0:NV, 0:NV]).then_inc(b1t_done, 1)
            pe.wait_ge(bvcol_ready, 1)
            for m in range(M):
                ins = nc.tensor.matmul(banks[:, 6, 0:D], probs[0][:, m, 0:P], wo[:, m, :], start=(m == 0), stop=(m == M - 1))
            ins.then_inc(bvwo_done, 1)

            def turn(src, dst_bank, done):
                for c in range(C):
                    for m in range(M):
                        ins = nc.tensor.transpose(banks[:, dst_bank, m * L + c * P:m * L + (c + 1) * P], src[:, c, m * P:(m + 1) * P], ident[:])
                ins.then_inc(done, 1)

            def norm_T(n):
                pe.wait_ge(xn_ready, 2 * (n + 1))
                if isinstance(n, int):
                    wait(pe, xT_evac, n)
                turn(xn, 1, xT_done)

            def context_T(n, t, par):
                pe.wait_ge(cin_full[par], 16 * (t + 1))
                if isinstance(n, int):
                    wait(pe, ctxT_evac, n)
                turn(cin[par], 0, ctxT_done)

            def project_T(w, src, dst_bank, m):
                for k in range(M):
                    ins = nc.tensor.matmul(banks[:, dst_bank, m * L:(m + 1) * L], w[:, k, m * P:(m + 1) * P], src[:, k, :],
                                           start=(k == 0), stop=(k == M - 1))
                return ins

            def k(n, m):
                if m == 0:
                    pe.wait_ge(ctxT_evac, n + 1)
                    if isinstance(n, int) and n == 0:
                        pe.wait_ge(biases_ready, 2)
                    wait(pe, av_evac, 4 * (n - 1))
                    if isinstance(n, int):
                        wait(pe, k_evac, n)
                ins = project_T(wk, ctxT, 7, m)
                if m == M - 1:
                    ins.then_inc(k_done, 1)

            def q(n, m):
                if m == 0:
                    pe.wait_ge(xT_evac, n + 1)
                    if isinstance(n, int) and n == 0:
                        pe.wait_ge(obias_ready, 1)
                    wait(pe, av_evac, 4 * (n - 2) + 3)
                    if isinstance(n, int):
                        wait(pe, q_evac, n)
                ins = project_T(wq, xnT, 6, m)
                if m == M - 1:
                    ins.then_inc(q_done, 1)

            def v(n, c):
                if c == 0:
                    wait(pe, exp_done, 8 * (n - 2) + 7)
                for m in range(M):
                    ins = nc.tensor.matmul(banks[:, 2, c * D:(c + 1) * D], ctxT[:, m, c * P:(c + 1) * P], wv[:, m, :],
                                           start=(m == 0), stop=(m == M - 1))
                if c == C - 1:
                    ins.then_inc(v_done, 1)

            def scores_max(n, par, u):
                hp, c = u // 2, u % 2
                if u == 0:
                    pe.wait_ge(qs_full, 16 * NTERM * (n + 1))
                    pe.wait_ge(ks_full, 16 * NTERM * (n + 1))
                wait(pe, mx_red, 16 * n + u - 1)
                if u == 0:
                    if isinstance(n, int) and n < 2:
                        pe.wait_ge(ctxT_evac, n + 2)
                    else:
                        pe.wait_ge(x2T_evac, n - 1)
                if u == 1:
                    if isinstance(n, int) and n < 2:
                        pe.wait_ge(xT_evac, n + 2)
                    else:
                        pe.wait_ge(lg_evac, n - 1)
                for i in range(2):
                    h = 2 * hp + i
                    ins = nc.tensor.matmul(banks[:, u % 2, i * L:(i + 1) * L], qs[par][0:KR, h, c * P:(c + 1) * P], ks[par][0:KR, h, :],
                                           start=True, stop=True)
                ins.then_inc(mx_done, 1)

            def turn_max(n, s, nxt):
                pe.wait_ge(mx_red, 16 * n + 8 * (s + 1))
                if s == 0:
                    if nxt:
                        pe.wait_ge(k_evac, n + 2)
                    else:
                        pe.wait_ge(av_evac, 4 * n)
                else:
                    pe.wait_ge(nm_evac, 2 * n + 1)
                for c in range(C):
                    ins = nc.tensor.matmul(banks[0:8, 7, c * P:(c + 1) * P], negmax[:, c, 8 * s:8 * s + 8], ident[:], start=True, stop=True)
                ins.then_inc(nm_done, 1)

            def scores(n, par, v_, nxt, post):
                g, c = v_ // 2, v_ % 2
                if v_ in (0, 4):
                    pe.wait_ge(row_full[v_ // 4], 16 * (n + 1))
                if v_ == 0 and nxt:
                    pe.wait_ge(v_evac, n + 2)
                if v_ == 0 and post:
                    pe.wait_ge(cT_evac, n)
                if v_ == 1 and post:
                    pe.wait_ge(x1_ready, 2 * n)
                if v_ >= 2:
                    pe.wait_ge(exp_done, 8 * n + v_ - 1)
                for j in range(4):
                    h = 4 * g + j
                    ins = nc.tensor.matmul(banks[:, 2 + 2 * (v_ % 2) + j // 2, (j % 2) * L:(j % 2 + 1) * L],
                                           ks[par][0:KR + 1, h, c * P:(c + 1) * P], qs[par][0:KR + 1, h, :], start=True, stop=True)
                ins.then_inc(st_done, 1)

            def attend(n, par, v_, nxt):
                g, c = v_ // 2, v_ % 2
                pe.wait_ge(exp_done, 8 * n + v_ + 1)
                if v_ == 0:
                    pe.wait_ge(v_evac, n + 1)
                    if nxt:
                        pe.wait_ge(q_evac, n + 2)
                if v_ == 2:
                    pe.wait_ge(nm_evac, 2 * n + 2)
                if c == 0 and g >= 2:
                    pe.wait_ge(av_evac, 4 * n + g - 1)
                for j in range(4):
                    ins = nc.tensor.matmul(banks[32 * j:32 * j + 32, 6 + g % 2, 0:L], vaug[par][:, c, 4 * g + j, :],
                                           probs[v_ % 2][:, j, :], start=(c == 0), stop=(c == C - 1))
                ins.then_inc(av_mm, 1)

            def turn_out(n, c):
                pe.wait_ge(av_evac, 4 * (n + 1))
                pe.wait_ge(exp_done, 8 * (n + 1))
                for g in range(4):
                    ins = nc.tensor.transpose(banks[:, 4 + c, g * P:(g + 1) * P], oT[:, g, c * P:(c + 1) * P], ident[:])
                ins.then_inc(tok_done, 1)

            def attended_T(n):
                pe.wait_ge(cn_ready, 2 * (n + 1))
                turn(cn, 3, cT_done)

            def output(n, c):
                if c == 0:
                    pe.wait_ge(cT_evac, n + 1)
                for m in range(M):
                    ins = nc.tensor.matmul(banks[:, 4, c * D:(c + 1) * D], cT[:, m, c * P:(c + 1) * P], wo[:, m, :],
                                           start=(m == 0), stop=(m == M - 1))
                if c == C - 1:
                    ins.then_inc(o_done, 1)

            def norm2_T(n, ahead):
                pe.wait_ge(xn2_ready, 2 * (n + 1))
                if ahead == 2:
                    pe.wait_ge(ctxT_evac, n + 4)
                turn(xn2b, 0, x2T_done)

            def router(n, ahead):
                pe.wait_ge(x2T_evac, n + 1)
                if ahead == 2:
                    pe.wait_ge(xT_evac, n + 4)
                for c in range(C):
                    for m in range(M):
                        ins = nc.tensor.matmul(banks[:, 1, c * E:(c + 1) * E], cT[:, m, c * P:(c + 1) * P], wr[:, m, :],
                                               start=(m == 0), stop=(m == M - 1))
                ins.then_inc(lg_done, 1)

            context_T(0, 0, 0)
            norm_T(0)
            for m in range(M):
                k(0, m)
            for m in range(M):
                q(0, m)
            for c in range(C):
                v(0, c)
            context_T(1, 0, 1)
            norm_T(1)

            def body(t, par, weights, ahead):
                n = 2 * t + par
                post = not isinstance(n, int) or n > 0
                for u in range(16):
                    scores_max(n, par, u)
                    if ahead:
                        if u < 2:
                            k(n + 1, u)
                        elif u < 4:
                            q(n + 1, u - 2)
                        elif u in (6, 7):
                            v(n + 1, u - 6)
                    if post:
                        if u in (4, 5):
                            turn_out(n - 1, u - 4)
                        elif u == 8:
                            attended_T(n - 1)
                        elif u in (11, 12):
                            output(n - 1, u - 11)
                    if u == 9:
                        turn_max(n, 0, ahead > 0)
                    if u in (13, 15):
                        scores(n, par, (u - 13) // 2, ahead > 0, post)
                turn_max(n, 1, ahead > 0)
                for v_ in range(8):
                    if v_ >= 2:
                        scores(n, par, v_, ahead > 0, post)
                    if v_ >= 1:
                        attend(n, par, v_ - 1, ahead > 0)
                    if ahead == 2 and v_ == 1:
                        context_T(n + 2, t + 1, par)
                    if ahead == 2 and v_ == 4:
                        norm_T(n + 2)
                    if post and v_ == 5:
                        norm2_T(n - 1, ahead)
                    if post and v_ == 7:
                        router(n - 1, ahead)
                attend(n, par, 7, ahead > 0)

            bodies(pe, body)
            turn_out(NB - 1, 0)
            turn_out(NB - 1, 1)
            attended_T(NB - 1)
            for c in range(C):
                output(NB - 1, c)
            norm2_T(NB - 1, 0)
            router(NB - 1, 0)

            pe.wait_ge(picked_ready, 1)
            flat = picked[:].rearrange("p i e -> p (i e)")
            nc.tensor.matmul(banks[:, 0, 0:NI * E], tri[:], flat, start=True, stop=True)
            nc.tensor.matmul(banks[:, 1, 0:NI * E], ones[:], flat, start=True, stop=True).then_inc(rank_done, 1)
            for n in range(2 * NI):
                kk, i = n // NI, n % NI
                pe.wait_ge(hot_ready, n + 1)
                nc.tensor.matmul(banks[:, 2, kk * NT:(kk + 1) * NT], hot_row[:, n % NHOT, :], hot_col[:, n % NHOT, :],
                                 start=(i == 0), stop=(i == NI - 1)).then_inc(hot_used, 1)

            pe.wait_ge(lists_ready, 3)
            pe.wait_ge(late_lo, len(LATE))

            def gathered_T(j, lap, slot_):
                par = slot_ % 2
                pe.wait_ge(xg_full[slot_], 16 * (lap + 1))
                wait(pe, xl_ready, j - 1)
                for m in range(M):
                    ins = nc.tensor.transpose(banks[:, par, m * P:(m + 1) * P], xg[slot_][:, m * P:(m + 1) * P], ident[:])
                ins.then_inc(gT_done, 1)

            known = {}

            def expert(j, key):
                if key not in known:
                    known[key] = pe.value_load(tile_expert[0:1, ds(j, 1)], min_val=0, max_val=E - 1)
                return known[key]

            def begin_first(j, par):
                pe.wait_ge(xl_ready, j + 1)
                wait(pe, hid_ready, 2 * (j - 1))

            def first(j, par, e, c):
                half, i = c // (HC // 2), c % (HC // 2)
                dst = banks[:, 2 + 2 * par + half, i * P:(i + 1) * P]
                for m in range(M):
                    a = m * H + c * P
                    hi, lo = weight_at(e, 0, 0, a, a + P), weight_at(e, 0, 1, a, a + P)
                    nc.tensor.matmul(dst, hi, xh[par][:, m, :], start=(m == 0), stop=False)
                    nc.tensor.matmul(dst, hi, xl[par][:, m, :], start=False, stop=False)
                    ins = nc.tensor.matmul(dst, lo, xh[par][:, m, :], start=False, stop=(m == M - 1))
                if i == HC // 2 - 1:
                    ins.then_inc(h_done, 1)

            def begin_second(j):
                pe.wait_ge(hl_ready, j + 1)
                wait(pe, y_ready, j - 1)

            def second(j, par, e, c):
                both = wall[:, ds(e, 1), 1, 0:2, c * D:(c + 1) * D].rearrange("p e s n -> p (e s) n")
                mm = [(banks[:, 6 + par, 0:2 * D], hh[par], both), (banks[:, 6 + par, 0:D], hl[par], both[:, 0, :])]
                for k, (dst, h_, w_) in enumerate(mm if c == 0 else mm[::-1]):
                    ins = nc.tensor.matmul(dst, h_[:, c * P:(c + 1) * P], w_, start=(c == 0 and k == 0), stop=(c == HC - 1 and k == 1))
                if c == HC - 1:
                    ins.then_inc(y_done, 1)

            gathered_T(0, 0, 0)
            gathered_T(1, 0, 1)
            begin_first(0, 0)
            e = expert(0, 0)
            for c in range(HC):
                first(0, 0, e, c)

            def step(j, t, i, last):
                static = isinstance(j, int)
                has_first, has_second = not static or j + 1 < NT, not static or j > 0
                if not static or j + 2 < NT:
                    gathered_T(j + 2, t + (i + 2) // RING, (i + 2) % RING)
                if i == 0:
                    known.clear()
                if has_first:
                    begin_first(j + 1, 1 - i % 2)
                    e1 = expert(j + 1, i + 1)
                if has_second:
                    begin_second(j - 1)
                    e2 = expert(j - 1, i - 1)
                for c in range(HC):
                    if has_first:
                        first(j + 1, 1 - i % 2, e1, c)
                    if has_second:
                        second(j - 1, 1 - i % 2, e2, c)

            tiles(pe, step)
            step(NT, NT // RING, NT % RING, True)


_INS = ['x', 'ctx_1024', 'g_xattn', 'g_ffn', 'L0_xattn_Wq', 'L0_xattn_bq', 'L0_xattn_Wk', 'L0_xattn_bk', 'L0_xattn_Wv',
        'L0_xattn_bv', 'L0_xattn_Wo', 'L0_xattn_bo', 'L0_ffn_Wr', 'L0_ffn_br', 'L0_ffn_W1', 'L0_ffn_b1', 'L0_ffn_W2', 'L0_ffn_b2']


def kernel(**inputs):
    import numpy as np
    import concourse.bacc as bacc
    from concourse.bass_utils import run_bass_kernel_spmd

    nc = bacc.Bacc("TRN2", target_bir_lowering=False, num_devices=1)
    arrays, args = {}, []
    for name in _INS:
        a = np.ascontiguousarray(inputs[name])
        arrays[f"in_{name}"] = a
        args.append(nc.dram_tensor(f"in_{name}", a.shape, mybir.dt.from_np(a.dtype), kind="ExternalInput").ap())
    out = nc.dram_tensor("out_dram", inputs["x"].shape, F32, kind="ExternalOutput").ap()
    flamingo(nc, *args, out)
    r = run_bass_kernel_spmd(nc, [arrays], core_ids=[0])
    return r.results[0]["out_dram"]
```

```python
from contextlib import ExitStack

import concourse.bass as bass
from concourse import mybir

ALU = mybir.AluOpType
ACT = mybir.ActivationFunctionType
AX = mybir.AxisListType
F32 = mybir.dt.float32
F16 = mybir.dt.float16
BF16 = mybir.dt.bfloat16
I32 = mybir.dt.int32
ds = bass.ds

P = 128
EPS = 1e-5
WSCALE = 256.0
HSCALE = 16.0
Q_TERM = [0, 0, 1, 1, 0, 2]
K_TERM = [0, 1, 0, 1, 2, 0]
NTERM = len(Q_TERM)


def flamingo(nc, x, ctx_in, g_xattn, g_ffn, Wq, bq, Wk, bk, Wv, bv, Wo, bo, Wr, br, W1, b1, W2, b2, out):
    NB, L, D = x.shape
    E, _, H = W1.shape
    NH, DH = 16, D // 16
    C = L // P
    M = D // P
    HC = H // P
    T = NB * L
    NI = T // P
    SUB = 2
    TS = SUB * P
    NT = (2 * T + E * (TS - 1)) // TS
    NS = NT * SUB
    KR = NTERM * DH
    BIG = 3.0e38

    x_rows = x.rearrange("b (c p) d -> b p c d", p=P)
    ctx_rows = ctx_in.rearrange("b (c p) d -> b p c d", p=P)

    ctx = ExitStack()
    with ctx:
        def sem(name):
            return ctx.enter_context(nc.semaphore(name))

        def dram(name, shape, dt):
            return nc.dram_tensor(name, shape, dt, kind="Internal").ap()

        cursor = [-(-nc.sbuf_base // 64) * 64]

        def sb(name, shape, dt, at=None):
            size = 1
            for s in shape[1:]:
                size *= s
            size *= 2 if dt in (F16, BF16) else 4
            size = -(-size // 32) * 32
            where = cursor if at is None else at
            t = nc.alloc_sbuf_tensor_at(name, shape, dt, offset=where[0])
            where[0] += size
            return t

        part_d = {s: [dram(f"{s}_parts{i}", (3, D, L), BF16) for i in range(2)] for s in "qk"}
        x1_d = dram("x1_rows", (T, D), F32)
        xn2_d = dram("xn2_rows", (T, D), F32)
        y_d = dram("y_rows", (2 * T + NS * P, D), F32)

        ident = sb("ident", [P, P], F32)
        tri = sb("tri", [P, P], BF16)
        ones = sb("ones", [P, P], BF16)
        logits = sb("logits", [P, NI, E], F32)
        b1_col = sb("b1_col", [P, E * HC], F32)
        gate1 = sb("gate1", [P, NI], F32)
        gate2 = sb("gate2", [P, NI], F32)
        tanh_x = sb("tanh_x", [P, 1], F32)
        tanh_f = sb("tanh_f", [P, 1], F32)
        slot_token = sb("slot_token", [P, NS], I32)
        slot_dest = sb("slot_dest", [P, NS], I32)
        tile_expert = sb("tile_expert", [1, NT], I32)
        W_KEPT = 6
        wall_at = cursor[0]
        wall = sb("wall", [P, E, 2, 2, M * H], F16)
        over = [cursor[0] - (E - W_KEPT) * 2 * 2 * M * H * 2]
        late = [cursor[0]]

        A = over
        over_at = A[0]
        xin = [sb(f"xin{i}", [P, C, D], F32, A) for i in range(2)]
        cin = [sb(f"cin{i}", [P, C, D], F32, A) for i in range(2)]
        xn = sb("xn", [P, C, D], F32, A)
        xnT = sb("xnT", [P, M, L], F32, A)
        ctxT = sb("ctxT", [P, M, L], F32, A)
        yq = sb("yq", [P, M, L], F32, A)
        yk = sb("yk", [P, M, L], F32, A)
        rest = sb("rest", [P, M, L], F32, A)
        qparts = sb("qparts", [P, 3, M, L], BF16, A)
        kparts = sb("kparts", [P, 3, M, L], BF16, A)
        wq = sb("wq", [P, M, D], F32, A)
        wk = sb("wk", [P, M, D], F32, A)
        wv = sb("wv", [P, M, D], F32, A)
        assert A[0] >= late[0]
        wo = sb("wo", [P, M, D], F32, A)
        wr = sb("wr", [P, M, E], F32, A)
        out_bias = sb("out_bias", [P, D], F32, A)
        bo_b = sb("bo_b", [P, D], F32, A)
        br_b = sb("br_b", [P, E], F32, A)
        bias_col = sb("bias_col", [P, 3, M], F32, A)
        stats = sb("stats", [P, C, 6], F32, A)
        mean_var = [sb(f"mean_var{i}", [P, C, 2], F32, A) for i in range(2)]
        var_eps = [sb(f"var_eps{i}", [P, C], F32, A) for i in range(2)]
        rstd = [sb(f"rstd{i}", [P, C], F32, A) for i in range(2)]
        minus_half = sb("minus_half", [P, C], F32, A)
        qs = [sb(f"qs{i}", [P, NH, L], BF16, A) for i in range(2)]
        ks = [sb(f"ks{i}", [P, NH, L], BF16, A) for i in range(2)]
        vaug = [sb(f"vaug{i}", [P, C, NH, 32], F32, A) for i in range(2)]
        probs = [sb(f"probs{i}", [P, 4, L], F32, A) for i in range(2)]
        negmax = sb("negmax", [P, C, NH], F32, A)
        negmax_row = [sb(f"negmax_row{i}", [8, L], BF16, A) for i in range(2)]
        oT = sb("oT", [P, 4, L], F32, A)
        recip = [sb(f"recip{i}", [P, NH], F32, A) for i in range(2)]
        cn = sb("cn", [P, C, D], F32, A)
        cT = sb("cT", [P, M, L], F32, A)
        xres = sb("xres", [P, C, D], F32, A)
        x1b = sb("x1b", [P, C, D], F32, A)
        xn2b = sb("xn2b", [P, C, D], F32, A)
        wst_at = A[0]
        wst = [sb(f"wst{i}", [P, M * H // 2], F32, A) for i in range(2)]
        assert A[0] <= nc.sbuf_usable_end, (A[0], nc.sbuf_usable_end)

        R = late
        b2_b = sb("b2_b", [P, E, D], F32, R)
        x1_all = sb("x1_all", [P, NI, D], F32, R)
        B0 = [R[0]]
        iota_e = sb("iota_e", [P, E], F32, B0)
        iota_b = sb("iota_b", [P, P], F32, B0)
        iota_h = sb("iota_h", [P, P], F16, B0)
        unused_row = sb("unused_row", [P, NS], F32, B0)
        tok_val = sb("tok_val", [P, NI], F32, B0)
        tok_neg = sb("tok_neg", [P, NI], F32, B0)
        t3 = sb("t3", [P, NI, E], F32, B0)
        oh1 = sb("oh1", [P, NI, E], F32, B0)
        oh2 = sb("oh2", [P, NI, E], F32, B0)
        picked = sb("picked", [P, NI, E], BF16, B0)
        masked = sb("masked", [P, NI, E], F32, B0)
        totals = sb("totals", [P, E, NI], F32, B0)
        before = sb("before", [P, E, NI], F32, B0)
        onesf = sb("onesf", [P, E * NI], F32, B0)
        best1 = sb("best1", [P, NI], F32, B0)
        best2 = sb("best2", [P, NI], F32, B0)
        index = sb("index", [P, NI], F32, B0)
        gexp = sb("gexp", [P, NI], F32, B0)
        e_end = sb("e_end", [P, E + 1], F32, B0)
        e_cnt = sb("e_cnt", [P, E], F32, B0)
        e_int = sb("e_int", [P, E], I32, B0)
        e_tiles = sb("e_tiles", [P, E], F32, B0)
        t_end = sb("t_end", [P, E + 1], F32, B0)
        e_off = sb("e_off", [P, E], F32, B0)
        slot = sb("slot", [P, 2, NI], F32, B0)
        slot_i = sb("slot_i", [P, 2, NI], I32, B0)
        slot_t = sb("slot_t", [P, 2, NI], I32, B0)
        slot_col = sb("slot_col", [P, 2, NI], F32, B0)
        slot_row = sb("slot_row", [P, 2, NI], F32, B0)
        NHOT, HOTS = 16, 8
        hot_row = sb("hot_row", [P, NHOT, P], F16, B0)
        hot_col = sb("hot_col", [P, NHOT, NS], F16, B0)
        tval = sb("tval", [P, 2, NS], F32, B0)
        tsum = sb("tsum", [P, NS], F32, B0)
        tflag = sb("tflag", [P, NS], F32, B0)
        tfull = sb("tfull", [P, NS], F32, B0)
        te3 = sb("te3", [1, NT, E], F32, B0)
        te_sum = sb("te_sum", [1, NT], F32, B0)
        assert B0[0] <= wst_at, (B0[0], wst_at)
        G0 = [B0[0]]
        gather_idx = [sb(f"gather_idx{i}", [P, SUB], I32, G0) for i in range(2)]
        xg = [sb(f"xg{i}", [P, SUB, D], F32, G0) for i in range(2)]
        assert G0[0] <= wst_at
        C0 = [R[0]]
        dest_idx = [sb(f"dest_idx{i}", [P, SUB], I32, C0) for i in range(2)]
        xh = [sb(f"xh{i}", [P, M, TS], F16, C0) for i in range(2)]
        xl = [sb(f"xl{i}", [P, M, TS], F16, C0) for i in range(2)]
        hid = [sb(f"hid{i}", [P, HC // 2, TS], F32, C0) for i in range(2)]
        yb = [sb(f"yb{i}", [P, SUB, D], F32, C0) for i in range(2)]
        hh = [sb("hh0", [P, HC, TS], F16, C0), sb("hh1", [P, HC, TS], F16, G0)]
        assert C0[0] <= B0[0]
        hl = [sb(f"hl{i}", [P, HC, TS], F16, G0) for i in range(2)]
        assert G0[0] <= nc.sbuf_usable_end, G0[0]
        D0 = [wall_at]
        DT = 4
        y1b = [sb(f"y1b{i}", [P, DT, D], F32, D0) for i in range(NI // DT)]
        y2b = [sb(f"y2b{i}", [P, DT, D], F32, D0) for i in range(NI // DT)]
        assert D0[0] <= over_at, D0[0]

        banks = ctx.enter_context(nc.psum_tensor("banks", [P, 8, 512], F32))

        def bank(i):
            return banks[:, i, :]

        passed = sem("passed")
        bias_rows = sem("bias_rows")
        qkv_full = sem("qkv_full")
        consts = sem("consts")
        ks_ones = sem("ks_ones")
        pool_const = sem("pool_const")
        pool_ready = sem("pool_ready")
        tanh_ready = sem("tanh_ready")
        bvcol_ready = sem("bvcol_ready")
        bvwo_done = sem("bvwo_done")
        obias_ready = sem("obias_ready")
        b1t_done = sem("b1t_done")
        biases_ready = sem("biases_ready")
        xin_full = [sem(f"xin_full{i}") for i in range(2)]
        cin_full = [sem(f"cin_full{i}") for i in range(2)]
        xres_full = sem("xres_full")
        xn_ready = sem("xn_ready")
        var_ready = [sem(f"var_ready{i}") for i in range(2)]
        rstd_ready = [sem(f"rstd_ready{i}") for i in range(2)]
        xT_done, xT_evac = sem("xT_done"), sem("xT_evac")
        ctxT_done, ctxT_evac = sem("ctxT_done"), sem("ctxT_evac")
        q_done, q_evac = sem("q_done"), sem("q_evac")
        k_done, k_evac = sem("k_done"), sem("k_evac")
        v_done, v_evac = sem("v_done"), sem("v_evac")
        q_split, k_split = sem("q_split"), sem("k_split")
        q_stored, k_stored = sem("q_stored"), sem("k_stored")
        qs_full, ks_full = sem("qs_full"), sem("ks_full")
        mx_done, mx_red = sem("mx_done"), sem("mx_red")
        nm_done, nm_evac = sem("nm_done"), sem("nm_evac")
        row_full = [sem(f"row_full{i}") for i in range(2)]
        st_done, exp_done = sem("st_done"), sem("exp_done")
        av_mm, av_evac = sem("av_mm"), sem("av_evac")
        tok_done, cn_ready = sem("tok_done"), sem("cn_ready")
        cT_done, cT_evac, o_done = sem("cT_done"), sem("cT_evac"), sem("o_done")
        xb_ready, x1_ready, xn2_ready = sem("xb_ready"), sem("x1_ready"), sem("xn2_ready")
        x1_stored, xn2_stored = sem("x1_stored"), sem("xn2_stored")
        x2T_done, x2T_evac = sem("x2T_done"), sem("x2T_evac")
        lg_done, lg_evac = sem("lg_done"), sem("lg_evac")
        w_full = [sem(f"w_full{i}") for i in range(2)]
        w_hi, w_scaled = sem("w_hi"), sem("w_scaled")
        stage_free = [sem(f"stage_free{i}") for i in range(2)]
        dve_chain = sem("dve_chain")
        pool_chain = sem("pool_chain")
        late_full = [sem(f"late_full{i}") for i in range(2)]
        late_hi, late_scaled, late_lo = sem("late_hi"), sem("late_scaled"), sem("late_lo")
        b2_full, x1_full = sem("b2_full"), sem("x1_full")
        iota_ready = sem("iota_ready")
        diff_ready, gexp_ready = sem("diff_ready"), sem("gexp_ready")
        picked_ready, rank_done = sem("picked_ready"), sem("rank_done")
        hot_ready, hot_used, lists_ready = sem("hot_ready"), sem("hot_used"), sem("lists_ready")
        idx_ready, dest_ready = sem("idx_ready"), sem("dest_ready")
        xg_full = [sem(f"xg_full{i}") for i in range(2)]
        gT_done, xh_ready, xl_ready = sem("gT_done"), sem("xh_ready"), sem("xl_ready")
        h_done, hid_ready, hh_ready, hl_ready = sem("h_done"), sem("hid_ready"), sem("hh_ready"), sem("hl_ready")
        y_done, y_ready = sem("y_done"), sem("y_ready")
        y_sent = [sem(f"y_sent{i}") for i in range(2)]
        y_back = [sem(f"y_back{i}") for i in range(NI // DT)]
        out_ready = sem("out_ready")
        out_sent = sem("out_sent")

        N_CONST = 4
        HOLDS = (nc.sync.engine, nc.gpsimd.engine)

        def hold(eng, s, v):
            eng.wait_ge(s, v)
            if not isinstance(v, int):
                eng.sem_inc(passed, 1)

        def wait(eng, s, v):
            if isinstance(v, int) and v <= 0:
                return
            hold(eng, s, v) if eng.engine in HOLDS else eng.wait_ge(s, v)

        def bodies(eng, body):
            body(0, 0, False, 2)
            body(0, 1, False, 2)
            with eng.Fori(1, NB // 2 - 1) as t:
                body(t, 0, True, 2)
                body(t, 1, True, 2)
            body(NB // 2 - 1, 0, False, 1)
            body(NB // 2 - 1, 1, False, 0)

        assert NB // 2 - 2 == W_KEPT

        def tiles(eng, step, extra, chain=None, per_step=0):
            laps = (NT - 1) // 2 - 1
            for j in range(4):
                step(j, j // 2, j % 2)
            with eng.Fori(2, laps) as t:
                if chain:
                    chain[1] = (t - 2) * 2 * per_step
                for i in range(2):
                    step(2 * t + i, t, i)
            if chain:
                chain[0], chain[1] = chain[0] + (laps - 3) * 2 * per_step, 0
            for j in range(2 * laps, NT + extra):
                step(j, j // 2, j % 2)

        def there(j, ahead=0):
            return not isinstance(j, int) or 0 <= j + ahead < NT

        def weight_at(e, w, part, a, b):
            return wall[:, ds(e, 1), w, part, a:b].rearrange("p e n -> p (e n)")

        LATE = [(e, w, half) for e in range(W_KEPT, E) for w in range(2) for half in range(2)]
        HALF = M * H // 2

        def weight_rows(e, w, half):
            if w == 0:
                return W1[e, half * P:(half + 1) * P, :]
            return W2[e, half * H // 2:(half + 1) * H // 2, :].rearrange("(c p) n -> p c n", p=P)

        def stage_view(buf, w):
            return buf[:, :] if w == 0 else buf[:, :].rearrange("p (c n) -> p c n", n=D)

        block = ctx.enter_context(nc.Block())

        @block.sync
        def _(sp):
            def load_x(n, t, par):
                wait(sp, xn_ready, 2 * (n - 1))
                sp.dma_start(xin[par][:], x_rows[n]).then_inc(xin_full[par], 16)
                wait(sp, ctxT_done, n - 1)
                sp.dma_start(cin[par][:], ctx_rows[n]).then_inc(cin_full[par], 16)

            def store_part(n, par, name):
                src, cut_, stored, full = (kparts, k_split, k_stored, ks_full) if name == "k" else (qparts, q_split, q_stored, qs_full)
                wait(sp, full, 16 * NTERM * (n - 1))
                hold(sp, cut_, n + 1)
                sp.dma_start(part_d[name][par].rearrange("s (m p) t -> p s m t", p=P), src[:]).then_inc(stored, 16)

            def load_part(n, par, name):
                terms, stored, dst, full = (K_TERM, k_stored, ks, ks_full) if name == "k" else (Q_TERM, q_stored, qs, qs_full)
                wait(sp, st_done, 8 * (n - 1))
                hold(sp, stored, 16 * (n + 1))
                for i, s in enumerate(terms):
                    sp.dma_start(dst[par][DH * i:DH * (i + 1), :, :],
                                 part_d[name][par][s].rearrange("(h d) t -> d h t", d=DH)).then_inc(full, 16)

            def max_row(n, par, s):
                hold(sp, nm_evac, 2 * n + s + 1)
                sp.dma_start(qs[par][KR:KR + 1, 8 * s:8 * s + 8, :], negmax_row[s][:]).then_inc(row_full[s], 16)

            def results(n):
                hold(sp, x1_ready, 2 * (n + 1))
                sp.dma_start(x1_d[ds(n * L, L), :].rearrange("(c p) d -> p c d", p=P), x1b[:]).then_inc(x1_stored, 16)
                hold(sp, xn2_ready, 2 * (n + 1))
                sp.dma_start(xn2_d[ds(n * L, L), :].rearrange("(c p) d -> p c d", p=P), xn2b[:]).then_inc(xn2_stored, 16)

            def residual(n):
                wait(sp, x1_ready, 2 * n)
                sp.dma_start(xres[:], x_rows[n]).then_inc(xres_full, 16)

            sp.dma_start(xin[0][:], x_rows[0]).then_inc(xin_full[0], 16)
            sp.dma_start(cin[0][:], ctx_rows[0]).then_inc(cin_full[0], 16)
            for i, b in enumerate((bq, bk, bv)):
                sp.dma_start(oT[E * HC + i * M:E * HC + (i + 1) * M, 0, 0:P], b.rearrange("(m p) -> m p", p=P)).then_inc(bias_rows, 16)
            sp.dma_start(oT[0:E * HC, 0, 0:P], b1.rearrange("e (c p) -> (e c) p", p=P)).then_inc(bias_rows, 16)
            for dst, w in ((wk, Wk), (wq, Wq), (wv, Wv)):
                sp.dma_start(dst[:], w.rearrange("(m p) n -> p m n", p=P)).then_inc(qkv_full, 16)
            for dst, w in ((wo, Wo), (wr, Wr)):
                sp.dma_start(dst[:], w.rearrange("(m p) n -> p m n", p=P)).then_inc(consts, 16)
            sp.dma_start(bo_b[:], bo.partition_broadcast(P)).then_inc(consts, 16)
            sp.dma_start(br_b[:], br.partition_broadcast(P)).then_inc(consts, 16)
            load_x(1, 0, 1)
            for name in "kq":
                store_part(0, 0, name)
                load_part(0, 0, name)

            def body(t, par, weights, ahead):
                n = 2 * t + par
                static = isinstance(n, int)
                post = not static or n > 0
                if post:
                    residual(n - 1)
                if ahead == 2:
                    load_x(n + 2, t + 1, par)

                if weights:
                    for w in range(2):
                        e = t - 1
                        wait(sp, stage_free[w], 2 * (t - 1) + par + 1)
                        if w == 0:
                            src = W1[ds(e, 1), par * P:(par + 1) * P, :].rearrange("e p n -> p (e n)")
                        else:
                            src = W2[ds(e, 1), par * H // 2:(par + 1) * H // 2, :].rearrange("e (c p) n -> p (e c) n", p=P)
                        sp.dma_start(stage_view(wst[w], w), src).then_inc(w_full[w], 16)
                if ahead:
                    store_part(n + 1, 1 - par, "k")
                max_row(n, par, 0)
                if ahead:
                    load_part(n + 1, 1 - par, "k")
                if ahead:
                    store_part(n + 1, 1 - par, "q")
                max_row(n, par, 1)
                if ahead:
                    load_part(n + 1, 1 - par, "q")
                if post:
                    results(n - 1)

            bodies(sp, body)
            hold(sp, k_stored, 16 * NB)
            hold(sp, q_stored, 16 * NB)
            hold(sp, v_done, NB)
            residual(NB - 1)
            for i, (e, w, half) in enumerate(LATE):
                if i == 0:
                    for w_ in range(2):
                        hold(sp, stage_free[w_], 2 * W_KEPT + 1)
                if i == 1:
                    results(NB - 1)
                    hold(sp, lg_evac, NB)
                    hold(sp, x1_stored, 16 * NB)
                    hold(sp, xn2_stored, 16 * NB)
                    sp.dma_start(b2_b[:].rearrange("p e d -> p (e d)"), b2.rearrange("e d -> (e d)").partition_broadcast(P)).then_inc(b2_full, 16)
                if i >= 2:
                    hold(sp, late_lo, i - 1)
                sp.dma_start(stage_view(wst[i % 2], w), weight_rows(e, w, half)).then_inc(late_full[i % 2], 16)
            sp.dma_start(x1_all[:], x1_d.rearrange("(i p) d -> p i d", p=P)).then_inc(x1_full, 16)
            hold(sp, y_sent[0], 16 * SUB * ((NT + 1) // 2))
            hold(sp, y_sent[1], 16 * SUB * (NT // 2))
            for i in range(NI // DT):
                sp.dma_start(y1b[i][:], y_d[i * DT * P:(i + 1) * DT * P, :].rearrange("(i p) d -> p i d", p=P)).then_inc(y_back[i], 16)
                sp.dma_start(y2b[i][:], y_d[T + i * DT * P:T + (i + 1) * DT * P, :].rearrange("(i p) d -> p i d", p=P)).then_inc(y_back[i], 16)
            hold(sp, out_sent, 16 * (NI // DT))

        @block.gpsimd
        def _(pool):
            chain = [0, 0]

            def link(ins):
                chain[0] += 1
                ins.then_inc(pool_chain, 1)
                hold(pool, pool_chain, chain[0] + chain[1])

            for i in range(2):
                pool.sem_inc(stage_free[i], 1)
                nc.gpsimd.memset(vaug[i][:], 0.0)
            nc.gpsimd.memset(ident[:], 0.0)
            nc.gpsimd.memset(minus_half[:], -0.5)
            nc.gpsimd.memset(ones[:], 1.0)
            nc.gpsimd.memset(tri[:], 1.0).then_inc(pool_const, 1)
            hold(pool, pool_const, 1)
            for i in range(2):
                nc.gpsimd.memset(vaug[i][:, :, :, DH:DH + 1], 1.0)
            nc.gpsimd.affine_select(out=ident[:], in_=ident[:], compare_op=ALU.not_equal, fill=1.0, base=0,
                                    pattern=[[-1, P]], channel_multiplier=1)
            nc.gpsimd.affine_select(out=tri[:], in_=tri[:], compare_op=ALU.is_gt, fill=0.0, base=0,
                                    pattern=[[1, P]], channel_multiplier=-1).then_inc(pool_ready, 1)

            def cut(src, dst):
                link(nc.gpsimd.tensor_tensor(rest[:], src[:], dst[:, 0], ALU.subtract))
                link(nc.gpsimd.tensor_copy(dst[:, 1], rest[:]))
                return nc.gpsimd.tensor_tensor(dst[:, 2], rest[:], dst[:, 1], ALU.subtract)

            def inverse_root(n, which):
                hold(pool, var_ready[which], n + 1)
                nc.gpsimd.tensor_tensor(rstd[which][:], var_eps[which][:], minus_half[:], ALU.pow).then_inc(rstd_ready[which], 1)

            def cut_k(n):
                hold(pool, k_evac, n + 1)
                wait(pool, q_split, n)
                cut(yk, kparts).then_inc(k_split, 1)

            def cut_q(n):
                hold(pool, q_evac, n + 1)
                hold(pool, k_split, n + 1)
                cut(yq, qparts).then_inc(q_split, 1)

            def residual(n):
                hold(pool, xres_full, 16 * (n + 1))
                if isinstance(n, int) and n == 0:
                    hold(pool, obias_ready, 1)
                nc.gpsimd.tensor_tensor(xres[:], xres[:], out_bias[:].unsqueeze(1).broadcast_to([P, C, D]),
                                        ALU.add).then_inc(xb_ready, 1)

            hold(pool, pool_ready, 1)
            inverse_root(0, 0)
            inverse_root(1, 0)
            cut_k(0)

            def body(t, par, weights, ahead):
                n = 2 * t + par
                post = not isinstance(n, int) or n > 0
                if ahead:
                    cut_k(n + 1)
                if post:
                    residual(n - 1)
                if ahead:
                    cut_q(n + 1)
                if weights:
                    for w in range(2):
                        hold(pool, w_scaled, 2 * (2 * (t - 1) + par) + w + 1)
                        nc.gpsimd.tensor_tensor(weight_at(t - 1, w, 1, par * HALF, (par + 1) * HALF), wst[w][:],
                                                weight_at(t - 1, w, 0, par * HALF, (par + 1) * HALF), ALU.subtract).then_inc(stage_free[w], 1)
                        if w == 0 and ahead == 2:
                            inverse_root(n + 2, 0)
                elif ahead == 2:
                    inverse_root(n + 2, 0)
                if post:
                    inverse_root(n - 1, 1)

            PER_BODY = 4
            body(0, 0, False, 2)
            body(0, 1, False, 2)
            with pool.Fori(1, NB // 2 - 1) as t:
                chain[1] = (t - 1) * (2 * PER_BODY)
                was = chain[0]
                body(t, 0, True, 2)
                body(t, 1, True, 2)
                assert chain[0] == was + 2 * PER_BODY
            chain[0], chain[1] = was + (NB // 2 - 2) * 2 * PER_BODY, 0
            body(NB // 2 - 1, 0, False, 1)
            body(NB // 2 - 1, 1, False, 0)

            residual(NB - 1)
            inverse_root(NB - 1, 1)
            hold(pool, lg_evac, NB)
            hold(pool, x1_stored, 16 * NB)
            hold(pool, xn2_stored, 16 * NB)
            nc.gpsimd.iota(iota_e[:], [[1, E]], base=-E, channel_multiplier=0, allow_small_or_imprecise_dtypes=True)
            nc.gpsimd.iota(iota_b[:], [[1, P]], base=0, channel_multiplier=0, allow_small_or_imprecise_dtypes=True)
            nc.gpsimd.iota(iota_h[:], [[1, P]], base=0, channel_multiplier=0, allow_small_or_imprecise_dtypes=True)
            nc.gpsimd.iota(unused_row[:], [[P, NS]], base=2 * T - T // 2, channel_multiplier=1, allow_small_or_imprecise_dtypes=True)
            nc.gpsimd.memset(onesf[:], 1.0)
            nc.gpsimd.iota(tok_val[:], [[P, NI]], base=-T // 2, channel_multiplier=1,
                           allow_small_or_imprecise_dtypes=True).then_inc(iota_ready, 1)
            for i, (e, w, half) in enumerate(LATE):
                hold(pool, late_scaled, i + 1)
                nc.gpsimd.tensor_tensor(wall[:, e, w, 1, half * HALF:(half + 1) * HALF], wst[i % 2][:],
                                        wall[:, e, w, 0, half * HALF:(half + 1) * HALF], ALU.subtract).then_inc(late_lo, 1)

            hold(pool, lists_ready, 1)

            def gather(j, lap, par):
                wait(pool, xg_full[par], 16 * SUB * lap)
                nc.gpsimd.tensor_copy(gather_idx[par][:], slot_token[:, ds(j * SUB, SUB)]).then_inc(idx_ready, 1)
                hold(pool, idx_ready, j + 1)
                wait(pool, gT_done, j - 1)
                for s in range(SUB):
                    nc.gpsimd.indirect_dma_start(xg[par][:, s, :], None, xn2_d,
                                                 bass.IndirectOffsetOnAxis(gather_idx[par][:, s:s + 1], 0)).then_inc(xg_full[par], 16)

            def destinations(j, lap, par):
                wait(pool, y_sent[par], 16 * SUB * lap)
                nc.gpsimd.tensor_copy(dest_idx[par][:], slot_dest[:, ds(j * SUB, SUB)]).then_inc(dest_ready, 1)
                hold(pool, dest_ready, j + 1)

            def scatter(j, par, s):
                hold(pool, y_ready, SUB * j + s + 1)
                nc.gpsimd.indirect_dma_start(y_d, bass.IndirectOffsetOnAxis(dest_idx[par][:, s:s + 1], 0),
                                             yb[par][:, s, :], None).then_inc(y_sent[par], 16)

            gather(0, 0, 0)
            gather(1, 0, 1)
            hold(pool, lists_ready, 3)

            def step(j, t, i):
                if there(j, 2):
                    gather(j + 2, t + 1, i)
                if there(j, -2):
                    scatter(j - 2, i, 1)
                if there(j, -1):
                    destinations(j - 1, t + (i - 1) // 2, 1 - i)
                    scatter(j - 1, 1 - i, 0)

            tiles(pool, step, 2)

        @block.scalar
        def _(act):
            act.dma_start(tanh_x[:], g_xattn.partition_broadcast(P)).then_inc(tanh_ready, 16)
            act.dma_start(tanh_f[:], g_ffn.partition_broadcast(P)).then_inc(tanh_ready, 16)
            act.wait_ge(tanh_ready, 32)
            nc.scalar.activation(tanh_x[:], tanh_x[:], ACT.Tanh).then_inc(tanh_ready, 1)
            nc.scalar.activation(tanh_f[:], tanh_f[:], ACT.Tanh).then_inc(tanh_ready, 1)
            act.wait_ge(b1t_done, 1)
            nc.scalar.activation(bias_col[:].rearrange("p i m -> p (i m)"), banks[:, 7, E * HC:E * HC + 3 * M], ACT.Copy).then_inc(biases_ready, 1)
            nc.scalar.activation(b1_col[:], banks[:, 7, 0:E * HC], ACT.Copy, scale=HSCALE).then_inc(biases_ready, 1)
            act.wait_ge(biases_ready, 1)
            act.wait_ge(pool_ready, 1)
            for m in range(M):
                ins = nc.scalar.activation(probs[0][:, m, 0:P], ident[:], ACT.Identity, bias=bias_col[:, 2, m:m + 1], scale=0.0)
            ins.then_inc(bvcol_ready, 1)

            def norm_T(n):
                act.wait_ge(xT_done, n + 1)
                wait(act, q_done, n)
                nc.scalar.activation(xnT[:].rearrange("p m t -> p (m t)"), bank(1), ACT.Copy).then_inc(xT_evac, 1)

            def context_T(n):
                act.wait_ge(ctxT_done, n + 1)
                wait(act, v_done, n)
                nc.scalar.activation(ctxT[:].rearrange("p m t -> p (m t)"), bank(0), ACT.Copy).then_inc(ctxT_evac, 1)

            def biased(n, which, src, done, split, stored, dst, parts_, evac):
                act.wait_ge(done, n + 1)
                wait(act, split, n)
                wait(act, stored, 16 * n)
                for m in range(M):
                    nc.scalar.activation(dst[:, m, :], banks[:, src, m * L:(m + 1) * L], ACT.Identity,
                                         bias=bias_col[:, which, m:m + 1])
                for m in range(M):
                    ins = nc.scalar.activation(parts_[:, 0, m, :], banks[:, src, m * L:(m + 1) * L], ACT.Identity,
                                               bias=bias_col[:, which, m:m + 1])
                ins.then_inc(evac, 1)

            def values(n, par):
                act.wait_ge(v_done, n + 1)
                wait(act, av_mm, 8 * (n - 1))
                for c in range(C):
                    ins = nc.scalar.activation(vaug[par][:, c, :, 0:DH], banks[:, 2, c * D:(c + 1) * D].rearrange("p (h d) -> p h d", d=DH), ACT.Copy)
                ins.then_inc(v_evac, 1)

            def prep(n):
                biased(n, 1, 7, k_done, k_split, k_stored, yk, kparts, k_evac)
                biased(n, 0, 6, q_done, q_split, q_stored, yq, qparts, q_evac)

            def attended_T(n):
                act.wait_ge(cT_done, n + 1)
                wait(act, lg_done, n)
                nc.scalar.activation(cT[:].rearrange("p m t -> p (m t)"), bank(3), ACT.Copy).then_inc(cT_evac, 1)

            def norm2_T(n):
                act.wait_ge(x2T_done, n + 1)
                act.wait_ge(o_done, n + 1)
                nc.scalar.activation(cT[:].rearrange("p m t -> p (m t)"), bank(0), ACT.Copy).then_inc(x2T_evac, 1)

            context_T(0)
            norm_T(0)
            prep(0)
            values(0, 0)
            context_T(1)
            norm_T(1)

            def body(t, par, weights, ahead):
                n = 2 * t + par
                post = not isinstance(n, int) or n > 0

                def high(w):
                    act.wait_ge(w_full[w], 16 * (2 * (t - 1) + par + 1))
                    nc.scalar.activation(weight_at(t - 1, w, 0, par * HALF, (par + 1) * HALF), wst[w][:], ACT.Copy,
                                         scale=WSCALE).then_inc(w_hi, 1)
                    act.wait_ge(w_hi, 2 * (2 * (t - 1) + par) + w + 1)
                    nc.scalar.activation(wst[w][:], wst[w][:], ACT.Copy, scale=WSCALE).then_inc(w_scaled, 1)

                if ahead:
                    prep(n + 1)
                if weights:
                    high(0)
                if ahead:
                    values(n + 1, 1 - par)
                if post:
                    attended_T(n - 1)
                if weights:
                    high(1)
                for v in range(8):
                    act.wait_ge(st_done, 8 * n + v + 1)
                    wait(act, av_mm, 8 * n + v - 1)
                    nc.scalar.activation(probs[v % 2][:].rearrange("p h t -> p (h t)"),
                                         banks[:, 2 + 2 * (v % 2):4 + 2 * (v % 2), :].rearrange("p b t -> p (b t)"),
                                         ACT.Exp, scale=float(DH) ** -0.5).then_inc(exp_done, 1)
                    if ahead == 2 and v == 1:
                        context_T(n + 2)
                    if ahead == 2 and v == 4:
                        norm_T(n + 2)
                    if post and v == 5:
                        norm2_T(n - 1)

            bodies(act, body)

            def late_high(i):
                e, w, half = LATE[i]
                act.wait_ge(late_full[i % 2], 16 * (i // 2 + 1))
                nc.scalar.activation(wall[:, e, w, 0, half * HALF:(half + 1) * HALF], wst[i % 2][:], ACT.Copy,
                                     scale=WSCALE).then_inc(late_hi, 1)
                act.wait_ge(late_hi, i + 1)
                nc.scalar.activation(wst[i % 2][:], wst[i % 2][:], ACT.Copy, scale=WSCALE).then_inc(late_scaled, 1)

            late_high(0)
            attended_T(NB - 1)
            norm2_T(NB - 1)
            for i in range(1, 2):
                late_high(i)
            act.wait_ge(diff_ready, 1)
            nc.scalar.activation(gexp[:], gexp[:], ACT.Exp).then_inc(gexp_ready, 1)
            for i in range(2, len(LATE)):
                late_high(i)

            act.wait_ge(lists_ready, 3)

            def high_x(j, par):
                act.wait_ge(gT_done, j + 1)
                wait(act, h_done, 4 * (j - 1))
                nc.scalar.activation(xh[par][:].rearrange("p m t -> p (m t)"), bank(4 + par), ACT.Copy,
                                     scale=WSCALE).then_inc(xh_ready, 1)

            def relu(j, e, b):
                half = b // 2
                if b % 2 == 0:
                    wait(act, hl_ready, 2 * (j - 1) + half + 1)
                act.wait_ge(h_done, 4 * j + b + 1)
                for c in (2 * b, 2 * b + 1):
                    ins = nc.scalar.activation(hid[half][:, c % (HC // 2), :], banks[:, b, c % 2 * TS:(c % 2 + 1) * TS],
                                               ACT.Relu, bias=b1_col[:, ds(e * HC + c, 1)], scale=HSCALE / WSCALE / WSCALE)
                ins.then_inc(hid_ready, 1)

            def step(j, t, i):
                if there(j, 1):
                    e = act.value_load(tile_expert[0:1, ds(j + 1, 1)], min_val=0, max_val=E - 1)
                    for b in range(2):
                        relu(j + 1, e, b)
                if there(j, 2):
                    high_x(j + 2, i)
                if there(j, 1):
                    for b in range(2, 4):
                        relu(j + 1, e, b)

            high_x(0, 0)
            high_x(1, 1)
            e = act.value_load(tile_expert[0:1, 0:1], min_val=0, max_val=E - 1)
            for b in range(4):
                relu(0, e, b)
            tiles(act, step, 0)
            for i in range(NI // DT):
                act.wait_ge(out_ready, i + 1)
                act.dma_start(out.rearrange("b (c p) d -> p (b c) d", p=P)[:, i * DT:(i + 1) * DT, :], y1b[i][:]).then_inc(out_sent, 16)

        @block.vector
        def _(dve):
            chain = [0, 0]

            def link(ins):
                chain[0] += 1
                ins.then_inc(dve_chain, 1)
                dve.wait_ge(dve_chain, chain[0] + chain[1])

            def variance(src, which):
                for c in range(C):
                    ins = nc.vector.bn_stats(stats[:, c, :], src[:, c, :])
                chain[0] += 1
                ins.then_inc(dve_chain, 1)
                hold(dve, dve_chain, chain[0] + chain[1])
                for c in range(C):
                    ins = nc.vector.bn_aggr(mean_var[which][:, c, :], stats[:, c, :])
                link(ins)
                nc.vector.tensor_scalar(var_eps[which][:], mean_var[which][:, :, 1], EPS, None, ALU.add).then_inc(var_ready[which], 1)

            def normalize(n, src, dst, which, ready):
                dve.wait_ge(rstd_ready[which], n + 1)
                for c in range(C):
                    nc.vector.tensor_scalar(dst[:, c, :], src[:, c, :], mean_var[which][:, c, 0:1], rstd[which][:, c:c + 1],
                                            ALU.subtract, ALU.mult).then_inc(ready, 1)

            def norm1_stats(n, t, par):
                dve.wait_ge(xin_full[par], 16 * (t + 1))
                variance(xin[par], 0)

            def norm1(n, par):
                wait(dve, xT_done, n)
                normalize(n, xin[par], xn, 0, xn_ready)

            def attended(n, c):
                dve.wait_ge(tok_done, 2 * n + c + 1)
                rows = bank(4 + c).rearrange("p (h w) -> p h w", w=32)
                link(nc.vector.reciprocal(recip[c][:].unsqueeze(2), rows[:, :, DH:DH + 1]))
                if c == 0:
                    wait(dve, cT_done, n)
                nc.vector.tensor_tensor(cn[:, c, :].rearrange("p (h d) -> p h d", d=DH), rows[:, :, 0:DH],
                                        recip[c][:].unsqueeze(2).broadcast_to([P, NH, DH]), ALU.mult).then_inc(cn_ready, 1)

            def residual(n):
                dve.wait_ge(o_done, n + 1)
                dve.wait_ge(xb_ready, n + 1)
                wait(dve, x1_stored, 16 * n)
                for c in range(C):
                    nc.vector.scalar_tensor_tensor(out=x1b[:, c, :], in0=banks[:, 4, c * D:(c + 1) * D], scalar=tanh_x[:],
                                                   in1=xres[:, c, :], op0=ALU.mult, op1=ALU.add).then_inc(x1_ready, 1)

            def norm2_stats(n):
                dve.wait_ge(x1_ready, 2 * (n + 1))
                variance(x1b, 1)

            def norm2(n):
                wait(dve, xn2_stored, 16 * n)
                wait(dve, x2T_done, n)
                normalize(n, x1b, xn2b, 1, xn2_ready)

            def router(n):
                dve.wait_ge(lg_done, n + 1)
                nc.vector.tensor_tensor(logits[:, ds(n * C, C), :], banks[:, 1, 0:C * E].rearrange("p (c e) -> p c e", e=E),
                                        br_b[:].unsqueeze(1).broadcast_to([P, C, E]), ALU.add).then_inc(lg_evac, 1)

            def reduce(n, u):
                hp, c = u // 2, u % 2
                dve.wait_ge(mx_done, 16 * n + u + 1)
                if u % 8 == 0:
                    wait(dve, nm_done, 2 * n - 1 + u // 8)
                nc.vector.tensor_reduce(negmax[:, c, 2 * hp:2 * hp + 2], bank(u % 2).rearrange("p (h k) -> p h k", k=L),
                                        AX.X, ALU.max, negate=True).then_inc(mx_red, 1)

            def max_row(n, s):
                dve.wait_ge(nm_done, 2 * n + s + 1)
                wait(dve, row_full[s], 16 * n)
                nc.vector.tensor_copy(negmax_row[s][:], banks[0:8, 7, 0:L]).then_inc(nm_evac, 1)

            for n in range(2):
                norm1_stats(n, 0, n)
                norm1(n, n)
                nc.vector.memset(ks[n][KR:KR + 1, :, :], 1.0).then_inc(ks_ones, 1)
            dve.wait_ge(q_evac, 1)
            link(nc.vector.tensor_tensor(x1b[:], yq[:], qparts[:, 0], ALU.subtract))
            link(nc.vector.tensor_copy(qparts[:, 1], x1b[:]))
            nc.vector.tensor_tensor(qparts[:, 2], x1b[:], qparts[:, 1], ALU.subtract).then_inc(q_split, 1)
            dve.wait_ge(consts, 16 * N_CONST)
            dve.wait_ge(bvwo_done, 1)
            dve.wait_ge(tanh_ready, 34)
            link(nc.vector.tensor_tensor(out_bias[:], banks[:, 6, 0:D], bo_b[:], ALU.add))
            nc.vector.tensor_scalar(out_bias[:], out_bias[:], tanh_x[:], None, ALU.mult).then_inc(obias_ready, 1)

            def body(t, par, weights, ahead):
                n = 2 * t + par
                post = not isinstance(n, int) or n > 0

                for u in range(16):
                    reduce(n, u)
                    if post and u in (5, 6):
                        attended(n - 1, u - 5)
                    if u == 10:
                        max_row(n, 0)
                    if post and u == 13:
                        residual(n - 1)
                max_row(n, 1)
                if ahead == 2:
                    norm1_stats(n + 2, t + 1, par)
                if post:
                    norm2_stats(n - 1)
                for g in range(4):
                    dve.wait_ge(av_mm, 8 * n + 2 * g + 2)
                    if g == 0:
                        wait(dve, tok_done, 2 * n)
                    nc.vector.tensor_copy(oT[:, g, :], banks[:, 6 + g % 2, 0:L]).then_inc(av_evac, 1)
                    if ahead == 2 and g == 0:
                        norm1(n + 2, par)
                    if post and g == 0:
                        norm2(n - 1)
                    if post and g == 3:
                        router(n - 1)

            PER_BODY = 2 + 2 + 2
            body(0, 0, False, 2)
            body(0, 1, False, 2)
            with dve.Fori(1, NB // 2 - 1) as t:
                chain[1] = (t - 1) * (2 * PER_BODY)
                was = chain[0]
                body(t, 0, True, 2)
                body(t, 1, True, 2)
                assert chain[0] == was + 2 * PER_BODY, (chain, was)
            chain[0], chain[1] = was + (NB // 2 - 2) * 2 * PER_BODY, 0
            body(NB // 2 - 1, 0, False, 1)
            body(NB // 2 - 1, 1, False, 0)
            attended(NB - 1, 0)
            attended(NB - 1, 1)
            residual(NB - 1)
            norm2_stats(NB - 1)
            norm2(NB - 1)
            router(NB - 1)

            dve.wait_ge(iota_ready, 1)
            dve.wait_ge(lg_evac, NB)
            dve.wait_ge(xn2_stored, 16 * NB)
            dve.wait_ge(x1_stored, 16 * NB)

            def over_e(a):
                return a.unsqueeze(2).broadcast_to([P, NI, E])

            iota_ie = iota_e[:].unsqueeze(1).broadcast_to([P, NI, E])

            def choose(values, best, onehot):
                link(nc.vector.tensor_reduce(best[:], values[:], AX.X, ALU.max))
                link(nc.vector.tensor_tensor(t3[:], values[:], over_e(best[:]), ALU.is_equal))
                link(nc.vector.tensor_tensor(t3[:], t3[:], iota_ie, ALU.mult))
                link(nc.vector.tensor_reduce(index[:], t3[:], AX.X, ALU.min))
                link(nc.vector.tensor_tensor(onehot[:], iota_ie, over_e(index[:]), ALU.is_equal))

            choose(logits, best1, oh1)
            link(nc.vector.scalar_tensor_tensor(out=masked[:], in0=oh1[:], scalar=-BIG, in1=logits[:], op0=ALU.mult, op1=ALU.add))
            choose(masked, best2, oh2)
            nc.vector.tensor_tensor(picked[:], oh1[:], oh2[:], ALU.add).then_inc(picked_ready, 1)
            nc.vector.tensor_tensor(gexp[:], best2[:], best1[:], ALU.subtract).then_inc(diff_ready, 1)
            dve.wait_ge(rank_done, 1)
            link(nc.vector.tensor_copy(totals[:], bank(1)[:, 0:NI * E].rearrange("p (i e) -> p e i", e=E)))
            tot = totals[:].rearrange("p e i -> p (e i)")
            bef = before[:].rearrange("p e i -> p (e i)")
            link(nc.vector.tensor_tensor_scan(bef, onesf[:], tot, 0.0, ALU.mult, ALU.add))
            link(nc.vector.memset(e_end[:, 0:1], 0.0))
            link(nc.vector.tensor_copy(e_end[:, 1:E + 1], before[:, :, NI - 1]))
            link(nc.vector.tensor_tensor(bef, bef, tot, ALU.subtract))
            link(nc.vector.tensor_tensor(e_cnt[:], e_end[:, 1:E + 1], e_end[:, 0:E], ALU.subtract))
            link(nc.vector.tensor_scalar(e_int[:], e_cnt[:], float(TS - 1), None, ALU.add))
            link(nc.vector.tensor_scalar(e_int[:], e_int[:], TS.bit_length() - 1, None, ALU.arith_shift_right))
            link(nc.vector.tensor_copy(e_tiles[:], e_int[:]))
            link(nc.vector.memset(t_end[:, 0:1], 0.0))
            link(nc.vector.tensor_tensor_scan(t_end[:, 1:E + 1], onesf[:, 0:E], e_tiles[:], 0.0, ALU.mult, ALU.add))
            link(nc.vector.scalar_tensor_tensor(out=e_off[:], in0=t_end[:, 0:E], scalar=float(TS), in1=e_end[:, 0:E],
                                                op0=ALU.mult, op1=ALU.subtract))
            link(nc.vector.tensor_tensor(t3[:], before[:].rearrange("p e i -> p i e"),
                                         e_off[:].unsqueeze(1).broadcast_to([P, NI, E]), ALU.add))
            link(nc.vector.tensor_tensor(t3[:], bank(0)[:, 0:NI * E].rearrange("p (i e) -> p i e", e=E), t3[:], ALU.add))
            for k, oh in enumerate((oh1, oh2)):
                link(nc.vector.tensor_tensor(oh[:], oh[:], t3[:], ALU.mult))
                link(nc.vector.tensor_reduce(slot[:, k, :], oh[:], AX.X, ALU.add))
            link(nc.vector.tensor_copy(slot_i[:], slot[:]))
            link(nc.vector.tensor_scalar(slot_t[:], slot_i[:], 7, None, ALU.arith_shift_right))
            link(nc.vector.tensor_copy(slot_col[:], slot_t[:]))
            link(nc.vector.tensor_scalar(slot_t[:], slot_i[:], P - 1, None, ALU.bitwise_and))
            link(nc.vector.tensor_copy(slot_row[:], slot_t[:]))
            link(nc.vector.tensor_scalar(tok_neg[:], tok_val[:], 0.0, None, ALU.is_ge))
            link(nc.vector.tensor_tensor(tok_val[:], tok_val[:], tok_neg[:], ALU.add))
            for n in range(2 * NI):
                k, i = n // NI, n % NI
                if n % HOTS == 0:
                    if n >= NHOT:
                        dve.wait_ge(hot_used, n - NHOT + HOTS)
                    nc.vector.tensor_tensor(hot_row[:, n % NHOT:n % NHOT + HOTS, :], iota_b[:].unsqueeze(1).broadcast_to([P, HOTS, P]),
                                            slot_row[:, k, i:i + HOTS].unsqueeze(2).broadcast_to([P, HOTS, P]), ALU.is_equal)
                nc.vector.tensor_scalar(hot_col[:, n % NHOT, :], iota_h[:, 0:NS], slot_col[:, k, i:i + 1], tok_val[:, i:i + 1],
                                        ALU.is_equal, ALU.mult).then_inc(hot_ready, 1)
            dve.wait_ge(hot_used, 2 * NI)
            link(nc.vector.tensor_copy(tval[:], banks[:, 2, 0:2 * NS].rearrange("p (k j) -> p k j", k=2)))
            link(nc.vector.tensor_tensor(tsum[:], tval[:, 0, :], tval[:, 1, :], ALU.add))
            link(nc.vector.tensor_scalar(tflag[:], tsum[:], 0.0, None, ALU.is_gt))
            link(nc.vector.tensor_tensor(tfull[:], tsum[:], tflag[:], ALU.subtract))
            link(nc.vector.tensor_scalar(tfull[:], tfull[:], float(T // 2), None, ALU.add))
            nc.vector.tensor_copy(slot_token[:], tfull[:]).then_inc(lists_ready, 1)
            link(nc.vector.tensor_tensor(te3[:], iota_b[0:1, 0:NT].unsqueeze(2).broadcast_to([1, NT, E]),
                                         t_end[0:1, 1:E + 1].unsqueeze(1).broadcast_to([1, NT, E]), ALU.is_ge))
            link(nc.vector.tensor_reduce(te_sum[:], te3[:], AX.X, ALU.add))
            nc.vector.tensor_scalar(tile_expert[:], te_sum[:], float(E - 1), None, ALU.min).then_inc(lists_ready, 1)
            link(nc.vector.tensor_scalar(tflag[:], tval[:, 1, :], 0.0, float(T), ALU.not_equal, ALU.mult))
            link(nc.vector.tensor_tensor(tfull[:], tfull[:], tflag[:], ALU.add))
            link(nc.vector.scalar_tensor_tensor(out=tflag[:], in0=tsum[:], scalar=0.0, in1=unused_row[:], op0=ALU.is_equal, op1=ALU.mult))
            nc.vector.tensor_tensor(slot_dest[:], tfull[:], tflag[:], ALU.add).then_inc(lists_ready, 1)
            dve.wait_ge(gexp_ready, 1)
            link(nc.vector.tensor_scalar(index[:], gexp[:], 1.0, None, ALU.add))
            link(nc.vector.reciprocal(index[:], index[:]))
            link(nc.vector.tensor_scalar(gate1[:], index[:], tanh_f[:], None, ALU.mult))
            link(nc.vector.tensor_tensor(gate2[:], gate1[:], gexp[:], ALU.mult))

            dve.wait_ge(lists_ready, 3)
            dve.wait_ge(b2_full, 16)

            def low_x(j, par):
                dve.wait_ge(xh_ready, j + 1)
                nc.vector.scalar_tensor_tensor(out=xl[par][:].rearrange("p m t -> p (m t)"), in0=bank(4 + par), scalar=WSCALE,
                                               in1=xh[par][:].rearrange("p m t -> p (m t)"), op0=ALU.mult,
                                               op1=ALU.subtract).then_inc(xl_ready, 1)

            def cut_hidden(j, par, half):
                dve.wait_ge(hid_ready, 4 * j + 2 * (half + 1))
                if half == 0:
                    wait(dve, y_done, SUB * (j - 1))
                cs = slice(half * (HC // 2), (half + 1) * (HC // 2))
                nc.vector.tensor_copy(hh[par][:, cs, :], hid[half][:]).then_inc(hh_ready, 1)
                dve.wait_ge(hh_ready, 2 * j + half + 1)
                nc.vector.tensor_tensor(hl[par][:, cs, :], hid[half][:], hh[par][:, cs, :], ALU.subtract).then_inc(hl_ready, 1)

            def result(j, lap, par, s, e):
                dve.wait_ge(y_done, SUB * j + s + 1)
                if s == 0:
                    wait(dve, y_sent[par], 16 * SUB * lap)
                link(nc.vector.scalar_tensor_tensor(out=yb[par][:, s, :], in0=banks[:, 6 + s, 0:D], scalar=1.0 / HSCALE / WSCALE,
                                                    in1=b2_b[:, ds(e, 1), :].rearrange("p e d -> p (e d)"), op0=ALU.mult, op1=ALU.add))
                nc.vector.scalar_tensor_tensor(out=yb[par][:, s, :], in0=banks[:, 6 + s, D:2 * D], scalar=1.0 / HSCALE / WSCALE,
                                               in1=yb[par][:, s, :], op0=ALU.mult, op1=ALU.add).then_inc(y_ready, 1)

            low_x(0, 0)
            low_x(1, 1)
            for half in range(2):
                cut_hidden(0, 0, half)

            def step(j, t, i):
                if there(j, -1):
                    e = dve.value_load(tile_expert[0:1, ds(j - 1, 1)], min_val=0, max_val=E - 1)
                    result(j - 1, t + (i - 1) // 2, 1 - i, 0, e)
                if there(j, 2):
                    low_x(j + 2, i)
                if there(j, -1):
                    result(j - 1, t + (i - 1) // 2, 1 - i, 1, e)
                if there(j, 1):
                    for half in range(2):
                        cut_hidden(j + 1, 1 - i, half)

            tiles(dve, step, 1, chain, SUB)

            dve.wait_ge(x1_full, 16)
            for i in range(NI // DT):
                dve.wait_ge(y_back[i], 32)
                for k in range(DT):
                    n = i * DT + k
                    ins = nc.vector.scalar_tensor_tensor(out=y1b[i][:, k, :], in0=y1b[i][:, k, :], scalar=gate1[:, n:n + 1],
                                                         in1=x1_all[:, n, :], op0=ALU.mult, op1=ALU.add)
                link(ins)
                for k in range(DT):
                    n = i * DT + k
                    ins = nc.vector.scalar_tensor_tensor(out=y1b[i][:, k, :], in0=y2b[i][:, k, :], scalar=gate2[:, n:n + 1],
                                                         in1=y1b[i][:, k, :], op0=ALU.mult, op1=ALU.add)
                ins.then_inc(out_ready, 1)

        @block.tensor
        def _(pe):
            pe.wait_ge(pool_ready, 1)
            pe.wait_ge(bias_rows, 16 * 4)
            NV = E * HC + 3 * M
            nc.tensor.transpose(banks[:, 7, 0:NV], oT[0:NV, 0, 0:P], ident[0:NV, 0:NV]).then_inc(b1t_done, 1)

            def turn(src, dst_bank, done):
                for c in range(C):
                    for m in range(M):
                        ins = nc.tensor.transpose(banks[:, dst_bank, m * L + c * P:m * L + (c + 1) * P], src[:, c, m * P:(m + 1) * P], ident[:])
                ins.then_inc(done, 1)

            def norm_T(n):
                pe.wait_ge(xn_ready, 2 * (n + 1))
                if isinstance(n, int):
                    wait(pe, xT_evac, n)
                turn(xn, 1, xT_done)

            def context_T(n, t, par):
                pe.wait_ge(cin_full[par], 16 * (t + 1))
                if isinstance(n, int):
                    wait(pe, ctxT_evac, n)
                turn(cin[par], 0, ctxT_done)

            def project_T(w, src, dst_bank, m):
                for k in range(M):
                    ins = nc.tensor.matmul(banks[:, dst_bank, m * L:(m + 1) * L], w[:, k, m * P:(m + 1) * P], src[:, k, :],
                                           start=(k == 0), stop=(k == M - 1))
                return ins

            def k(n, m):
                if m == 0:
                    pe.wait_ge(ctxT_evac, n + 1)
                    if isinstance(n, int) and n == 0:
                        pe.wait_ge(biases_ready, 2)
                        pe.wait_ge(qkv_full, 16 * 3)
                    wait(pe, av_evac, 4 * (n - 1))
                    if isinstance(n, int):
                        wait(pe, k_evac, n)
                ins = project_T(wk, ctxT, 7, m)
                if m == M - 1:
                    ins.then_inc(k_done, 1)

            def q(n, m):
                if m == 0:
                    pe.wait_ge(xT_evac, n + 1)
                    if isinstance(n, int) and n == 1:
                        pe.wait_ge(obias_ready, 1)
                    wait(pe, av_evac, 4 * (n - 2) + 3)
                    if isinstance(n, int):
                        wait(pe, q_evac, n)
                ins = project_T(wq, xnT, 6, m)
                if m == M - 1:
                    ins.then_inc(q_done, 1)

            def v(n, c):
                if c == 0:
                    wait(pe, exp_done, 8 * (n - 2) + 7)
                for m in range(M):
                    ins = nc.tensor.matmul(banks[:, 2, c * D:(c + 1) * D], ctxT[:, m, c * P:(c + 1) * P], wv[:, m, :],
                                           start=(m == 0), stop=(m == M - 1))
                if c == C - 1:
                    ins.then_inc(v_done, 1)

            def scores_max(n, par, u):
                hp, c = u // 2, u % 2
                if u == 0:
                    pe.wait_ge(qs_full, 16 * NTERM * (n + 1))
                    pe.wait_ge(ks_full, 16 * NTERM * (n + 1))
                wait(pe, mx_red, 16 * n + u - 1)
                if u == 0:
                    if isinstance(n, int) and n < 2:
                        pe.wait_ge(ctxT_evac, n + 2)
                    else:
                        pe.wait_ge(x2T_evac, n - 1)
                if u == 1:
                    if isinstance(n, int) and n < 2:
                        pe.wait_ge(xT_evac, n + 2)
                    else:
                        pe.wait_ge(lg_evac, n - 1)
                for i in range(2):
                    h = 2 * hp + i
                    ins = nc.tensor.matmul(banks[:, u % 2, i * L:(i + 1) * L], qs[par][0:KR, h, c * P:(c + 1) * P], ks[par][0:KR, h, :],
                                           start=True, stop=True)
                ins.then_inc(mx_done, 1)

            def turn_max(n, s, nxt):
                pe.wait_ge(mx_red, 16 * n + 8 * (s + 1))
                if s == 0:
                    if nxt:
                        pe.wait_ge(k_evac, n + 2)
                    else:
                        pe.wait_ge(av_evac, 4 * n)
                else:
                    pe.wait_ge(nm_evac, 2 * n + 1)
                for c in range(C):
                    ins = nc.tensor.transpose(banks[0:8, 7, c * P:(c + 1) * P], negmax[:, c, 8 * s:8 * s + 8], ident[:])
                ins.then_inc(nm_done, 1)

            def scores(n, par, v_, nxt, post):
                g, c = v_ // 2, v_ % 2
                if v_ in (0, 4):
                    pe.wait_ge(row_full[v_ // 4], 16 * (n + 1))
                if v_ == 0 and nxt:
                    pe.wait_ge(v_evac, n + 2)
                if v_ == 0 and post:
                    pe.wait_ge(cT_evac, n)
                if v_ == 1 and post:
                    pe.wait_ge(x1_ready, 2 * n)
                if v_ >= 2:
                    pe.wait_ge(exp_done, 8 * n + v_ - 1)
                for j in range(4):
                    h = 4 * g + j
                    ins = nc.tensor.matmul(banks[:, 2 + 2 * (v_ % 2) + j // 2, (j % 2) * L:(j % 2 + 1) * L],
                                           ks[par][0:KR + 1, h, c * P:(c + 1) * P], qs[par][0:KR + 1, h, :], start=True, stop=True)
                ins.then_inc(st_done, 1)

            def attend(n, par, v_, nxt):
                g, c = v_ // 2, v_ % 2
                pe.wait_ge(exp_done, 8 * n + v_ + 1)
                if v_ == 0:
                    pe.wait_ge(v_evac, n + 1)
                    if nxt:
                        pe.wait_ge(q_evac, n + 2)
                if v_ == 2:
                    pe.wait_ge(nm_evac, 2 * n + 2)
                if c == 0 and g >= 2:
                    pe.wait_ge(av_evac, 4 * n + g - 1)
                for j in range(4):
                    ins = nc.tensor.matmul(banks[32 * j:32 * j + 32, 6 + g % 2, 0:L], vaug[par][:, c, 4 * g + j, :],
                                           probs[v_ % 2][:, j, :], start=(c == 0), stop=(c == C - 1))
                ins.then_inc(av_mm, 1)

            def turn_out(n, c):
                pe.wait_ge(av_evac, 4 * (n + 1))
                pe.wait_ge(exp_done, 8 * (n + 1))
                for g in range(4):
                    ins = nc.tensor.transpose(banks[:, 4 + c, g * P:(g + 1) * P], oT[:, g, c * P:(c + 1) * P], ident[:])
                ins.then_inc(tok_done, 1)

            def attended_T(n):
                pe.wait_ge(cn_ready, 2 * (n + 1))
                turn(cn, 3, cT_done)

            def output(n, c):
                if c == 0:
                    pe.wait_ge(cT_evac, n + 1)
                for m in range(M):
                    ins = nc.tensor.matmul(banks[:, 4, c * D:(c + 1) * D], cT[:, m, c * P:(c + 1) * P], wo[:, m, :],
                                           start=(m == 0), stop=(m == M - 1))
                if c == C - 1:
                    ins.then_inc(o_done, 1)

            def norm2_T(n, ahead):
                pe.wait_ge(xn2_ready, 2 * (n + 1))
                if ahead == 2:
                    pe.wait_ge(ctxT_evac, n + 4)
                turn(xn2b, 0, x2T_done)

            def router(n, ahead):
                pe.wait_ge(x2T_evac, n + 1)
                if ahead == 2:
                    pe.wait_ge(xT_evac, n + 4)
                for c in range(C):
                    for m in range(M):
                        ins = nc.tensor.matmul(banks[:, 1, c * E:(c + 1) * E], cT[:, m, c * P:(c + 1) * P], wr[:, m, :],
                                               start=(m == 0), stop=(m == M - 1))
                ins.then_inc(lg_done, 1)

            context_T(0, 0, 0)
            norm_T(0)
            for m in range(M):
                k(0, m)
            for m in range(M):
                q(0, m)
            for c in range(C):
                v(0, c)
            context_T(1, 0, 1)
            norm_T(1)
            pe.wait_ge(consts, 16 * N_CONST)
            pe.wait_ge(q_evac, 1)
            pe.wait_ge(bvcol_ready, 1)
            for m in range(M):
                ins = nc.tensor.matmul(banks[:, 6, 0:D], probs[0][:, m, 0:P], wo[:, m, :], start=(m == 0), stop=(m == M - 1))
            ins.then_inc(bvwo_done, 1)
            pe.wait_ge(ks_ones, 2)

            def body(t, par, weights, ahead):
                n = 2 * t + par
                post = not isinstance(n, int) or n > 0
                for u in range(16):
                    scores_max(n, par, u)
                    if ahead:
                        if u in (0, 1):
                            k(n + 1, u)
                        elif u in (2, 3):
                            q(n + 1, u - 2)
                        elif u in (6, 7):
                            v(n + 1, u - 6)
                    if post:
                        if u in (4, 5):
                            turn_out(n - 1, u - 4)
                        elif u == 8:
                            attended_T(n - 1)
                        elif u in (11, 12):
                            output(n - 1, u - 11)
                    if u == 9:
                        turn_max(n, 0, ahead > 0)
                    if u in (14, 15):
                        scores(n, par, u - 14, ahead > 0, post)
                turn_max(n, 1, ahead > 0)
                for v_ in range(8):
                    if v_ >= 2:
                        scores(n, par, v_, ahead > 0, post)
                    if v_ >= 1:
                        attend(n, par, v_ - 1, ahead > 0)
                    if ahead == 2 and v_ == 1:
                        context_T(n + 2, t + 1, par)
                    if ahead == 2 and v_ == 4:
                        norm_T(n + 2)
                    if post and v_ == 5:
                        norm2_T(n - 1, ahead)
                    if post and v_ == 7:
                        router(n - 1, ahead)
                attend(n, par, 7, ahead > 0)

            bodies(pe, body)
            turn_out(NB - 1, 0)
            turn_out(NB - 1, 1)
            attended_T(NB - 1)
            for c in range(C):
                output(NB - 1, c)
            norm2_T(NB - 1, 0)
            router(NB - 1, 0)

            pe.wait_ge(picked_ready, 1)
            flat = picked[:].rearrange("p i e -> p (i e)")
            nc.tensor.matmul(banks[:, 0, 0:NI * E], tri[:], flat, start=True, stop=True)
            nc.tensor.matmul(banks[:, 1, 0:NI * E], ones[:], flat, start=True, stop=True).then_inc(rank_done, 1)
            for n in range(2 * NI):
                kk, i = n // NI, n % NI
                pe.wait_ge(hot_ready, n + 1)
                nc.tensor.matmul(banks[:, 2, kk * NS:(kk + 1) * NS], hot_row[:, n % NHOT, :], hot_col[:, n % NHOT, :],
                                 start=(i == 0), stop=(i == NI - 1)).then_inc(hot_used, 1)


            def gathered_T(j, lap, par):
                pe.wait_ge(xg_full[par], 16 * SUB * (lap + 1))
                wait(pe, xl_ready, j - 1)
                for s in range(SUB):
                    for m in range(M):
                        ins = nc.tensor.transpose(banks[:, 4 + par, m * TS + s * P:m * TS + (s + 1) * P], xg[par][:, s, m * P:(m + 1) * P], ident[:])
                ins.then_inc(gT_done, 1)

            def first(j, par, e, c):
                if c == 0:
                    pe.wait_ge(xl_ready, j + 1)
                if c % 2 == 0:
                    wait(pe, hid_ready, 4 * (j - 1) + c // 2 + 1)
                dst = banks[:, c // 2, c % 2 * TS:(c % 2 + 1) * TS]
                for m in range(M):
                    a = m * H + c * P
                    hi, lo = weight_at(e, 0, 0, a, a + P), weight_at(e, 0, 1, a, a + P)
                    nc.tensor.matmul(dst, hi, xh[par][:, m, :], start=(m == 0), stop=False)
                    nc.tensor.matmul(dst, hi, xl[par][:, m, :], start=False, stop=False)
                    ins = nc.tensor.matmul(dst, lo, xh[par][:, m, :], start=False, stop=(m == M - 1))
                if c % 2 == 1:
                    ins.then_inc(h_done, 1)

            def second(j, par, e, s, c):
                if c == 0:
                    pe.wait_ge(hl_ready, 2 * (j + 1))
                    wait(pe, y_ready, SUB * (j - 1) + s + 1)
                both = wall[:, ds(e, 1), 1, 0:2, c * D:(c + 1) * D].rearrange("p e s n -> p (e s) n")
                mm = [(banks[:, 6 + s, 0:2 * D], hh[par], both), (banks[:, 6 + s, 0:D], hl[par], both[:, 0, :])]
                for k, (dst, h_, w_) in enumerate(mm if c == 0 else mm[::-1]):
                    ins = nc.tensor.matmul(dst, h_[:, c, s * P:(s + 1) * P], w_, start=(c == 0 and k == 0), stop=(c == HC - 1 and k == 1))
                if c == HC - 1:
                    ins.then_inc(y_done, 1)

            gathered_T(0, 0, 0)
            gathered_T(1, 0, 1)
            pe.wait_ge(lists_ready, 2)
            pe.wait_ge(late_lo, len(LATE))
            e = pe.value_load(tile_expert[0:1, 0:1], min_val=0, max_val=E - 1)
            for c in range(HC):
                first(0, 0, e, c)

            def step(j, t, i):
                if there(j, 1):
                    e1 = pe.value_load(tile_expert[0:1, ds(j + 1, 1)], min_val=0, max_val=E - 1)
                if there(j, -1):
                    e2 = pe.value_load(tile_expert[0:1, ds(j - 1, 1)], min_val=0, max_val=E - 1)
                for c in range(HC):
                    if there(j, 1):
                        first(j + 1, 1 - i, e1, c)
                    if there(j, -1):
                        for k in range(SUB):
                            n = SUB * c + k
                            second(j - 1, 1 - i, e2, n // HC, n % HC)
                    if there(j, 2) and c == HC // 2:
                        gathered_T(j + 2, t + 1, i)

            tiles(pe, step, 1)


_INS = ['x', 'ctx_1024', 'g_xattn', 'g_ffn', 'L0_xattn_Wq', 'L0_xattn_bq', 'L0_xattn_Wk', 'L0_xattn_bk', 'L0_xattn_Wv',
        'L0_xattn_bv', 'L0_xattn_Wo', 'L0_xattn_bo', 'L0_ffn_Wr', 'L0_ffn_br', 'L0_ffn_W1', 'L0_ffn_b1', 'L0_ffn_W2', 'L0_ffn_b2']


def kernel(**inputs):
    import numpy as np
    import concourse.bacc as bacc
    from concourse.bass_utils import run_bass_kernel_spmd

    nc = bacc.Bacc("TRN2", target_bir_lowering=False, num_devices=1)
    arrays, args = {}, []
    for name in _INS:
        a = np.ascontiguousarray(inputs[name])
        arrays[f"in_{name}"] = a
        args.append(nc.dram_tensor(f"in_{name}", a.shape, mybir.dt.from_np(a.dtype), kind="ExternalInput").ap())
    out = nc.dram_tensor("out_dram", inputs["x"].shape, F32, kind="ExternalOutput").ap()
    flamingo(nc, *args, out)
    r = run_bass_kernel_spmd(nc, [arrays], core_ids=[0])
    return r.results[0]["out_dram"]
```
